# Optimizing a Trainium2 kernel written in Bass

```python
import numpy as np
import jax
import jax.numpy as jnp

def _softmax(x, axis=-1):
    return jax.nn.softmax(x, axis=axis)

def _gelu(x):
    return jax.nn.gelu(x, approximate=True)

def _silu(x):
    return jax.nn.silu(x)

def _sigmoid(x):
    return jax.nn.sigmoid(x)

def _layernorm(x, axis=-1, eps=1e-05):
    m = jnp.mean(x, axis=axis, keepdims=True)
    v = jnp.var(x, axis=axis, keepdims=True)
    return (x - m) / jnp.sqrt(v + eps)

def _scatter_add(tgt, idx, src, axis=0):
    return tgt.at[idx].add(src)

def _segment_sum(src, seg, n):
    return jax.ops.segment_sum(src, seg, n)
kernel_name = 'mk_seq_postln_d2_jaxref_r8_b4c302'

def setup_inputs(seed: int=0):
    np.random.seed(seed)
    _w = jnp.asarray

    def _L0_attn_setup():
        import jax, jax.numpy as jnp
        import numpy as np
        H = 512
        D = H // 4
        key = jax.random.key(seed)
        k1, k2, k3, k4, k5 = jax.random.split(key, 5)
        x = jax.random.normal(k1, (4, 512, H), dtype=jnp.float32)
        s_in = 1.0 / np.sqrt(H)
        Wqkv = jax.random.normal(k2, (H, 3 * D), dtype=jnp.float32) * s_in
        bqkv = jax.random.normal(k3, (3 * D,), dtype=jnp.float32) * 0.01
        Wo = jax.random.normal(k4, (D, H), dtype=jnp.float32) * (1.0 / np.sqrt(D))
        bo = jax.random.normal(k5, (H,), dtype=jnp.float32) * 0.01
        return {'x': x, 'Wqkv': Wqkv, 'bqkv': bqkv, 'Wo': Wo, 'bo': bo}
    _L0_attn_in = _L0_attn_setup()

    def _L0_ffn_setup():
        import jax, jax.numpy as jnp
        import numpy as np
        RMS_EPS = 1e-05
        key = jax.random.key(seed)
        k1, k2, k3, k4 = jax.random.split(key, 4)
        B, S, H, I = (1, 256, 512, 1792)
        x = jax.random.normal(k1, (B, S, H), dtype=jnp.float32)
        ln_w = jnp.ones((H,), dtype=jnp.float32)
        gate_w = jax.random.normal(k2, (I, H), dtype=jnp.float32) * 0.02
        up_w = jax.random.normal(k3, (I, H), dtype=jnp.float32) * 0.02
        down_w = jax.random.normal(k4, (H, I), dtype=jnp.float32) * 0.02
        return {'x': x, 'ln_w': ln_w, 'gate_w': gate_w, 'up_w': up_w, 'down_w': down_w}
    _L0_ffn_in = _L0_ffn_setup()

    def _L1_attn_setup():
        import jax, jax.numpy as jnp
        import numpy as np
        import math
        D_MODEL = 512
        NUM_HEADS = 32
        NUM_KV_HEADS = 8
        HEAD_DIM = D_MODEL // NUM_HEADS
        GROUP = NUM_HEADS // NUM_KV_HEADS
        SEQ_LEN = 256
        BATCH = 2
        ROPE_THETA = 10000.0

        def apply_rope(x, start_pos=0):
            b, h, s, hd = x.shape
            inv_freq = 1.0 / ROPE_THETA ** (jnp.arange(0, hd, 2, dtype=jnp.float32) / hd)
            pos = jnp.arange(start_pos, start_pos + s, dtype=jnp.float32)
            ang = pos[:, None] * inv_freq[None, :]
            cos = jnp.cos(ang).astype(x.dtype)
            sin = jnp.sin(ang).astype(x.dtype)
            xr = x[..., 0::2]
            xi = x[..., 1::2]
            out_r = xr * cos - xi * sin
            out_i = xr * sin + xi * cos
            return jnp.stack([out_r, out_i], axis=-1).reshape(b, h, s, hd)
        key = jax.random.key(seed)
        ks = jax.random.split(key, 5)
        qkv_dim = HEAD_DIM * (NUM_HEADS + 2 * NUM_KV_HEADS)
        scale = 1.0 / math.sqrt(D_MODEL)
        return {'x': jax.random.normal(ks[0], (BATCH, SEQ_LEN, D_MODEL), jnp.float32), 'w_qkv': jax.random.normal(ks[1], (qkv_dim, D_MODEL), jnp.float32) * scale, 'b_qkv': jax.random.normal(ks[2], (qkv_dim,), jnp.float32) * 0.01, 'w_o': jax.random.normal(ks[3], (D_MODEL, D_MODEL), jnp.float32) * scale, 'b_o': jax.random.normal(ks[4], (D_MODEL,), jnp.float32) * 0.01}
    _L1_attn_in = _L1_attn_setup()

    def _L1_ffn_setup():
        import jax, jax.numpy as jnp
        import numpy as np
        B, S, D = (4, 256, 512)
        NUM_EXPERTS, TOP_K = (3, 2)

        def _expert_outputs(h, w1, b1, w2, b2):
            pre = jnp.einsum('bsd,edf->ebsf', h, w1) + b1[:, None, None, :]
            act = jnp.stack([jnp.tanh(pre[0]), jax.nn.gelu(pre[1], approximate=False), jax.nn.silu(pre[2])])
            return jnp.einsum('ebsf,efd->ebsd', act, w2) + b2[:, None, None, :]
        key = jax.random.key(seed)
        ks = jax.random.split(key, 8)
        scale_in = 1.0 / np.sqrt(D)
        scale_gate = 1.0 / np.sqrt(D + 1)
        return {'h': jax.random.normal(ks[0], (B, S, D), dtype=jnp.float32), 'gate_w': jax.random.uniform(ks[1], (D + 1, NUM_EXPERTS), minval=-scale_gate, maxval=scale_gate, dtype=jnp.float32), 'gate_b': jnp.zeros((NUM_EXPERTS,), dtype=jnp.float32), 'w1': jax.random.uniform(ks[2], (NUM_EXPERTS, D, D), minval=-scale_in, maxval=scale_in, dtype=jnp.float32), 'b1': jnp.zeros((NUM_EXPERTS, D), dtype=jnp.float32), 'w2': jax.random.uniform(ks[3], (NUM_EXPERTS, D, D), minval=-scale_in, maxval=scale_in, dtype=jnp.float32), 'b2': jnp.zeros((NUM_EXPERTS, D), dtype=jnp.float32)}
    _L1_ffn_in = _L1_ffn_setup()
    _d = {'L0_attn_x': _L0_attn_in['x'], 'L0_attn_Wqkv': _L0_attn_in['Wqkv'], 'L0_attn_bqkv': _L0_attn_in['bqkv'], 'L0_attn_Wo': _L0_attn_in['Wo'], 'L0_attn_bo': _L0_attn_in['bo'], 'L0_ffn_ln_w': _L0_ffn_in['ln_w'], 'L0_ffn_gate_w': _L0_ffn_in['gate_w'], 'L0_ffn_up_w': _L0_ffn_in['up_w'], 'L0_ffn_down_w': _L0_ffn_in['down_w'], 'L1_attn_w_qkv': _L1_attn_in['w_qkv'], 'L1_attn_b_qkv': _L1_attn_in['b_qkv'], 'L1_attn_w_o': _L1_attn_in['w_o'], 'L1_attn_b_o': _L1_attn_in['b_o'], 'L1_ffn_gate_w': _L1_ffn_in['gate_w'], 'L1_ffn_gate_b': _L1_ffn_in['gate_b'], 'L1_ffn_w1': _L1_ffn_in['w1'], 'L1_ffn_b1': _L1_ffn_in['b1'], 'L1_ffn_w2': _L1_ffn_in['w2'], 'L1_ffn_b2': _L1_ffn_in['b2']}
    _x0 = _d['L0_attn_x']
    _d['L0_attn_x'] = jax.random.normal(jax.random.fold_in(jax.random.key(seed), 1), (2, 512, 512), dtype=_x0.dtype)
    del _x0
    return _d

def reference(L0_attn_x, L0_attn_Wqkv, L0_attn_bqkv, L0_attn_Wo, L0_attn_bo, L0_ffn_ln_w, L0_ffn_gate_w, L0_ffn_up_w, L0_ffn_down_w, L1_attn_w_qkv, L1_attn_b_qkv, L1_attn_w_o, L1_attn_b_o, L1_ffn_gate_w, L1_ffn_gate_b, L1_ffn_w1, L1_ffn_b1, L1_ffn_w2, L1_ffn_b2):

    def _L0_attn_ref(x, Wqkv, bqkv, Wo, bo):
        import jax, jax.numpy as jnp
        import numpy as np
        H = 512
        D = H // 4
        B, S, C = x.shape
        d = C // 4
        qkv = jnp.einsum('bsc,cf->bsf', x, Wqkv) + bqkv
        qkv = qkv.reshape(B, S, 3, d)
        q, k, v = (qkv[:, :, 0], qkv[:, :, 1], qkv[:, :, 2])
        scale = 1.0 / jnp.sqrt(jnp.float32(d)).astype(x.dtype)
        attn = jnp.einsum('bqd,bkd->bqk', q, k) * scale
        attn = jax.nn.softmax(attn, axis=-1)
        out = jnp.einsum('bqk,bkd->bqd', attn, v)
        return jnp.einsum('bqd,dc->bqc', out, Wo) + bo

    def _L0_ffn_ref(x, ln_w, gate_w, up_w, down_w):
        import jax, jax.numpy as jnp
        import numpy as np
        RMS_EPS = 1e-05
        var = jnp.mean(jnp.square(x), axis=-1, keepdims=True)
        nx = x * jax.lax.rsqrt(var + RMS_EPS) * ln_w
        g = jnp.einsum('bsh,ih->bsi', nx, gate_w)
        u = jnp.einsum('bsh,ih->bsi', nx, up_w)
        return jnp.einsum('bsi,hi->bsh', jax.nn.silu(g) * u, down_w)

    def _L1_attn_ref(x, w_qkv, b_qkv, w_o, b_o):
        import jax, jax.numpy as jnp
        import numpy as np
        import math
        D_MODEL = 512
        NUM_HEADS = 32
        NUM_KV_HEADS = 8
        HEAD_DIM = D_MODEL // NUM_HEADS
        GROUP = NUM_HEADS // NUM_KV_HEADS
        SEQ_LEN = 256
        BATCH = 2
        ROPE_THETA = 10000.0

        def apply_rope(x, start_pos=0):
            b, h, s, hd = x.shape
            inv_freq = 1.0 / ROPE_THETA ** (jnp.arange(0, hd, 2, dtype=jnp.float32) / hd)
            pos = jnp.arange(start_pos, start_pos + s, dtype=jnp.float32)
            ang = pos[:, None] * inv_freq[None, :]
            cos = jnp.cos(ang).astype(x.dtype)
            sin = jnp.sin(ang).astype(x.dtype)
            xr = x[..., 0::2]
            xi = x[..., 1::2]
            out_r = xr * cos - xi * sin
            out_i = xr * sin + xi * cos
            return jnp.stack([out_r, out_i], axis=-1).reshape(b, h, s, hd)
        bs, seq_len, d_model = x.shape
        qkv = x @ w_qkv.T + b_qkv
        q_dim = NUM_HEADS * HEAD_DIM
        kv_dim = NUM_KV_HEADS * HEAD_DIM
        q, k, v = jnp.split(qkv, [q_dim, q_dim + kv_dim], axis=-1)
        q = q.reshape(bs, seq_len, NUM_HEADS, HEAD_DIM).transpose(0, 2, 1, 3)
        k = k.reshape(bs, seq_len, NUM_KV_HEADS, HEAD_DIM).transpose(0, 2, 1, 3)
        v = v.reshape(bs, seq_len, NUM_KV_HEADS, HEAD_DIM).transpose(0, 2, 1, 3)
        q = apply_rope(q, 0)
        k = apply_rope(k, 0)
        k = jnp.repeat(k, GROUP, axis=1)
        v = jnp.repeat(v, GROUP, axis=1)
        scores = jnp.einsum('bhqd,bhkd->bhqk', q, k) / math.sqrt(HEAD_DIM)
        causal = jnp.tril(jnp.ones((seq_len, seq_len), dtype=bool))
        scores = jnp.where(causal[None, None, :, :], scores, jnp.float32(-1e+20))
        attn = jax.nn.softmax(scores, axis=-1)
        out = jnp.einsum('bhqk,bhkd->bhqd', attn, v)
        out = out.transpose(0, 2, 1, 3).reshape(bs, seq_len, d_model)
        return out @ w_o.T + b_o

    def _L1_ffn_ref(h, gate_w, gate_b, w1, b1, w2, b2):
        import jax, jax.numpy as jnp
        import numpy as np
        B, S, D = (4, 256, 512)
        NUM_EXPERTS, TOP_K = (3, 2)

        def _expert_outputs(h, w1, b1, w2, b2):
            pre = jnp.einsum('bsd,edf->ebsf', h, w1) + b1[:, None, None, :]
            act = jnp.stack([jnp.tanh(pre[0]), jax.nn.gelu(pre[1], approximate=False), jax.nn.silu(pre[2])])
            return jnp.einsum('ebsf,efd->ebsd', act, w2) + b2[:, None, None, :]
        b, s, d = h.shape
        vision_len = int(s * 0.3)
        text_strength = jnp.mean(jnp.abs(h[:, vision_len:, :]), axis=(1, 2), keepdims=True)
        vision_strength = jnp.mean(jnp.abs(h[:, :vision_len, :]), axis=(1, 2), keepdims=True)
        modality_ratio = text_strength / (vision_strength + 1e-08)
        modality_ratio = jnp.broadcast_to(modality_ratio, (b, s, 1))
        router_input = jnp.concatenate([h, modality_ratio], axis=-1)
        gate_logits = router_input @ gate_w + gate_b
        gate_scores = jax.nn.softmax(gate_logits, axis=-1)
        top_val, top_idx = jax.lax.top_k(gate_scores, TOP_K)
        top_val = top_val / (jnp.sum(top_val, axis=-1, keepdims=True) + 1e-08)
        expert_out = _expert_outputs(h, w1, b1, w2, b2)
        moe_out = jnp.zeros_like(h)
        batch_idx = jnp.arange(b)
        for i in range(TOP_K):
            j = top_idx[:, 0, i]
            out_i = expert_out[j, batch_idx]
            moe_out = moe_out + top_val[..., i:i + 1] * out_i
        return moe_out
    x = L0_attn_x
    x = _layernorm(x + _L0_attn_ref(x, L0_attn_Wqkv, L0_attn_bqkv, L0_attn_Wo, L0_attn_bo), axis=-1)
    x = _layernorm(x + _L0_ffn_ref(x, L0_ffn_ln_w, L0_ffn_gate_w, L0_ffn_up_w, L0_ffn_down_w), axis=-1)
    x = _layernorm(x + _L1_attn_ref(x, L1_attn_w_qkv, L1_attn_b_qkv, L1_attn_w_o, L1_attn_b_o), axis=-1)
    x = _layernorm(x + _L1_ffn_ref(x, L1_ffn_gate_w, L1_ffn_gate_b, L1_ffn_w1, L1_ffn_b1, L1_ffn_w2, L1_ffn_b2), axis=-1)
    return x

_drawn_inputs = setup_inputs


def setup_inputs(seed=0):
    import zlib

    import numpy as np

    out = dict(_drawn_inputs(seed))
    spreads = {'L0_ffn_ln_w': (1.0, 0.2),
     'L1_ffn_gate_b': (0.0, 0.8),
     'L1_ffn_b1': (0.0, 0.268),
     'L1_ffn_b2': (0.0, 0.1)}
    factors = {'L0_attn_bqkv': 3.316, 'L0_attn_bo': 3.917, 'L1_attn_b_qkv': 4.684, 'L1_attn_b_o': 6.378}
    for name, (base, spread) in spreads.items():
        noise = np.random.default_rng([zlib.crc32(name.encode()), seed]).standard_normal(out[name].shape)
        drawn = base * np.exp(spread * noise) if base else spread * noise
        out[name] = jnp.asarray(drawn.astype(out[name].dtype))
    for name, factor in factors.items():
        out[name] = (out[name] * factor).astype(out[name].dtype)
    return out
```

```python
from contextlib import ExitStack

import numpy as np

import concourse.bass as bass
from concourse import mybir
from concourse.alu_op_type import AluOpType as ALU

ACT = mybir.ActivationFunctionType
F32 = mybir.dt.float32
F32R = mybir.dt.float32r
BF16 = mybir.dt.bfloat16
F16 = mybir.dt.float16
AX = mybir.AxisListType

P = 128
B = 2
S = 512
H = 512
T = S // P
HT = H // P
D0 = H // 4
F = 1792
NI = F // P
NH, NKV, HD = 32, 8, 16
GROUP = NH // NKV
PAIRS = NH // 2
HR = 64
E = 3
FE = H // P
VW = 3 * HD + 1
QKV1 = (NH + 2 * NKV) * HD
LN_EPS = 1e-5
RMS_EPS = 1e-5
SCALE0 = float(D0) ** -0.5
SCALE1 = float(HD) ** -0.5
SHIFT1 = 14 * float(np.log(2.0))
MASKED = -1e30
RING = 4
CHUNK = 3 * H
VISION = int(S * 0.3)
UW = (1024, 1024, 768, 768, 1024, 512)
UO = tuple(sum(UW[:u]) for u in range(6))
UHEADS = (2, 2, 2, 2, 4, 4)
WSLOTS = 3


def split_chunks():
    chunks = [("w_qkv0", None, HT * 3 * D0), ("w_o0", None, H)]
    for b in range(B):
        chunks += [("w_ffn", i, 3 * H) for i in range(NI)]
    for b in range(B):
        chunks += [("w_qkv1", i, CHUNK) for i in range(2)] + [("w_o1", i, 2 * H) for i in range(2)]
    for b in range(B):
        chunks += [("w_moe", i, 2 * H) for i in range(E * FE)]
    return chunks


def post_ln_layers(nc, dram):
    chunks = split_chunks()
    FIRST = {}
    for n, (name, i, _) in enumerate(chunks):
        FIRST.setdefault((name, i), []).append(n)
    ctx = ExitStack()
    with ctx:
        offset = [(nc.sbuf_base + 63) // 64 * 64]
        limit = nc.sbuf_usable_end

        def at(name, shape, dt, off):
            return nc.alloc_sbuf_tensor_at(name, shape, dt, offset=off)

        def size(shape, dt):
            n = int(np.prod(shape[1:])) * (2 if dt in (BF16, F16) else 4)
            return (n + 63) // 64 * 64

        def sb(name, shape, dt):
            t = at(name, shape, dt, offset[0])
            offset[0] += size(shape, dt)
            assert offset[0] <= limit, (name, offset[0], limit)
            return t

        def region(base, items):
            out = []
            for name, shape, dt in items:
                out.append(at(name, shape, dt, base))
                base += size(shape, dt)
            assert base <= limit, (items[-1][0], base, limit)
            return out, base

        def sem(name):
            return ctx.enter_context(nc.semaphore(name))

        xs = [sb(f"xs{b}", [P, T, H], F32) for b in range(B)]
        XTh = sb("XTh", [P, HT, S], F32R)
        XTl = sb("XTl", [P, HT, S], F32R)
        ident = sb("ident", [P, P], F32)
        identb = sb("identb", [P, P], BF16)
        maskb = sb("maskb", [P, P], BF16)
        onesf = sb("onesf", [P, P], F32)
        row0 = sb("row0", [P, P], F32)
        smallc = sb("smallc", [P, 64], F32)
        mv = sb("mv", [P, T, 2], F32)
        stats = sb("stats", [P, T, 6], F32)
        std = sb("std", [P, T], F32)
        rstd = sb("rstd", [P, T], F32)
        eps = sb("eps", [P, 1], F32)
        shift = sb("shift", [P, 1], F32)
        raw = [sb(f"raw{i}", [P, CHUNK], F32) for i in range(RING)]
        base = offset[0]

        (w0h, w0l, wo0h, wo0l, QTh, QTl, KTh, KTl, vT, Vh0, Vl0, P0, PTh, PTl, OTh, OTl, xT, mx0, nm0, sum0, rs0,
         xb0, bo0), _ = region(base, [
            ("w0h", [P, HT, 3 * D0], F32R), ("w0l", [P, HT, 3 * D0], F32R),
            ("wo0h", [P, H], F32R), ("wo0l", [P, H], F32R),
            ("QTh", [P, S], F32R), ("QTl", [P, S], F32R), ("KTh", [P, S], F32R), ("KTl", [P, S], F32R),
            ("vT", [P, S], F32), ("Vh0", [P, T, D0], F32R), ("Vl0", [P, T, D0], F32R),
            ("P0", [P, T, S], F32), ("PTh", [P, T, S], F32R), ("PTl", [P, T, S], F32R),
            ("OTh", [P, S], F32R), ("OTl", [P, S], F32R), ("xT", [P, HT, S], F32),
            ("mx0", [P, T], F32), ("nm0", [P, T], F32), ("sum0", [P, T], F32), ("rs0", [P, T], F32),
            ("xb0", [P, T, H], F32), ("bo0", [P, H], F32)])
        (nx, ss, rr, sq), f_end = region(base, [("nx", [P, T, H], F32), ("ss", [P, T], F32), ("rr", [P, T], F32),
                                                ("sq", [P, H], F32)])
        fwh, f_end = region(f_end, [(f"fwh{i}", [P, 3 * H], F32R) for i in range(WSLOTS)])
        fwl, f_end = region(f_end, [(f"fwl{i}", [P, 3 * H], F32R) for i in range(WSLOTS)])
        sg, f_end = region(f_end, [(f"sg{i}", [P, S], F32) for i in range(2)])
        hh, f_end = region(f_end, [(f"hh{i}", [P, S], F32) for i in range(2)])
        hhi, f_end = region(f_end, [(f"hhi{i}", [P, S], F32R) for i in range(2)])
        hlo, f_end = region(f_end, [(f"hlo{i}", [P, S], F32R) for i in range(2)])
        (Qop, Kop, Vs, Otok, mtok, mTh, mTl, cosb, sinb, bq1, bo1, osum, orec), a_end = region(base, [
            ("Qop", [P, PAIRS, S], F32R), ("Kop", [P, NKV, S], F32R), ("Vs", [P, T, NKV, VW], BF16),
            ("Otok", [P, T, H], F32), ("mtok", [P, 2, PAIRS, T], F32), ("mTh", [P, P], F32R), ("mTl", [P, P], F32R),
            ("cosb", [P, T, HD], F32), ("sinb", [P, T, HD], F32), ("bq1", [P, QKV1], F32), ("bo1", [P, H], F32),
            ("osum", [P, 8, HD], F32), ("orec", [P, 8], F32)])
        PW = 5120
        (Ph0, Ph1, Pl0, Pl1), a_end1 = region(a_end, [
            ("Ph0", [P, PW], F16), ("Ph1", [P, PW], F16), ("Pl0", [P, PW], F16), ("Pl1", [P, PW], F16)])
        Ph, Pl = [Ph0, Ph1], [Pl0, Pl1]
        (w1h, w1l, qkv, t1, t2, rot, vr), a_end2 = region(a_end, [
            ("w1h", [P, HT, QKV1], F32R), ("w1l", [P, HT, QKV1], F32R), ("qkv", [P, QKV1], F32),
            ("t1", [P, 640], F32), ("t2", [P, 640], F32), ("rot", [P, 640], F32), ("vr", [P, 128], F32)])
        a_end = max(a_end1, a_end2)
        (Qs0, Ks0, Ks1), a_end3 = region(a_end, [
            ("Qs0", [P, NH, HR], F32R), ("Ks0", [P, NKV, HR], F32R), ("Ks1", [P, NKV, HR], F32R)])
        Pf, a_end4 = region(a_end, [(f"Pf{i}", [P, 1024], F32) for i in range(3)])
        a_end = max(a_end3, a_end4)
        (wo1h, wo1l), _ = region(base, [("wo1h", [P, HT, H], F32R), ("wo1l", [P, HT, H], F32R)])
        (gwr, gwh, gwl, lgT, lg, asum, awt, asum2, rat, b2b, zacc, gb, wsum), m_end = region(base, [
            ("gwr", [P, HT, P], F32), ("gwh", [P, HT, P], F32R), ("gwl", [P, HT, P], F32R), ("lgT", [P, S], F32),
            ("lg", [P, T, E], F32), ("asum", [P, T], F32), ("awt", [P, 2, T], F32), ("asum2", [P, 2], F32),
            ("rat", [P, 2], F32), ("b2b", [P, E, H], F32), ("zacc", [P, T, H], F32), ("gb", [P, 2, E], F32), ("wsum", [P, 2, T], F32)])
        g, m_end = region(m_end, [(f"g{i}", [P, T, E], F32) for i in range(17)])
        mwh, m_end = region(m_end, [(f"mwh{i}", [P, 2 * H], F32R) for i in range(WSLOTS)])
        mwl, m_end = region(m_end, [(f"mwl{i}", [P, 2 * H], F32R) for i in range(WSLOTS)])
        ea, m_end = region(m_end, [(f"ea{i}", [P, S], F32) for i in range(2)])
        eah, m_end = region(m_end, [(f"eah{i}", [P, S], F32R) for i in range(2)])
        eal, m_end = region(m_end, [(f"eal{i}", [P, S], F32R) for i in range(2)])

        ps = ctx.enter_context(nc.psum_tensor("ps", [P, 8, 512], F32))

        BQ, LNW, B1C = 0, 3, 8

        s_const_dma = sem("const_dma")
        s_const = sem("const_made")
        s_x_in = [sem(f"x_in{b}") for b in range(B)]
        s_raw = [sem(f"raw_landed{i}") for i in range(RING)]
        s_whi = sem("weights_hi")
        s_wlo = sem("weights_lo")
        s_stage = sem("stage_done")
        s_tp = sem("transposed")
        s_tphi = sem("xT_hi")
        s_tplo = sem("xT_lo")
        s_y = sem("y_full")
        s_var = sem("ln_var")
        s_std = sem("ln_std")
        s_chain = sem("dve_step")
        s_achain = sem("act_step")
        s_pchain = sem("pool_step")
        s_lnout = sem("ln_out")
        s_a0qkv, s_a0act, s_a0lo = sem("a0_qkv_full"), sem("a0_qkv_hi"), sem("a0_qk_lo")
        s_a0vt, s_a0vhi, s_a0vlo = sem("a0_v_transposed"), sem("a0_v_hi"), sem("a0_v_lo")
        s_a0s, s_a0nm, s_a0p = sem("a0_scores"), sem("a0_negmax"), sem("a0_probs")
        s_a0pt, s_a0pthi, s_a0ptlo = sem("a0_pT"), sem("a0_pT_hi"), sem("a0_pT_lo")
        s_a0ot, s_a0othi, s_a0otlo = sem("a0_oT"), sem("a0_oT_hi"), sem("a0_oT_lo")
        s_fss, s_fnx = sem("f_rms"), sem("f_nx")
        s_fg, s_fu, s_fsg, s_fh = sem("f_gate_full"), sem("f_up_full"), sem("f_silu"), sem("f_h")
        s_fhi, s_flo, s_fdn = sem("f_h_hi"), sem("f_h_lo"), sem("f_down")
        s_init = sem("a1_operands_init")
        s_q, s_qe = sem("a1_qkv_full"), sem("a1_qkv_read")
        s_rot, s_qhi, s_qlo, s_v = sem("a1_rotated"), sem("a1_qk_hi"), sem("a1_qk_lo"), sem("a1_v_parts")
        s_tq, s_eq, s_ek = sem("a1_qk_transposed"), sem("a1_q_operand"), sem("a1_k_operand")
        s_s1, s_mx = sem("a1_scores_for_max"), sem("a1_max")
        s_mt, s_mth, s_mtl, s_md = sem("a1_maxT"), sem("a1_maxT_hi"), sem("a1_maxT_lo"), sem("a1_max_rows")
        s_s2, s_p, s_pm, s_ph, s_pl = sem("a1_scores"), sem("a1_probs"), sem("a1_masked"), sem("a1_p_hi"), sem("a1_p_lo")
        s_o, s_oe = sem("a1_out"), sem("a1_out_read")
        s_gw, s_lgT, s_lgTe, s_lg, s_as, s_rt, s_rk, s_rkb, s_w = (
            sem("m_gate_w"), sem("m_logitsT"), sem("m_logitsT_read"), sem("m_logits"), sem("m_abs"), sem("m_ratio"),
            sem("m_rank"), sem("m_rank_bc"), sem("m_weights"))
        s_pre, s_ea, s_eh, s_el, s_e2, s_acc = (sem("m_pre"), sem("m_act"), sem("m_act_hi"), sem("m_act_lo"),
                                                sem("m_expert_out"), sem("m_acc"))
        s_gwd = sem("m_const_dma")
        s_a1d = sem("a1_const_dma")
        s_out = sem("out_written")

        N_CONST_DMA = 2

        def f32(ap):
            return ap.bitcast(F32)

        TP = {("A0", 0): 0, ("A0", 1): 1, ("F0", 0): 2, ("F0", 1): 3, ("A1", 0): 4, ("O1", 0): 5, ("A1", 1): 6,
              ("O1", 1): 7, ("M", 0): 8, ("M", 1): 9}
        TPP = {("F0", 0): 0, ("F0", 1): 1, ("A1", 0): 2, ("O1", 0): 3, ("A1", 1): 4, ("O1", 1): 5, ("M", 0): 6,
               ("M", 1): 7}
        LN = {("A0", 0): 0, ("A0", 1): 1, ("F0", 0): 2, ("F0", 1): 3, ("A1", 0): 4, ("A1", 1): 5, ("M", 0): 6,
              ("M", 1): 7}
        Y = {("A0", 0): 0, ("A0", 1): 1, ("A1", 0): 2, ("A1", 1): 3}
        ENGINES = 4

        def stage_end(eng, n):
            eng.drain().then_inc(s_stage, 1)
            eng.wait_ge(s_stage, ENGINES * (n + 1))

        block = ctx.enter_context(nc.Block())

        @block.sync
        def _(sp):
            sp.dma_start(smallc[:], dram["smallc"]).then_inc(s_const_dma, 16)

            def load(n):
                name, i, cols = chunks[n]
                if n >= RING:
                    sp.wait_ge(s_wlo, n - RING + 1)
                src = dram[name] if i is None else dram[name][i]
                sp.dma_start(raw[n % RING][:, 0:cols], src).then_inc(s_raw[n % RING], 16)

            load(0)
            for b in range(B):
                if b:
                    sp.wait_ge(s_stage, ENGINES * b)
                sp.dma_start(xT[:], dram["xT"][b]).then_inc(s_x_in[b], 16)
                sp.dma_start(xs[b][:], dram["x"][b]).then_inc(s_x_in[b], 16)
                if b == 0:
                    sp.dma_start(bo0[:], dram["bo0"].partition_broadcast(P)).then_inc(s_const_dma, 16)
                    load(1)
                    load(2)
                    load(3)
            n = 4
            while chunks[n][0] == "w_ffn":
                load(n)
                n += 1
            sp.wait_ge(s_stage, ENGINES * 4)
            for dst, name, bc in ((cosb, "cosb", False), (sinb, "sinb", False), (bq1, "bq1", True), (bo1, "bo1", True)):
                src = dram[name].partition_broadcast(P) if bc else dram[name]
                sp.dma_start(dst[:], src).then_inc(s_a1d, 16)
            for b in range(B):
                for _ in range(2):
                    load(n)
                    n += 1
                load(n)
                load(n + 1)
                n += 2
                sp.wait_ge(s_mth, b + 1)
                sp.wait_ge(s_mtl, b + 1)
                for k, mt in enumerate((mTh, mTl)):
                    for s in range(2):
                        row = HR * s + 3 * HD + k
                        dst = f32(Qop[row:row + 1, :, :]).rearrange("o p (t q) -> o (p t) q", q=P)
                        sp.dma_start(dst, f32(mt[HR * s:HR * (s + 1), :])).then_inc(s_md, 16)
            sp.wait_ge(s_stage, ENGINES * 6)
            for dst, name, bc in ((gwr, "gwr", False), (awt, "awt", False)):
                sp.dma_start(dst[:], dram[name]).then_inc(s_gwd, 16)
            sp.dma_start(b2b[:], dram["b2"].partition_broadcast(P)).then_inc(s_gwd, 16)
            sp.dma_start(gb[:], dram["gb"].partition_broadcast(P)).then_inc(s_gwd, 16)
            while n < len(chunks):
                load(n)
                n += 1
            for b in range(B):
                sp.wait_ge(s_lnout, 4 * (LN["M", b] + 1))
                sp.dma_start(dram["out"][b], xs[b][:]).then_inc(s_out, 16)
            sp.wait_ge(s_out, 16 * B)

        @block.gpsimd
        def _(pool):
            nc.gpsimd.memset(eps[:], LN_EPS)
            nc.gpsimd.memset(shift[:], SHIFT1)
            nc.gpsimd.memset(onesf[:], 1.0).then_inc(s_const, 1)
            nc.gpsimd.memset(ident[:], 0.0).then_inc(s_pchain, 1)
            nc.gpsimd.memset(row0[:], 0.0).then_inc(s_pchain, 1)
            nc.gpsimd.memset(maskb[:], 0.0).then_inc(s_pchain, 1)
            pool.wait_ge(s_pchain, 2)
            nc.gpsimd.affine_select(out=ident[:], in_=ident[:], compare_op=ALU.not_equal, fill=1.0, base=0,
                                    pattern=[[-1, P]], channel_multiplier=1).then_inc(s_const, 1)
            nc.gpsimd.affine_select(out=row0[:], in_=row0[:], compare_op=ALU.not_equal, fill=1.0, base=0,
                                    pattern=[[0, P]], channel_multiplier=1).then_inc(s_const, 1)

            pool.wait_ge(s_pchain, 3)
            nc.gpsimd.affine_select(out=maskb[:], in_=maskb[:], compare_op=ALU.is_ge, fill=MASKED, base=0,
                                    pattern=[[-1, P]], channel_multiplier=1).then_inc(s_const, 1)
            stage_end(pool, 0)
            stage_end(pool, 1)
            stage_end(pool, 2)
            stage_end(pool, 3)
            for b in range(B):
                if b == 0:
                    nc.gpsimd.memset(f32(Kop[:]), 0.0)
                    nc.gpsimd.memset(Vs[:, :, :, VW - 1:VW], 1.0).then_inc(s_init, 1)
                nc.gpsimd.memset(f32(Qs0[:, :, 3 * HD:HR]), 0.0)
                for k in (Ks0, Ks1):
                    nc.gpsimd.memset(f32(k[:, :, 3 * HD + 2:HR]), 0.0)
                    last = nc.gpsimd.memset(f32(k[:, :, 3 * HD:3 * HD + 2]), -1.0)
                last.then_inc(s_init, 1)
                for gg in range(NKV):
                    for u in range(6):
                        n_u = (b * NKV + gg) * 6 + u
                        cols = UW[u]
                        slot = Pf[n_u % 3]
                        pool.wait_ge(s_p, n_u + 1)
                        heads = UHEADS[u]
                        v = slot[:, 0:cols].rearrange("p (h q) -> p h q", h=heads)[:, :, 0:P]
                        nc.gpsimd.affine_select(out=v, in_=v, compare_op=ALU.is_ge, fill=0.0, base=0,
                                                pattern=[[0, heads], [1, P]],
                                                channel_multiplier=-1).then_inc(s_pm, 1)
                        gi = b * NKV + gg
                        if gi >= 2:
                            pool.wait_ge(s_o, 2 * (gi - 1))
                        pool.wait_ge(s_pm, n_u + 1)
                        nc.gpsimd.affine_select(out=Ph[gg % 2][:, UO[u]:UO[u] + cols], in_=slot[:, 0:cols],
                                                compare_op=ALU.is_equal, fill=0.0, base=0, pattern=[[0, cols]],
                                                channel_multiplier=0).then_inc(s_ph, 1)
                stage_end(pool, 4 + b)
            stage_end(pool, 6)
            stage_end(pool, 7)

        @block.scalar
        def _(act):
            def evac(out, in_, sm, func=ACT.Identity, **kw):
                return nc.scalar.activation(out, in_, func, **kw).then_inc(sm, 1)

            def tp_hi(key, scale=None):
                for h in range(HT):
                    act.wait_ge(s_tp, 4 * TPP[key] + h + 1)
                    kw = {} if scale is None else {"scale": scale[:, h:h + 1]}
                    evac(XTh[:, h, :], ps[:, h, :], s_tphi, **kw)

            def ln_std(key):
                act.wait_ge(s_var, LN[key] + 1)
                nc.scalar.activation(std[:], mv[:, :, 1], ACT.Sqrt, bias=eps[:]).then_inc(s_std, 1)

            def split_hi(n, out):
                cols = chunks[n][2]
                act.wait_ge(s_raw[n % RING], 16 * (n // RING + 1))
                evac(out, raw[n % RING][:, 0:cols], s_whi)

            flat = lambda t: t.rearrange("p a n -> p (a n)")
            split_hi(0, flat(w0h[:]))
            act.wait_ge(s_const, 4)
            act.wait_ge(s_const_dma, 16 * N_CONST_DMA)
            for b in range(B):
                act.wait_ge(s_x_in[b], 32)
                for h in range(HT):
                    evac(XTh[:, h, :], xT[:, h, :], s_tphi)
                if b == 0:
                    split_hi(1, wo0h[:])
                for k, out in enumerate((QTh, KTh, vT)):
                    act.wait_ge(s_a0qkv, 3 * b + k + 1)
                    evac(out[:], ps[:, 4 + k, :], s_a0act, bias=smallc[:, BQ + k:BQ + k + 1])
                act.wait_ge(s_a0vt, b + 1)
                evac(Vh0[:].rearrange("p t d -> p (t d)"), ps[:, 7, :], s_a0vhi)
                for q in range(T):
                    act.wait_ge(s_a0nm, T * b + q + 1)
                    nc.scalar.activation(P0[:, q, :], ps[:, q, :], ACT.Exp, bias=nm0[:, q:q + 1], scale=SCALE0,
                                         accum_out=sum0[:, q:q + 1]).then_inc(s_a0p, 1)
                for k in range(T):
                    act.wait_ge(s_a0pt, T * b + k + 1)
                    evac(PTh[:, k, :], ps[:, 4 + k, :], s_a0pthi)
                act.wait_ge(s_a0ot, b + 1)
                evac(OTh[:], ps[:, 0, :], s_a0othi)
                ln_std(("A0", b))
                stage_end(act, b)
            n = 2
            for b in range(B):
                for t in range(T):
                    last = nc.scalar.activation(nx[:, t, :], xs[b][:, t, :], ACT.Square, accum_out=ss[:, t:t + 1])
                last.then_inc(s_achain, 1)
                act.wait_ge(s_achain, b + 1)
                nc.scalar.activation(rr[:], ss[:], ACT.Sqrt, bias=eps[:], scale=1.0 / H).then_inc(s_fss, 1)
                split_hi(n, fwh[(b * NI) % WSLOTS][:])
                tp_hi(("F0", b), smallc[:, LNW:LNW + HT])
                for i in range(NI):
                    gi = b * NI + i
                    n += 1
                    if i + 1 < NI:
                        if gi + 1 >= WSLOTS:
                            act.wait_ge(s_fdn, gi - WSLOTS + 2)
                        split_hi(n, fwh[(gi + 1) % WSLOTS][:])
                    act.wait_ge(s_fg, gi + 1)
                    if gi >= 2:
                        act.wait_ge(s_fh, gi - 1)
                    nc.scalar.activation(sg[gi % 2][:], ps[:, 4 + gi % 2, :], ACT.Silu).then_inc(s_fsg, 1)
                    act.wait_ge(s_fh, gi + 1)
                    if gi >= 2:
                        act.wait_ge(s_fdn, gi - 1)
                    evac(hhi[gi % 2][:], hh[gi % 2][:], s_fhi)
                ln_std(("F0", b))
                stage_end(act, 2 + b)
            for b in range(B):
                for k in range(2):
                    split_hi(n, flat(w1h[:, 2 * k:2 * k + 2, :]))
                    n += 1
                tp_hi(("A1", b))
                act.wait_ge(s_init, b + 2)
                for t in range(T):
                    bt = b * T + t
                    act.wait_ge(s_rot, bt + 1)
                    if t >= 1:
                        act.wait_ge(s_tq, 5 * bt)
                    r = rot[:, 0:NH * HD].rearrange("p (h d) -> p h d", d=HD)
                    o = Qs0[:].rearrange("p h (k d) -> p h k d", d=HD)
                    for k in (0, 2):
                        nc.scalar.activation(o[:, :, k, :], r, ACT.Identity)
                    r = rot[:, NH * HD:].rearrange("p (h d) -> p h d", d=HD)
                    o = (Ks0, Ks1)[t % 2][:].rearrange("p h (k d) -> p h k d", d=HD)
                    nc.scalar.activation(o[:, :, 0, :], r, ACT.Identity)
                    nc.scalar.activation(o[:, :, 1, :], r, ACT.Identity).then_inc(s_qhi, 1)
                    for k in range(4):
                        u = 5 * bt + k
                        act.wait_ge(s_tq, u + 1)
                        evac(Qop[:, 4 * k:4 * k + 4, t * P:(t + 1) * P],
                             ps[:, 4 + u % 4, :].rearrange("p (a q) -> p a q", a=4), s_eq)
                act.wait_ge(s_mt, b + 1)
                evac(mTh[:], ps[:, 4, 0:P], s_mth)
                for gg in range(NKV):
                    for u in range(6):
                        n_u = (b * NKV + gg) * 6 + u
                        act.wait_ge(s_s2, n_u + 1)
                        if n_u >= 3:
                            act.wait_ge(s_pl, n_u - 2)
                        banks = 1 if u == 5 else 2
                        r0 = 2 * (n_u % 3)
                        src = ps[:, r0:r0 + banks, 0:UW[u] // banks]
                        nc.scalar.activation(Pf[n_u % 3][:, 0:UW[u]].rearrange("p (a n) -> p a n", a=banks), src,
                                             ACT.Exp, bias=shift[:], scale=SCALE1).then_inc(s_p, 1)
                for k in range(2):
                    split_hi(n, flat(wo1h[:, 2 * k:2 * k + 2, :]))
                    n += 1
                tp_hi(("O1", b))
                ln_std(("A1", b))
                stage_end(act, 4 + b)
            for b in range(B):
                if b == 0:
                    act.wait_ge(s_gwd, 64)
                    evac(gwh[:], gwr[:], s_gw)
                split_hi(n, mwh[(b * E * FE) % WSLOTS][:])
                tp_hi(("M", b))
                act.wait_ge(s_lgT, b + 1)
                evac(lgT[:], ps[:, 4, :], s_lgTe)
                act.wait_ge(s_rk, 2 * b + 1)
                nc.scalar.activation(g[1][:], g[0][:], ACT.Exp).then_inc(s_rt, 1)
                for i in range(E * FE):
                    gi = b * E * FE + i
                    n += 1
                    if i + 1 < E * FE:
                        if gi + 1 >= WSLOTS:
                            act.wait_ge(s_e2, gi - WSLOTS + 2)
                        split_hi(n, mwh[(gi + 1) % WSLOTS][:])
                    act.wait_ge(s_pre, gi + 1)
                    if gi >= 2:
                        act.wait_ge(s_el, gi - 1)
                    func = (ACT.Tanh, ACT.Gelu, ACT.Silu)[i // FE]
                    nc.scalar.activation(ea[gi % 2][:], ps[:, 4 + gi % 2, :], func,
                                         bias=smallc[:, B1C + i:B1C + i + 1]).then_inc(s_ea, 1)
                    act.wait_ge(s_ea, gi + 1)
                    if gi >= 2:
                        act.wait_ge(s_e2, gi - 1)
                    evac(eah[gi % 2][:], ea[gi % 2][:], s_eh)
                ln_std(("M", b))
                stage_end(act, 6 + b)

        @block.vector
        def _(dve):
            steps = [0]

            def step(ins):
                steps[0] += 1
                ins.then_inc(s_chain, 1)
                dve.wait_ge(s_chain, steps[0])

            def sub(out, a, hi, sm):
                return nc.vector.tensor_tensor(out, a, f32(hi), ALU.subtract).then_inc(sm, 1)

            def split_lo(n, out, hi):
                cols = chunks[n][2]
                dve.wait_ge(s_whi, n + 1)
                sub(out, raw[n % RING][:, 0:cols], hi, s_wlo)

            def tp_lo(key, scale=None):
                n = TP[key]
                for h in range(HT):
                    dve.wait_ge(s_tphi, 4 * n + h + 1)
                    if scale is None:
                        sub(XTl[:, h, :], ps[:, h, :], XTh[:, h, :], s_tplo)
                    else:
                        nc.vector.scalar_tensor_tensor(XTl[:, h, :], ps[:, h, :], scale[:, h:h + 1],
                                                       f32(XTh[:, h, :]), ALU.mult, ALU.subtract).then_inc(s_tplo, 1)

            def layer_norm(key, z, out):
                for t in range(T):
                    last = nc.vector.bn_stats(stats[:, t, :], z[:, t, :])
                step(last)
                for t in range(T):
                    last = nc.vector.bn_aggr(mv[:, t, :], stats[:, t, :])
                last.then_inc(s_var, 1)
                dve.wait_ge(s_std, LN[key] + 1)
                step(nc.vector.reciprocal(rstd[:], std[:]))
                for t in range(T):
                    nc.vector.tensor_scalar(out[:, t, :], z[:, t, :], mv[:, t, 0:1], rstd[:, t:t + 1], ALU.subtract,
                                            ALU.mult).then_inc(s_lnout, 1)
                dve.wait_ge(s_lnout, 4 * (LN[key] + 1))

            flat = lambda t: t[:].rearrange("p a n -> p (a n)")
            split_lo(0, flat(w0l), flat(w0h))
            dve.wait_ge(s_const, 4)
            nc.vector.tensor_copy(identb[:], ident[:]).then_inc(s_const, 1)
            for b in range(B):
                dve.wait_ge(s_x_in[b], 32)
                for h in range(HT):
                    dve.wait_ge(s_tphi, 4 * b + h + 1)
                    sub(XTl[:, h, :], xT[:, h, :], XTh[:, h, :], s_tplo)
                if b == 0:
                    split_lo(1, wo0l[:], wo0h[:])
                dve.wait_ge(s_const_dma, 16 * N_CONST_DMA)
                step(nc.vector.tensor_tensor(xb0[:], xs[b][:], bo0[:, None, :].to_broadcast([P, T, H]), ALU.add))
                for k, (lo, hi) in enumerate(((QTl, QTh), (KTl, KTh))):
                    dve.wait_ge(s_a0act, 3 * b + k + 1)
                    nc.vector.scalar_tensor_tensor(lo[:], ps[:, 4 + k, :], smallc[:, BQ + k:BQ + k + 1], f32(hi[:]),
                                                   ALU.add, ALU.subtract).then_inc(s_a0lo, 1)
                dve.wait_ge(s_a0vhi, b + 1)
                sub(flat(Vl0), ps[:, 7, :], flat(Vh0), s_a0vlo)
                for q in range(T):
                    dve.wait_ge(s_a0s, T * b + q + 1)
                    step(nc.vector.reduce_max(mx0[:, q:q + 1], ps[:, q, :], AX.X))
                    nc.vector.tensor_scalar(nm0[:, q:q + 1], mx0[:, q:q + 1], -SCALE0, None,
                                            ALU.mult).then_inc(s_a0nm, 1)
                for k in range(T):
                    dve.wait_ge(s_a0pthi, T * b + k + 1)
                    sub(PTl[:, k, :], ps[:, 4 + k, :], PTh[:, k, :], s_a0ptlo)
                dve.wait_ge(s_a0othi, b + 1)
                sub(OTl[:], ps[:, 0, :], OTh[:], s_a0otlo)
                dve.wait_ge(s_a0p, T * (b + 1))
                step(nc.vector.reciprocal(rs0[:], sum0[:]))
                for t in range(T):
                    dve.wait_ge(s_y, 4 * Y["A0", b] + t + 1)
                    last = nc.vector.scalar_tensor_tensor(xs[b][:, t, :], ps[:, 4 + t, :], rs0[:, t:t + 1],
                                                          xb0[:, t, :], ALU.mult, ALU.add)
                step(last)
                layer_norm(("A0", b), xs[b], xs[b])
                stage_end(dve, b)
            n = 2
            for b in range(B):
                dve.wait_ge(s_fss, b + 1)
                step(nc.vector.reciprocal(ss[:], rr[:]))
                for t in range(T):
                    nc.vector.tensor_scalar(nx[:, t, :], xs[b][:, t, :], ss[:, t:t + 1], None,
                                            ALU.mult).then_inc(s_fnx, 1)
                split_lo(n, fwl[(b * NI) % WSLOTS][:], fwh[(b * NI) % WSLOTS][:])
                tp_lo(("F0", b), smallc[:, LNW:LNW + HT])
                for i in range(NI):
                    gi = b * NI + i
                    if i + 1 < NI:
                        split_lo(n + 1, fwl[(gi + 1) % WSLOTS][:], fwh[(gi + 1) % WSLOTS][:])
                    n += 1
                    dve.wait_ge(s_fsg, gi + 1)
                    dve.wait_ge(s_fu, gi + 1)
                    nc.vector.tensor_tensor(hh[gi % 2][:], sg[gi % 2][:], ps[:, 6 + gi % 2, :],
                                            ALU.mult).then_inc(s_fh, 1)
                    dve.wait_ge(s_fhi, gi + 1)
                    sub(hlo[gi % 2][:], hh[gi % 2][:], hhi[gi % 2][:], s_flo)
                dve.wait_ge(s_fdn, NI * (b + 1))
                for t in range(T):
                    last = nc.vector.tensor_tensor(xs[b][:, t, :], ps[:, t, :], xs[b][:, t, :], ALU.add)
                step(last)
                layer_norm(("F0", b), xs[b], xs[b])
                stage_end(dve, 2 + b)
            for b in range(B):
                for k in range(2):
                    sl = slice(2 * k, 2 * k + 2)
                    split_lo(n, w1l[:, sl, :].rearrange("p a n -> p (a n)"),
                             w1h[:, sl, :].rearrange("p a n -> p (a n)"))
                    n += 1
                tp_lo(("A1", b))
                dve.wait_ge(s_a1d, 64)
                dve.wait_ge(s_init, b + 2)
                for t in range(T):
                    bt = b * T + t
                    dve.wait_ge(s_q, bt + 1)
                    if bt % T:
                        dve.wait_ge(s_qhi, bt)
                    nc.vector.tensor_tensor(qkv[:], ps[:, 2 * (t % 2):2 * (t % 2) + 2, :].rearrange(
                        "p a n -> p (a n)")[:, 0:QKV1], bq1[:], ALU.add).then_inc(s_qe, 1)
                    dve.wait_ge(s_qe, bt + 1)
                    nqk = NH + NKV
                    x4 = qkv[:, 0:640].rearrange("p (h i c) -> p h i c", h=nqk, c=2)
                    c4 = cosb[:, t, None, :].to_broadcast([P, nqk, HD]).rearrange("p h (i c) -> p h i c", c=2)
                    n4 = sinb[:, t, None, :].to_broadcast([P, nqk, HD]).rearrange("p h (i c) -> p h i c", c=2)
                    v4 = lambda tt: tt[:].rearrange("p (h i c) -> p h i c", h=nqk, c=2)
                    nc.vector.tensor_tensor(v4(t1), x4, c4, ALU.mult)
                    step(nc.vector.tensor_tensor(v4(t2), x4[:, :, :, ::-1], n4, ALU.mult))
                    nc.vector.tensor_tensor(rot[:], t1[:], t2[:], ALU.add).then_inc(s_rot, 1)
                    v = qkv[:, 640:768].rearrange("p (g d) -> p g d", d=HD)
                    r3 = vr[:].rearrange("p (g d) -> p g d", d=HD)
                    part = lambda k: Vs[:, t, :, k * HD:(k + 1) * HD]
                    step(nc.vector.tensor_copy(part(0), v))
                    step(nc.vector.tensor_tensor(r3, v, part(0), ALU.subtract))
                    step(nc.vector.tensor_copy(part(1), r3))
                    nc.vector.tensor_tensor(part(2), r3, part(1), ALU.subtract).then_inc(s_v, 1)
                    dve.wait_ge(s_qhi, bt + 1)
                    r = rot[:, 0:NH * HD].rearrange("p (h d) -> p h d", d=HD)
                    o = Qs0[:].rearrange("p h (k d) -> p h k d", d=HD)
                    nc.vector.tensor_tensor(o[:, :, 1, :], r, f32(o[:, :, 0, :]), ALU.subtract)
                    r = rot[:, NH * HD:].rearrange("p (h d) -> p h d", d=HD)
                    o = (Ks0, Ks1)[t % 2][:].rearrange("p h (k d) -> p h k d", d=HD)
                    nc.vector.tensor_tensor(o[:, :, 2, :], r, f32(o[:, :, 0, :]), ALU.subtract).then_inc(s_qlo, 1)
                    u = 5 * bt + 4
                    dve.wait_ge(s_tq, u + 1)
                    src = ps[:, 4 + u % 4, :].rearrange("p (a q) -> p a q", a=4)
                    for s in range(2):
                        last = nc.vector.tensor_copy(Kop[HR * s:HR * s + HR, s::2, t * P:(t + 1) * P],
                                                     src[HR * s:HR * s + HR])
                    last.then_inc(s_ek, 1)
                for p in range(PAIRS):
                    for u in range(3):
                        n_u = (b * PAIRS + p) * 3 + u
                        r0 = 2 * (n_u % 2)
                        dve.wait_ge(s_s1, n_u + 1)
                        if u < 2:
                            q = 3 - u
                            last = nc.vector.reduce_max(mtok[:, :, p, q],
                                                        ps[:, r0:r0 + 2, 0:(q + 1) * P], AX.X)
                        else:
                            for q in range(2):
                                w = (q + 1) * P
                                last = nc.vector.reduce_max(
                                    mtok[:, :, p, q],
                                    ps[:, r0 + q, 0:2 * w].rearrange("p (s k) -> p s k", s=2), AX.X)
                        last.then_inc(s_mx, 1)
                dve.wait_ge(s_mth, b + 1)
                sub(mTl[:], ps[:, 4, 0:P], mTh[:], s_mtl)

                def read_out(gg):
                    for k in range(2):
                        n_o = 2 * (b * NKV + gg) + k
                        dve.wait_ge(s_o, n_o + 1)
                        src = ps[:, 6 + k, 0:8 * VW].rearrange("p (h c) -> p h c", c=VW)
                        nc.vector.reciprocal(orec[:], src[:, :, VW - 1])
                        step(nc.vector.tensor_reduce(osum[:], src[:, :, 0:3 * HD].rearrange(
                            "p h (k d) -> p h d k", k=3), AX.X, ALU.add))
                        G, s = gg // 2, gg % 2
                        dst = Otok[:, 2 * k:2 * k + 2, :].rearrange("p t (g j s d) -> p t g j s d", g=4, j=4, s=2)
                        nc.vector.tensor_tensor(
                            dst[:, :, G, :, s, :], osum[:].rearrange("p (t j) d -> p t j d", t=2),
                            orec[:].rearrange("p (t j) -> p t j", t=2)[:, :, :, None].to_broadcast([P, 2, 4, HD]),
                            ALU.mult).then_inc(s_oe, 1)
                        dve.wait_ge(s_oe, n_o + 1)

                for gg in range(NKV):
                    for u in range(6):
                        n_u = (b * NKV + gg) * 6 + u
                        dve.wait_ge(s_ph, n_u + 1)
                        sl = slice(UO[u], UO[u] + UW[u])
                        nc.vector.tensor_tensor(Pl[gg % 2][:, sl], Pf[n_u % 3][:, 0:UW[u]], Ph[gg % 2][:, sl],
                                                ALU.subtract).then_inc(s_pl, 1)
                    if gg:
                        read_out(gg - 1)
                read_out(NKV - 1)
                for k in range(2):
                    sl = slice(2 * k, 2 * k + 2)
                    split_lo(n, wo1l[:, sl, :].rearrange("p a n -> p (a n)"),
                             wo1h[:, sl, :].rearrange("p a n -> p (a n)"))
                    n += 1
                tp_lo(("O1", b))
                step(nc.vector.tensor_tensor(xs[b][:], xs[b][:], bo1[:, None, :].to_broadcast([P, T, H]), ALU.add))
                for t in range(T):
                    dve.wait_ge(s_y, 4 * Y["A1", b] + t + 1)
                    last = nc.vector.tensor_tensor(xs[b][:, t, :], ps[:, 4 + t, :], xs[b][:, t, :], ALU.add)
                step(last)
                layer_norm(("A1", b), xs[b], xs[b])
                stage_end(dve, 4 + b)
            for b in range(B):
                x = xs[b]
                dve.wait_ge(s_gwd, 64)
                if b == 0:
                    dve.wait_ge(s_gw, 1)
                    sub(flat(gwl), flat(gwr), flat(gwh), s_gw)
                tp_lo(("M", b))
                step(nc.vector.tensor_reduce(asum[:], x[:], AX.X, ALU.add, apply_absolute_value=True))
                step(nc.vector.tensor_tensor(wsum[:, 0, :],
                                             asum[:], awt[:, 0, :], ALU.mult))
                step(nc.vector.tensor_tensor(wsum[:, 1, :], asum[:], awt[:, 1, :], ALU.mult))
                for k in range(2):
                    last = nc.vector.reduce_sum(asum2[:, k:k + 1], wsum[:, k, :], AX.X)
                last.then_inc(s_as, 1)
                dve.wait_ge(s_rkb, 3 * b + 1)
                step(nc.vector.tensor_scalar(rat[:, 1:2], ps[:, 6, 1:2], 1e-8, None, ALU.add))
                step(nc.vector.reciprocal(rat[:, 1:2], rat[:, 1:2]))
                step(nc.vector.tensor_tensor(rat[:, 0:1], ps[:, 6, 0:1], rat[:, 1:2], ALU.mult))
                step(nc.vector.scalar_tensor_tensor(lg[:, 0, :], gb[:, 0, :], rat[:, 0:1], gb[:, 1, :], ALU.mult,
                                                    ALU.add))
                dve.wait_ge(s_lg, b + 1)
                logits = ps[:, 5, :].rearrange("p (t e) -> p t e", t=T)[:, :, 0:E]
                step(nc.vector.tensor_tensor(g[2][:], logits, lg[:, 0:1, :].to_broadcast([P, T, E]), ALU.add))
                col = lambda t, k: t[:, :, k:k + 1]
                bc = lambda a: a.to_broadcast([P, T, E])
                tt = nc.vector.tensor_tensor
                step(nc.vector.reduce_max(g[3][:, :, 0:1], g[2][:], AX.X))
                tt(g[0][:], g[2][:], bc(col(g[3], 0)), ALU.subtract).then_inc(s_rk, 1)
                dve.wait_ge(s_rt, b + 1)
                step(nc.vector.reduce_sum(g[3][:, :, 1:2], g[1][:], AX.X))
                step(nc.vector.reciprocal(g[3][:, :, 2:3], g[3][:, :, 1:2]))
                step(tt(g[4][:], g[1][:], bc(col(g[3], 2)), ALU.mult))
                a, c, d = (col(g[4], k) for k in range(3))
                tt(col(g[6], 0), a, c, ALU.max)
                step(tt(col(g[6], 1), a, c, ALU.min))
                step(tt(col(g[6], 2), col(g[6], 0), d, ALU.min))
                tt(col(g[5], 0), col(g[6], 0), d, ALU.max)
                step(tt(col(g[5], 1), col(g[6], 1), col(g[6], 2), ALU.max))
                tt(col(g[7], 0), a, c, ALU.is_lt)
                tt(col(g[7], 1), a, d, ALU.is_lt)
                step(tt(col(g[7], 2), c, d, ALU.is_lt))
                step(nc.vector.tensor_scalar(g[8][:], g[7][:], -1.0, 1.0, ALU.mult, ALU.add))
                tt(col(g[9], 0), col(g[7], 0), col(g[7], 1), ALU.add)
                tt(col(g[9], 1), col(g[8], 0), col(g[7], 2), ALU.add)
                tt(col(g[9], 2), col(g[8], 1), col(g[8], 2), ALU.add).then_inc(s_rk, 1)
                step(tt(col(g[10], 0), col(g[5], 0), col(g[5], 1), ALU.add))
                step(nc.vector.tensor_scalar(col(g[10], 1), col(g[10], 0), 1e-8, None, ALU.add))
                step(nc.vector.reciprocal(col(g[10], 2), col(g[10], 1)))
                step(tt(g[11][:, :, 0:2], g[5][:, :, 0:2], col(g[10], 2).to_broadcast([P, T, 2]), ALU.mult))
                dve.wait_ge(s_rkb, 3 * b + 3)
                rank = ps[:, 7, 0:E]
                nc.vector.tensor_scalar(g[12][:, 0, :], rank, 0.0, None, ALU.is_equal)
                step(nc.vector.tensor_scalar(g[13][:, 0, :], rank, 1.0, None, ALU.is_equal))
                tt(g[14][:], g[12][:, 0:1, :].to_broadcast([P, T, E]), bc(col(g[11], 0)), ALU.mult)
                step(tt(g[15][:], g[13][:, 0:1, :].to_broadcast([P, T, E]), bc(col(g[11], 1)), ALU.mult))
                step(tt(g[16][:], g[14][:], g[15][:], ALU.add))
                w = g[16]
                for t in range(T):
                    last = nc.vector.scalar_tensor_tensor(zacc[:, t, :], b2b[:, 0, :], w[:, t, 0:1], x[:, t, :],
                                                          ALU.mult, ALU.add)
                step(last)
                for e in (1, 2):
                    for t in range(T):
                        last = nc.vector.scalar_tensor_tensor(zacc[:, t, :], b2b[:, e, :], w[:, t, e:e + 1],
                                                              zacc[:, t, :], ALU.mult, ALU.add)
                    step(last)
                split_lo(n, mwl[(b * E * FE) % WSLOTS][:], mwh[(b * E * FE) % WSLOTS][:])
                for i in range(E * FE):
                    gi = b * E * FE + i
                    if i + 1 < E * FE:
                        split_lo(n + 1, mwl[(gi + 1) % WSLOTS][:], mwh[(gi + 1) % WSLOTS][:])
                    n += 1
                    dve.wait_ge(s_eh, gi + 1)
                    sub(eal[gi % 2][:], ea[gi % 2][:], eah[gi % 2][:], s_el)
                    if i % FE == FE - 1:
                        e = i // FE
                        dve.wait_ge(s_e2, gi + 1)
                        for t in range(T):
                            last = nc.vector.scalar_tensor_tensor(zacc[:, t, :], ps[:, t, :], w[:, t, e:e + 1],
                                                                  zacc[:, t, :], ALU.mult, ALU.add)
                        last.then_inc(s_acc, 1)
                        dve.wait_ge(s_acc, b * E + e + 1)
                layer_norm(("M", b), zacc, x)
                stage_end(dve, 6 + b)

        @block.tensor
        def _(pe):
            mm = nc.tensor.matmul

            def mm3(out, lh, ll, rh, rl, first, last):
                mm(out, lh, rh, start=first, stop=False)
                mm(out, ll, rh, start=False, stop=False)
                return mm(out, lh, rl, start=False, stop=last)

            def transposes(key, src):
                for h in range(HT):
                    for t in range(T):
                        last = nc.tensor.transpose(ps[:, h, t * P:(t + 1) * P], src[:, t, h * P:(h + 1) * P], ident[:])
                    last.then_inc(s_tp, 1)

            def xt_ready(key, h):
                pe.wait_ge(s_tplo, 4 * TP[key] + h + 1)

            tok = lambda t: slice(t * P, (t + 1) * P)
            pe.wait_ge(s_const, 5)
            for b in range(B):
                pe.wait_ge(s_wlo, 1)
                for k in range(3):
                    for h in range(HT):
                        if k == 0:
                            xt_ready(("A0", b), h)
                        c = slice(k * D0, (k + 1) * D0)
                        last = mm3(ps[:, 4 + k, :], w0h[:, h, c], w0l[:, h, c], XTh[:, h, :], XTl[:, h, :], h == 0,
                                   h == HT - 1)
                    last.then_inc(s_a0qkv, 1)
                pe.wait_ge(s_a0lo, 2 * (b + 1))
                for q in range(T):
                    mm3(ps[:, q, :], QTh[:, tok(q)], QTl[:, tok(q)], KTh[:], KTl[:], True, True).then_inc(s_a0s, 1)
                pe.wait_ge(s_a0act, 3 * (b + 1))
                for t in range(T):
                    last = nc.tensor.transpose(ps[:, 7, tok(t)], vT[:, tok(t)], ident[:])
                last.then_inc(s_a0vt, 1)
                pe.wait_ge(s_a0p, T * (b + 1))
                pe.wait_ge(s_a0vlo, b + 1)
                for k in range(T):
                    for q in range(T):
                        last = nc.tensor.transpose(ps[:, 4 + k, tok(q)], P0[:, q, tok(k)], ident[:])
                    last.then_inc(s_a0pt, 1)
                for k in range(T):
                    pe.wait_ge(s_a0ptlo, T * b + k + 1)
                    last = mm3(ps[:, 0, :], Vh0[:, k, :], Vl0[:, k, :], PTh[:, k, :], PTl[:, k, :], k == 0, k == T - 1)
                last.then_inc(s_a0ot, 1)
                pe.wait_ge(s_a0otlo, b + 1)
                pe.wait_ge(s_wlo, 2)
                for t in range(T):
                    mm3(ps[:, 4 + t, :], OTh[:, tok(t)], OTl[:, tok(t)], wo0h[:], wo0l[:], True,
                        True).then_inc(s_y, 1)
                stage_end(pe, b)
            n = 2
            for b in range(B):
                pe.wait_ge(s_fnx, T * (b + 1))
                transposes(("F0", b), nx)

                def down(gi):
                    pe.wait_ge(s_flo, gi + 1)
                    i = gi % NI
                    for t in range(T):
                        last = mm3(ps[:, t, :], hhi[gi % 2][:, tok(t)], hlo[gi % 2][:, tok(t)],
                                   fwh[gi % WSLOTS][:, 2 * H:], fwl[gi % WSLOTS][:, 2 * H:], i == 0, i == NI - 1)
                    last.then_inc(s_fdn, 1)

                for i in range(NI):
                    gi = b * NI + i
                    pe.wait_ge(s_wlo, n + 1)
                    n += 1
                    if gi >= 2:
                        pe.wait_ge(s_fsg, gi - 1)
                        pe.wait_ge(s_fh, gi - 1)
                    for k, sm in enumerate((s_fg, s_fu)):
                        for h in range(HT):
                            if i == 0 and k == 0:
                                xt_ready(("F0", b), h)
                            c = slice(k * H + h * P, k * H + (h + 1) * P)
                            last = mm3(ps[:, 4 + 2 * k + gi % 2, :], fwh[gi % WSLOTS][:, c], fwl[gi % WSLOTS][:, c],
                                       XTh[:, h, :], XTl[:, h, :], h == 0, h == HT - 1)
                        last.then_inc(sm, 1)
                    if i:
                        down(gi - 1)
                down(b * NI + NI - 1)
                stage_end(pe, 2 + b)
            for b in range(B):
                transposes(("A1", b), xs[b])
                n += 2
                pe.wait_ge(s_wlo, n)
                for h in range(HT):
                    xt_ready(("A1", b), h)

                def project(t):
                    bt = b * T + t
                    if t >= 2:
                        pe.wait_ge(s_qe, bt - 1)
                    r0 = 2 * (t % 2)
                    for c0, c1, bank in ((0, 512, r0), (512, QKV1, r0 + 1)):
                        for h in range(HT):
                            last = mm3(ps[:, bank, 0:c1 - c0], XTh[:, h, tok(t)], XTl[:, h, tok(t)],
                                       w1h[:, h, c0:c1], w1l[:, h, c0:c1], h == 0, h == HT - 1)
                    last.then_inc(s_q, 1)

                def operands(t):
                    bt = b * T + t
                    pe.wait_ge(s_qlo, bt + 1)
                    for k in range(5):
                        u = 5 * bt + k
                        if u % (5 * T) >= 4:
                            v = u - 4
                            if v % 5 == 4:
                                pe.wait_ge(s_ek, v // 5 + 1)
                            else:
                                pe.wait_ge(s_eq, 4 * (v // 5) + v % 5 + 1)
                        for a in range(4):
                            if k < 4:
                                src = Qs0[:, 8 * k + 2 * a:8 * k + 2 * a + 2, :]
                            else:
                                src = (Ks0, Ks1)[t % 2][:, 2 * a:2 * a + 2, :]
                            last = nc.tensor.transpose(ps[:, 4 + u % 4, tok(a)],
                                                       f32(src.rearrange("p a n -> p (a n)")), ident[:])
                        last.then_inc(s_tq, 1)

                for t in range(T):
                    project(t)
                    if t:
                        operands(t - 1)
                operands(T - 1)
                pe.wait_ge(s_eq, 16 * (b + 1))
                pe.wait_ge(s_ek, T * (b + 1))
                for p in range(PAIRS):
                    G = p // 4
                    for u in range(3):
                        n_u = (b * PAIRS + p) * 3 + u
                        r0 = 2 * (n_u % 2)
                        if n_u % (3 * PAIRS) >= 2:
                            pe.wait_ge(s_mx, n_u - 1)
                        if u < 2:
                            q = 3 - u
                            for s in range(2):
                                mm(ps[:, r0 + s, 0:(q + 1) * P], Qop[:, p, tok(q)], Kop[:, 2 * G + s, 0:(q + 1) * P],
                                   start=True, stop=False)
                                last = mm(ps[:, r0 + s, q * P:(q + 1) * P], identb[:], maskb[:], start=False,
                                          stop=True)
                        else:
                            for q in range(2):
                                w = (q + 1) * P
                                out = ps[:, r0 + q, 0:2 * w].rearrange("p (s k) -> p s k", s=2)
                                mm(out, Qop[:, p, tok(q)], Kop[:, 2 * G:2 * G + 2, 0:w], start=True, stop=False)
                                last = mm(out[:, :, q * P:w], identb[:], maskb[:, None, :].to_broadcast([P, 2, P]),
                                          start=False, stop=True)
                        last.then_inc(s_s1, 1)
                pe.wait_ge(s_mx, 3 * PAIRS * (b + 1))
                nc.tensor.transpose(ps[:, 4, 0:P], mtok[:].rearrange("p s h t -> p (s h t)"), ident[:]).then_inc(s_mt, 1)
                pe.wait_ge(s_mtl, b + 1)
                pe.wait_ge(s_md, 64 * (b + 1))

                def scores(gg):
                    G, s = gg // 2, gg % 2
                    for u in range(6):
                        n_u = (b * NKV + gg) * 6 + u
                        r0 = 2 * (n_u % 3)
                        if n_u % (6 * NKV) >= 3:
                            pe.wait_ge(s_p, n_u - 2)
                        kt = (0, 0, 1, 1, 2, 3)[u]
                        lhsT = Kop[:, 2 * G + s, tok(kt)]
                        if u < 4:
                            for a in range(2):
                                j = 2 * (u % 2) + a
                                last = mm(ps[:, r0 + a, 0:S - kt * P], lhsT, Qop[:, 4 * G + j, kt * P:S],
                                          start=True, stop=True)
                        elif u == 4:
                            for a in range(2):
                                j = 4 * G + 2 * a
                                last = mm(ps[:, r0 + a, :].rearrange("p (j q) -> p j q", j=2), lhsT,
                                          Qop[:, j:j + 2, 2 * P:S], start=True, stop=True)
                        else:
                            last = mm(ps[:, r0, :].rearrange("p (j q) -> p j q", j=4), lhsT,
                                      Qop[:, 4 * G:4 * G + 4, 3 * P:S], start=True, stop=True)
                        last.then_inc(s_s2, 1)

                def values(gg):
                    gi = b * NKV + gg
                    pe.wait_ge(s_pl, 6 * (gi + 1))
                    if gg:
                        pe.wait_ge(s_oe, 2 * gi)
                    for q in range(T):
                        for j in range(4):
                            c = ((q % 2) * 4 + j) * VW
                            out = ps[:, 6 + q // 2, c:c + VW]
                            for kt in range(q + 1):
                                o = (UO[j // 2] + (j % 2) * 512 + q * P, UO[2 + j // 2] + (j % 2) * 384 + (q - 1) * P,
                                     UO[4] + j * 256 + (q - 2) * P, UO[5] + j * P)[kt]
                                for part in (Ph, Pl):
                                    last = mm(out, part[gg % 2][:, o:o + P], Vs[:, kt, gg, :],
                                              start=kt == 0 and part is Ph, stop=kt == q and part is Pl)
                        if q % 2:
                            last.then_inc(s_o, 1)

                for gg in range(NKV):
                    scores(gg)
                    if gg:
                        values(gg - 1)
                values(NKV - 1)
                pe.wait_ge(s_oe, 2 * NKV * (b + 1))
                transposes(("O1", b), Otok)
                n += 2
                pe.wait_ge(s_wlo, n)
                for h in range(HT):
                    xt_ready(("O1", b), h)
                for t in range(T):
                    for h in range(HT):
                        last = mm3(ps[:, 4 + t, :], XTh[:, h, tok(t)], XTl[:, h, tok(t)], wo1h[:, h, :], wo1l[:, h, :],
                                   h == 0, h == HT - 1)
                    last.then_inc(s_y, 1)
                stage_end(pe, 4 + b)
            for b in range(B):
                transposes(("M", b), xs[b])
                pe.wait_ge(s_gw, 2)
                for h in range(HT):
                    xt_ready(("M", b), h)
                    last = mm3(ps[:, 4, :], gwh[:, h, :], gwl[:, h, :], XTh[:, h, :], XTl[:, h, :], h == 0,
                               h == HT - 1)
                last.then_inc(s_lgT, 1)
                pe.wait_ge(s_as, b + 1)
                mm(ps[:, 6, 0:2], onesf[:], asum2[:], start=True, stop=True).then_inc(s_rkb, 1)
                pe.wait_ge(s_lgTe, b + 1)
                for t in range(T):
                    last = nc.tensor.transpose(ps[:, 5, tok(t)], lgT[:, tok(t)], ident[:])
                last.then_inc(s_lg, 1)
                pe.wait_ge(s_rk, 2 * (b + 1))
                mm(ps[:, 7, 0:E], row0[:], g[9][:, 0, :], start=True, stop=True).then_inc(s_rkb, 2)

                def second(gi):
                    i = gi % (E * FE)
                    pe.wait_ge(s_el, gi + 1)
                    if i % FE == 0 and gi >= FE:
                        pe.wait_ge(s_acc, gi // FE)
                    for t in range(T):
                        last = mm3(ps[:, t, :], eah[gi % 2][:, tok(t)], eal[gi % 2][:, tok(t)],
                                   mwh[gi % WSLOTS][:, H:], mwl[gi % WSLOTS][:, H:], i % FE == 0, i % FE == FE - 1)
                    last.then_inc(s_e2, 1)

                for i in range(E * FE):
                    gi = b * E * FE + i
                    pe.wait_ge(s_wlo, n + 1)
                    n += 1
                    if gi >= 2:
                        pe.wait_ge(s_ea, gi - 1)
                    for h in range(HT):
                        last = mm3(ps[:, 4 + gi % 2, :], mwh[gi % WSLOTS][:, tok(h)], mwl[gi % WSLOTS][:, tok(h)], XTh[:, h, :],
                                   XTl[:, h, :], h == 0, h == HT - 1)
                    last.then_inc(s_pre, 1)
                    if i:
                        second(gi - 1)
                second(b * E * FE + E * FE - 1)
                stage_end(pe, 6 + b)


_IN = ("x", "xT", "smallc", "bo0", "w_qkv0", "w_o0", "w_ffn", "cosb", "sinb", "bq1", "bo1",
       "w_qkv1", "w_o1", "gwr", "awt", "b2", "gb", "w_moe")


def tiles(w):
    return np.ascontiguousarray(w.reshape(-1, P, w.shape[1]).transpose(1, 0, 2)).reshape(P, -1)


def lay_out(a):
    f = np.float32
    x = a["L0_attn_x"]
    heads = np.arange(NH * HD).reshape(NKV // 2, 2, GROUP, HD).transpose(0, 2, 1, 3).reshape(-1)
    cols = np.concatenate([heads, np.arange(NH * HD, QKV1)])
    inv = 1.0 / 10000.0 ** (np.arange(0, HD, 2, dtype=f) / HD)
    ang = np.arange(S, dtype=f)[:, None] * inv[None, :].astype(f)
    cos = np.repeat(np.cos(ang).astype(f), 2, axis=1)
    sin = np.stack([-np.sin(ang), np.sin(ang)], axis=-1).astype(f).reshape(S, HD)
    by_tile = lambda v: np.ascontiguousarray(v.reshape(T, P, -1).transpose(1, 0, 2))
    smallc = np.zeros((P, 64), f)
    smallc[:, 0:3] = a["L0_attn_bqkv"].reshape(3, P).T
    smallc[:, 3:7] = a["L0_ffn_ln_w"].reshape(HT, P).T
    smallc[:, 8:20] = a["L1_ffn_b1"].reshape(E * FE, P).T
    gate, up, down = (a["L0_ffn_" + k] for k in ("gate_w", "up_w", "down_w"))
    w_ffn = np.concatenate([
        gate.reshape(NI, P, HT, P).transpose(0, 3, 2, 1).reshape(NI, P, H),
        up.reshape(NI, P, HT, P).transpose(0, 3, 2, 1).reshape(NI, P, H),
        down.T.reshape(NI, P, H)], axis=2)
    w_qkv1 = tiles(a["L1_attn_w_qkv"][cols].T).reshape(P, 2, CHUNK).transpose(1, 0, 2)
    w_o1 = tiles(a["L1_attn_w_o"].T[heads]).reshape(P, 2, 2 * H).transpose(1, 0, 2)
    w1, w2 = a["L1_ffn_w1"], a["L1_ffn_w2"]
    w_moe = np.concatenate([
        w1.reshape(E, HT, P, FE, P).transpose(0, 3, 2, 1, 4).reshape(E * FE, P, H),
        w2.reshape(E * FE, P, H)], axis=2)
    gwr = np.zeros((P, HT, P), f)
    gwr[:, :, 0:E] = a["L1_ffn_gate_w"][0:H].reshape(HT, P, E).transpose(1, 0, 2)
    text = (np.arange(S) >= VISION).astype(f)
    awt = np.stack([text / ((S - VISION) * H), (1 - text) / (VISION * H)]).astype(f)
    return {
        "x": x.reshape(B, T, P, H).transpose(0, 2, 1, 3),
        "xT": x.transpose(0, 2, 1).reshape(B, HT, P, S).transpose(0, 2, 1, 3),
        "smallc": smallc,
        "bo0": a["L0_attn_bo"], "w_qkv0": tiles(a["L0_attn_Wqkv"]), "w_o0": a["L0_attn_Wo"], "w_ffn": w_ffn,
        "cosb": by_tile(cos), "sinb": by_tile(sin),
        "bq1": a["L1_attn_b_qkv"][cols], "bo1": a["L1_attn_b_o"], "w_qkv1": w_qkv1, "w_o1": w_o1,
        "gwr": gwr, "awt": awt.reshape(2, T, P).transpose(2, 0, 1), "b2": a["L1_ffn_b2"],
        "gb": np.stack([a["L1_ffn_gate_w"][H], a["L1_ffn_gate_b"]]), "w_moe": w_moe,
    }


def kernel(**inputs):
    import concourse.bacc as bacc
    from concourse.bass_utils import run_bass_kernel_spmd

    nc = bacc.Bacc("TRN2", target_bir_lowering=False, num_devices=1)
    arrays = {n: np.ascontiguousarray(v) for n, v in lay_out({k: np.asarray(v) for k, v in inputs.items()}).items()}
    dram = {n: nc.dram_tensor(f"in_{n}", arrays[n].shape, mybir.dt.from_np(arrays[n].dtype),
                              kind="ExternalInput").ap() for n in _IN}
    dram["out"] = nc.dram_tensor("out_0", (B, P, T, H), F32, kind="ExternalOutput").ap()
    post_ln_layers(nc, dram)
    r = run_bass_kernel_spmd(nc, [{f"in_{n}": arrays[n] for n in _IN}], core_ids=[0])
    return r.results[0]["out_0"].transpose(0, 2, 1, 3).reshape(B, S, H)
```

```python
from contextlib import ExitStack

import numpy as np

import concourse.bass as bass
from concourse import mybir
from concourse.alu_op_type import AluOpType as ALU

ACT = mybir.ActivationFunctionType
F32 = mybir.dt.float32
F32R = mybir.dt.float32r
BF16 = mybir.dt.bfloat16
F16 = mybir.dt.float16
AX = mybir.AxisListType

P = 128
B = 2
S = 512
H = 512
T = S // P
HT = H // P
D0 = H // 4
F = 1792
NI = F // P
NH, NKV, HD = 32, 8, 16
GROUP = NH // NKV
PAIRS = NH // 2
HR = 64
E = 3
FE = H // P
VW = 3 * HD + 1
QK = (NH + NKV) * HD
QKV1 = QK + NKV * HD
LN_EPS = 1e-5
RMS_EPS = 1e-5
SCALE0 = float(D0) ** -0.5
SCALE1 = float(HD) ** -0.5
SHIFT1 = 14 * float(np.log(2.0))
MASKED = -1e30
RING = 4
CHUNK = 3 * H
VISION = int(S * 0.3)
UW = (1024, 1024, 768, 768, 1024, 512)
UO = tuple(sum(UW[:u]) for u in range(6))
WSLOTS = 3


def split_chunks():
    chunks = [("w_qkv0", None, HT * 3 * D0), ("w_o0", None, H)]
    for b in range(B):
        chunks += [("w_ffn", i, 3 * H) for i in range(NI)]
    for b in range(B):
        chunks += [("w_qkv1", i, CHUNK) for i in range(2)] + [("w_o1", i, 2 * H) for i in range(2)]
    for b in range(B):
        chunks += [("w_moe", i, 2 * H) for i in range(E * FE)]
    return chunks


def post_ln_layers(nc, dram):
    chunks = split_chunks()
    FIRST = {}
    for n, (name, i, _) in enumerate(chunks):
        FIRST.setdefault((name, i), []).append(n)
    ctx = ExitStack()
    with ctx:
        offset = [(nc.sbuf_base + 63) // 64 * 64]
        limit = nc.sbuf_usable_end

        def at(name, shape, dt, off):
            return nc.alloc_sbuf_tensor_at(name, shape, dt, offset=off)

        def size(shape, dt):
            n = int(np.prod(shape[1:])) * (2 if dt in (BF16, F16) else 4)
            return (n + 63) // 64 * 64

        def sb(name, shape, dt):
            t = at(name, shape, dt, offset[0])
            offset[0] += size(shape, dt)
            assert offset[0] <= limit, (name, offset[0], limit)
            return t

        def region(base, items):
            out = []
            for name, shape, dt in items:
                out.append(at(name, shape, dt, base))
                base += size(shape, dt)
            assert base <= limit, (items[-1][0], base, limit)
            return out, base

        def sem(name):
            return ctx.enter_context(nc.semaphore(name))

        xs = [sb(f"xs{b}", [P, T, H], F32) for b in range(B)]
        XTh = sb("XTh", [P, HT, S], F32R)
        XTl = sb("XTl", [P, HT, S], F32R)
        ident = sb("ident", [P, P], F32)
        identb = sb("identb", [P, P], BF16)
        maskb = sb("maskb", [P, P], BF16)
        maskT = sb("maskT", [P, P], BF16)
        onesf = sb("onesf", [P, P], F32)
        row0 = sb("row0", [P, P], F32)
        smallc = sb("smallc", [P, 64], F32)
        mv = sb("mv", [P, T, 2], F32)
        stats = sb("stats", [P, T, 6], F32)
        std = sb("std", [P, T], F32)
        rstd = sb("rstd", [P, T], F32)
        eps = sb("eps", [P, 1], F32)
        shift = sb("shift", [P, 1], F32)
        cosb = sb("cosb", [P, T, HD], F32)
        sinb = sb("sinb", [P, T, HD], F32)
        bq1 = sb("bq1", [P, QKV1], F32)
        bo1 = sb("bo1", [P, H], F32)
        raw = [sb(f"raw{i}", [P, CHUNK], F32) for i in range(RING)]
        base = offset[0]

        (w0h, w0l, wo0h, wo0l, QTh, QTl, KTh, KTl, vT, Vh0, Vl0, P0, PTh, PTl, OTh, OTl, xT, mx0, nm0, sum0, rs0,
         xb0, bo0), a0_end = region(base, [
            ("w0h", [P, HT, 3 * D0], F32R), ("w0l", [P, HT, 3 * D0], F32R),
            ("wo0h", [P, H], F32R), ("wo0l", [P, H], F32R),
            ("QTh", [P, S], F32R), ("QTl", [P, S], F32R), ("KTh", [P, S], F32R), ("KTl", [P, S], F32R),
            ("vT", [P, S], F32), ("Vh0", [P, T, D0], F32R), ("Vl0", [P, T, D0], F32R),
            ("P0", [P, T, S], F32), ("PTh", [P, T, S], F32R), ("PTl", [P, T, S], F32R),
            ("OTh", [P, S], F32R), ("OTl", [P, S], F32R), ("xT", [P, HT, S], F32),
            ("mx0", [P, T], F32), ("nm0", [P, T], F32), ("sum0", [P, T], F32), ("rs0", [P, T], F32),
            ("xb0", [P, T, H], F32), ("bo0", [P, H], F32)])
        (nx, ss, rr), f_end = region(a0_end, [("nx", [P, T, H], F32), ("ss", [P, T], F32), ("rr", [P, T], F32)])
        fwh, f_end = region(f_end, [(f"fwh{i}", [P, 3 * H], F32R) for i in range(WSLOTS)])
        fwl, f_end = region(f_end, [(f"fwl{i}", [P, 3 * H], F32R) for i in range(WSLOTS)])
        sg, f_end = region(f_end, [(f"sg{i}", [P, S], F32) for i in range(2)])
        hh, f_end = region(f_end, [(f"hh{i}", [P, S], F32) for i in range(2)])
        hhi, f_end = region(f_end, [(f"hhi{i}", [P, S], F32R) for i in range(2)])
        hlo, f_end = region(f_end, [(f"hlo{i}", [P, S], F32R) for i in range(2)])
        PW = 5120
        (Ph0, Ph1, Pl0, Pl1), p_end = region(base, [
            ("Ph0", [P, PW], F16), ("Ph1", [P, PW], F16), ("Pl0", [P, PW], F16), ("Pl1", [P, PW], F16)])
        Ph, Pl = [Ph0, Ph1], [Pl0, Pl1]
        (w1h, w1l, qkv0, qkv1, rot0, rot1, t2), end = region(base, [
            ("w1h", [P, HT, QKV1], F32R), ("w1l", [P, HT, QKV1], F32R), ("qkv0", [P, QKV1], F32),
            ("qkv1", [P, QKV1], F32), ("rot0", [P, QK], F32), ("rot1", [P, QK], F32), ("t2", [P, QK], F32)])
        qkv, rot = [qkv0, qkv1], [rot0, rot1]
        assert end <= p_end
        Pf, pf_end = region(p_end, [(f"Pf{i}", [P, 1024], F32) for i in range(3)])
        (Qs0, Ks0, Ks1), end = region(p_end, [
            ("Qs0", [P, NH, HR], F32R), ("Ks0", [P, NKV, HR], F32R), ("Ks1", [P, NKV, HR], F32R)])
        assert end <= pf_end <= a0_end
        (Qop, Kop, Vs, Otok, mtok, mTh, mTl, osum, orec, vr, OTh1, OTl1), a_end = region(pf_end, [
            ("Qop", [P, PAIRS, S], F32R), ("Kop", [P, NKV, S], F32R), ("Vs", [P, T, NKV, VW], BF16),
            ("Otok", [P, T, H], F32), ("mtok", [P, 2, PAIRS, T], F32), ("mTh", [P, P], F32R),
            ("mTl", [P, P], F32R), ("osum", [P, 8, HD], F32), ("orec", [P, 8], F32), ("vr", [P, NKV * HD], F32),
            ("OTh1", [P, HT, S], F32R), ("OTl1", [P, HT, S], F32R)])
        Qs = [Qs0, at("Qs1", [P, NH, HR], F32R, pf_end + size([P, PAIRS, S], F32R) + size([P, NKV, S], F32R)
                      + size([P, T, NKV, VW], BF16))]
        (wo1h, wo1l), _ = region(pf_end, [("wo1h", [P, HT, H], F32R), ("wo1l", [P, HT, H], F32R)])
        mwh, m_end = region(base, [(f"mwh{i}", [P, 2 * H], F32R) for i in range(WSLOTS)])
        mwl, m_end = region(m_end, [(f"mwl{i}", [P, 2 * H], F32R) for i in range(WSLOTS)])
        (gwr, gwh, gwl, lgT, lg, asum, awt, asum2, rat, gb, wsum), m_end = region(m_end, [
            ("gwr", [P, HT, P], F32), ("gwh", [P, HT, P], F32R), ("gwl", [P, HT, P], F32R), ("lgT", [P, S], F32),
            ("lg", [P, T, E], F32), ("asum", [P, T], F32), ("awt", [P, 2, T], F32), ("asum2", [P, 2], F32),
            ("rat", [P, 2], F32), ("gb", [P, 2, E], F32), ("wsum", [P, 2, T], F32)])
        g, m_end = region(m_end, [(f"g{i}", [P, T, E], F32) for i in range(17)])
        assert m_end <= p_end
        ea, m_end = region(p_end, [(f"ea{i}", [P, S], F32) for i in range(2)])
        eah, m_end = region(m_end, [(f"eah{i}", [P, S], F32R) for i in range(2)])
        eal, m_end = region(m_end, [(f"eal{i}", [P, S], F32R) for i in range(2)])
        assert m_end <= pf_end
        (b2b, zacc), m_end = region(pf_end + PAIRS * S * 4, [("b2b", [P, E, H], F32), ("zacc", [P, T, H], F32)])
        assert m_end <= pf_end + (PAIRS + NKV) * S * 4

        ps = ctx.enter_context(nc.psum_tensor("ps", [P, 8, 512], F32))

        A0BANKS = ((4, 7, 0), (0, 3, 4))
        A1BANKS = ((0, 4), (4, 0))

        BQ, LNW, B1C = 0, 3, 8

        s_const_dma = sem("const_dma")
        s_const = sem("const_made")
        s_x_in = [sem(f"x_in{b}") for b in range(B)]
        s_raw = [sem(f"raw_landed{i}") for i in range(RING)]
        s_whi = sem("weights_hi")
        s_wlo = sem("weights_lo")
        s_yread = sem("y_read")
        s_tp = sem("transposed")
        s_tphi = sem("xT_hi")
        s_tplo = sem("xT_lo")
        s_y = sem("y_full")
        s_var = sem("ln_var")
        s_std = sem("ln_std")
        s_chain = sem("dve_step")
        s_achain = sem("act_step")
        s_pchain = sem("pool_step")
        s_lnout = sem("ln_out")
        s_a0qkv, s_a0act, s_a0lo = sem("a0_qkv_full"), sem("a0_qkv_hi"), sem("a0_qk_lo")
        s_a0vt, s_a0vhi, s_a0vlo = sem("a0_v_transposed"), sem("a0_v_hi"), sem("a0_v_lo")
        s_a0s, s_a0nm, s_a0p = sem("a0_scores"), sem("a0_negmax"), sem("a0_probs")
        s_a0pt, s_a0pthi, s_a0ptlo = sem("a0_pT"), sem("a0_pT_hi"), sem("a0_pT_lo")
        s_a0ot, s_a0othi, s_a0otlo = sem("a0_oT"), sem("a0_oT_hi"), sem("a0_oT_lo")
        s_fss, s_fnx = sem("f_rms"), sem("f_nx")
        s_fg, s_fu, s_fsg, s_fh = sem("f_gate_full"), sem("f_up_full"), sem("f_silu"), sem("f_h")
        s_fhi, s_flo, s_fdn = sem("f_h_hi"), sem("f_h_lo"), sem("f_down")
        s_init = sem("a1_operands_init")
        s_q, s_qe = sem("a1_qkv_full"), sem("a1_qkv_read")
        s_rot, s_qhi, s_qlo, s_v = sem("a1_rotated"), sem("a1_qk_hi"), sem("a1_qk_lo"), sem("a1_v_parts")
        s_tq, s_eq, s_ek = sem("a1_qk_transposed"), sem("a1_q_operand"), sem("a1_k_operand")
        s_s1, s_mx = sem("a1_scores_for_max"), sem("a1_max")
        s_mt, s_mth, s_mtl, s_md = sem("a1_maxT"), sem("a1_maxT_hi"), sem("a1_maxT_lo"), sem("a1_max_rows")
        s_s2, s_p, s_ph, s_pl = sem("a1_scores"), sem("a1_probs"), sem("a1_p_hi"), sem("a1_p_lo")
        s_o, s_oe = sem("a1_out"), sem("a1_out_read")
        s_cos, s_xb = sem("a1_x_cos"), sem("a1_residual_bias")
        s_gw, s_lgT, s_lgTe, s_lg, s_as, s_rt, s_rk, s_rkb, s_w = (
            sem("m_gate_w"), sem("m_logitsT"), sem("m_logitsT_read"), sem("m_logits"), sem("m_abs"), sem("m_ratio"),
            sem("m_rank"), sem("m_rank_bc"), sem("m_weights"))
        s_pre, s_ea, s_eh, s_el, s_e2, s_acc = (sem("m_pre"), sem("m_act"), sem("m_act_hi"), sem("m_act_lo"),
                                                sem("m_expert_out"), sem("m_acc"))
        s_gwd = sem("m_const_dma")
        s_a1d = sem("a1_const_dma")
        s_out = sem("out_written")

        N_CONST_DMA = 2

        def f32(ap):
            return ap.bitcast(F32)

        def rope(ap):
            return ap.rearrange("p (h i c) -> p h i c", h=NH + NKV, c=2)

        def table(t, k):
            return t[:, k, None, :].to_broadcast([P, NH + NKV, HD]).rearrange("p h (i c) -> p h i c", c=2)

        TP = {("A0", 0): 0, ("A0", 1): 1, ("F0", 0): 2, ("F0", 1): 3, ("A1", 0): 4, ("O1", 0): 5, ("A1", 1): 6,
              ("O1", 1): 7, ("M", 0): 8, ("M", 1): 9}
        TPP = {("F0", 0): 0, ("F0", 1): 1, ("A1", 0): 2, ("O1", 0): 3, ("A1", 1): 4, ("O1", 1): 5, ("M", 0): 6,
               ("M", 1): 7}
        LN = {("A0", 0): 0, ("A0", 1): 1, ("F0", 0): 2, ("F0", 1): 3, ("A1", 0): 4, ("A1", 1): 5, ("M", 0): 6,
              ("M", 1): 7}
        Y = {("A0", 0): 0, ("A0", 1): 1, ("A1", 0): 2, ("A1", 1): 3}
        TPB = {("F0", 0): 4, ("F0", 1): 4, ("A1", 0): 4, ("O1", 0): 0, ("A1", 1): 4, ("O1", 1): 0, ("M", 0): 4,
               ("M", 1): 4}

        block = ctx.enter_context(nc.Block())

        @block.sync
        def _(sp):
            sp.dma_start(smallc[:], dram["smallc"]).then_inc(s_const_dma, 16)

            def load(n):
                name, i, cols = chunks[n]
                if n >= RING:
                    sp.wait_ge(s_wlo, n - RING + 1)
                src = dram[name] if i is None else dram[name][i]
                sp.dma_start(raw[n % RING][:, 0:cols], src).then_inc(s_raw[n % RING], 16)

            load(0)
            for b in range(B):
                if b:
                    sp.wait_ge(s_tplo, HT * b)
                sp.dma_start(xT[:], dram["xT"][b]).then_inc(s_x_in[b], 16)
                sp.dma_start(xs[b][:], dram["x"][b]).then_inc(s_x_in[b], 16)
                if b == 0:
                    sp.dma_start(bo0[:], dram["bo0"].partition_broadcast(P)).then_inc(s_const_dma, 16)
                    for dst, name, bc in ((cosb, "cosb", False), (sinb, "sinb", False), (bq1, "bq1", True),
                                          (bo1, "bo1", True)):
                        src = dram[name].partition_broadcast(P) if bc else dram[name]
                        sp.dma_start(dst[:], src).then_inc(s_a1d, 16)
                    load(1)
                    load(2)
                    load(3)
            n = 4
            while chunks[n][0] == "w_ffn":
                load(n)
                n += 1
            for b in range(B):
                for _ in range(2):
                    load(n)
                    n += 1
                load(n)
                load(n + 1)
                n += 2
                sp.wait_ge(s_mth, b + 1)
                sp.wait_ge(s_mtl, b + 1)
                for k, mt in enumerate((mTh, mTl)):
                    for s in range(2):
                        row = HR * s + 3 * HD + k
                        dst = f32(Qop[row:row + 1, :, :]).rearrange("o p (t q) -> o (p t) q", q=P)
                        sp.dma_start(dst, f32(mt[HR * s:HR * (s + 1), :])).then_inc(s_md, 16)
            sp.wait_ge(s_o, 2 * NKV * B)
            for dst, name, bc in ((gwr, "gwr", False), (awt, "awt", False)):
                sp.dma_start(dst[:], dram[name]).then_inc(s_gwd, 16)
            sp.dma_start(b2b[:], dram["b2"].partition_broadcast(P)).then_inc(s_gwd, 16)
            sp.dma_start(gb[:], dram["gb"].partition_broadcast(P)).then_inc(s_gwd, 16)
            while n < len(chunks):
                load(n)
                n += 1
            for b in range(B):
                sp.wait_ge(s_lnout, 4 * (LN["M", b] + 1))
                sp.dma_start(dram["out"][b], xs[b][:]).then_inc(s_out, 16)
            sp.wait_ge(s_out, 16 * B)

        @block.gpsimd
        def _(pool):
            nc.gpsimd.memset(eps[:], LN_EPS)
            nc.gpsimd.memset(shift[:], SHIFT1)
            nc.gpsimd.memset(onesf[:], 1.0).then_inc(s_const, 1)
            nc.gpsimd.memset(ident[:], 0.0).then_inc(s_pchain, 1)
            nc.gpsimd.memset(row0[:], 0.0).then_inc(s_pchain, 1)
            nc.gpsimd.memset(maskb[:], 0.0).then_inc(s_pchain, 1)
            nc.gpsimd.memset(maskT[:], 0.0).then_inc(s_pchain, 1)
            pool.wait_ge(s_pchain, 2)
            nc.gpsimd.affine_select(out=ident[:], in_=ident[:], compare_op=ALU.not_equal, fill=1.0, base=0,
                                    pattern=[[-1, P]], channel_multiplier=1).then_inc(s_const, 1)
            nc.gpsimd.affine_select(out=row0[:], in_=row0[:], compare_op=ALU.not_equal, fill=1.0, base=0,
                                    pattern=[[0, P]], channel_multiplier=1).then_inc(s_const, 1)

            pool.wait_ge(s_pchain, 3)
            nc.gpsimd.affine_select(out=maskb[:], in_=maskb[:], compare_op=ALU.is_ge, fill=MASKED, base=0,
                                    pattern=[[-1, P]], channel_multiplier=1).then_inc(s_const, 1)
            pool.wait_ge(s_pchain, 4)
            nc.gpsimd.affine_select(out=maskT[:], in_=maskT[:], compare_op=ALU.is_ge, fill=MASKED, base=0,
                                    pattern=[[1, P]], channel_multiplier=-1).then_inc(s_const, 1)
            for b in range(B):
                if b == 0:
                    pool.wait_ge(s_fdn, NI * B)
                    nc.gpsimd.memset(f32(Kop[:]), 0.0)
                    nc.gpsimd.memset(Vs[:, :, :, VW - 1:VW], 1.0).then_inc(s_init, 1)
                if b:
                    pool.wait_ge(s_o, 2 * NKV * b)
                    pool.wait_ge(s_pl, 6 * NKV * b)
                    pool.wait_ge(s_tp, 4 * (TPP["O1", b - 1] + 1))
                for q in Qs:
                    nc.gpsimd.memset(f32(q[:, :, 3 * HD:HR]), 0.0)
                for k in (Ks0, Ks1):
                    nc.gpsimd.memset(f32(k[:, :, 3 * HD + 2:HR]), 0.0)
                    last = nc.gpsimd.memset(f32(k[:, :, 3 * HD:3 * HD + 2]), -1.0)
                last.then_inc(s_init, 1)
                for t in range(T):
                    bt = b * T + t
                    pool.wait_ge(s_qe, bt + 1)
                    if t >= 2:
                        pool.wait_ge(s_qhi, bt - 1)
                        pool.wait_ge(s_qlo, bt - 1)
                    x = qkv[t % 2]
                    nc.gpsimd.tensor_tensor(rope(rot[t % 2][:]), rope(x[:, 0:QK]), table(cosb, t),
                                            ALU.mult).then_inc(s_cos, 1)
                    v = x[:, QK:].rearrange("p (g d) -> p g d", d=HD)
                    r3 = vr[:].rearrange("p (g d) -> p g d", d=HD)
                    part = lambda k: Vs[:, t, :, k * HD:(k + 1) * HD]
                    for k, (op, src) in enumerate(((None, v), ((v, 0), r3), (None, r3), ((r3, 1), part(2)))):
                        if k:
                            pool.wait_ge(s_v, 4 * bt + k)
                        if op is None:
                            nc.gpsimd.tensor_copy(part(k // 2), src).then_inc(s_v, 1)
                        else:
                            nc.gpsimd.tensor_tensor(src, op[0], part(op[1]), ALU.subtract).then_inc(s_v, 1)
                pool.wait_ge(s_tplo, 4 * (TP["A1", b] + 1))
                pool.wait_ge(s_a1d, 64)
                nc.gpsimd.tensor_tensor(xs[b][:], xs[b][:], bo1[:, None, :].to_broadcast([P, T, H]),
                                        ALU.add).then_inc(s_xb, 1)
                for gg in range(NKV):
                    for u in range(6):
                        n_u = (b * NKV + gg) * 6 + u
                        cols = UW[u]
                        slot = Pf[n_u % 3]
                        pool.wait_ge(s_p, n_u + 1)
                        gi = b * NKV + gg
                        if gi >= 2:
                            pool.wait_ge(s_o, 2 * (gi - 1))
                        nc.gpsimd.affine_select(out=Ph[gg % 2][:, UO[u]:UO[u] + cols], in_=slot[:, 0:cols],
                                                compare_op=ALU.is_equal, fill=0.0, base=0, pattern=[[0, cols]],
                                                channel_multiplier=0).then_inc(s_ph, 1)

        @block.scalar
        def _(act):
            def evac(out, in_, sm, func=ACT.Identity, **kw):
                return nc.scalar.activation(out, in_, func, **kw).then_inc(sm, 1)

            def tp_hi(key, scale=None):
                for h in range(HT):
                    act.wait_ge(s_tp, 4 * TPP[key] + h + 1)
                    kw = {} if scale is None else {"scale": scale[:, h:h + 1]}
                    dst = OTh1 if key[0] == "O1" else XTh
                    evac(dst[:, h, :], ps[:, TPB[key] + h, :], s_tphi, **kw)

            def ln_std(key):
                act.wait_ge(s_var, LN[key] + 1)
                nc.scalar.activation(std[:], mv[:, :, 1], ACT.Sqrt, bias=eps[:]).then_inc(s_std, 1)

            def split_hi(n, out):
                cols = chunks[n][2]
                act.wait_ge(s_raw[n % RING], 16 * (n // RING + 1))
                evac(out, raw[n % RING][:, 0:cols], s_whi)

            flat = lambda t: t.rearrange("p a n -> p (a n)")
            split_hi(0, flat(w0h[:]))
            act.wait_ge(s_const, 5)
            act.wait_ge(s_const_dma, 16 * N_CONST_DMA)

            def rms(b):
                act.wait_ge(s_lnout, 4 * (LN["A0", b] + 1))
                if b:
                    act.wait_ge(s_tp, 4 * b)
                for t in range(T):
                    last = nc.scalar.activation(nx[:, t, :], xs[b][:, t, :], ACT.Square, accum_out=ss[:, t:t + 1])
                last.then_inc(s_achain, 1)
                act.wait_ge(s_achain, b + 1)
                nc.scalar.activation(rr[:], ss[:], ACT.Sqrt, bias=eps[:], scale=1.0 / H).then_inc(s_fss, 1)

            def x_hi(b):
                act.wait_ge(s_x_in[b], 32)
                if b:
                    act.wait_ge(s_a0qkv, 3 * b)
                for h in range(HT):
                    evac(XTh[:, h, :], xT[:, h, :], s_tphi)

            x_hi(0)
            split_hi(1, wo0h[:])
            for b in range(B):
                q0, v0, o0 = A0BANKS[b]
                for k, out in enumerate((QTh, KTh, vT)):
                    act.wait_ge(s_a0qkv, 3 * b + k + 1)
                    evac(out[:], ps[:, q0 + k, :], s_a0act, bias=smallc[:, BQ + k:BQ + k + 1])
                if b:
                    rms(0)
                act.wait_ge(s_a0vt, b + 1)
                evac(Vh0[:].rearrange("p t d -> p (t d)"), ps[:, v0, :], s_a0vhi)
                for q in range(T):
                    act.wait_ge(s_a0nm, T * b + q + 1)
                    nc.scalar.activation(P0[:, q, :], ps[:, o0 + q, :], ACT.Exp, bias=nm0[:, q:q + 1], scale=SCALE0,
                                         accum_out=sum0[:, q:q + 1]).then_inc(s_a0p, 1)
                for k in range(T):
                    act.wait_ge(s_a0pt, T * b + k + 1)
                    evac(PTh[:, k, :], ps[:, q0 + k, :], s_a0pthi)
                if b + 1 < B:
                    x_hi(b + 1)
                act.wait_ge(s_a0ot, b + 1)
                evac(OTh[:], ps[:, o0, :], s_a0othi)
                if b == 0:
                    ln_std(("A0", 0))
                else:
                    split_hi(2, fwh[0][:])
            n = 2
            for b in range(B):
                tp_hi(("F0", b), smallc[:, LNW:LNW + HT])
                if b == 0:
                    ln_std(("A0", 1))
                for i in range(NI):
                    gi = b * NI + i
                    n += 1
                    if gi + 1 < B * NI:
                        if gi + 1 >= WSLOTS:
                            act.wait_ge(s_fdn, gi - WSLOTS + 2)
                        split_hi(n, fwh[(gi + 1) % WSLOTS][:])
                    act.wait_ge(s_fg, gi + 1)
                    if gi >= 2:
                        act.wait_ge(s_fh, gi - 1)
                    nc.scalar.activation(sg[gi % 2][:], ps[:, 4 + gi % 2, :], ACT.Silu).then_inc(s_fsg, 1)
                    act.wait_ge(s_fh, gi + 1)
                    if gi >= 2:
                        act.wait_ge(s_fdn, gi - 1)
                    evac(hhi[gi % 2][:], hh[gi % 2][:], s_fhi)
                    if b == 0 and i == 4:
                        rms(1)
                    if b == 1 and i == 3:
                        ln_std(("F0", 0))
                    if b == 1 and i == NI - 2:
                        for k in range(2):
                            split_hi(2 + NI * B + k, flat(w1h[:, 2 * k:2 * k + 2, :]))
            for b in range(B):
                n += 2
                tp_hi(("A1", b))
                act.wait_ge(s_init, b + 2)

                def q_operands(t):
                    for k in range(4):
                        u = 5 * (b * T + t) + k
                        act.wait_ge(s_tq, u + 1)
                        evac(Qop[:, 4 * k:4 * k + 4, t * P:(t + 1) * P],
                             ps[:, ob + u % 4, :].rearrange("p (a q) -> p a q", a=4), s_eq)

                ob = A1BANKS[b][1]
                for t in range(T):
                    bt = b * T + t
                    if t:
                        q_operands(t - 1)
                    act.wait_ge(s_rot, bt + 1)
                    r = rot[t % 2][:, 0:NH * HD].rearrange("p (h d) -> p h d", d=HD)
                    o = Qs[t % 2][:].rearrange("p h (k d) -> p h k d", d=HD)
                    for k in (0, 2):
                        nc.scalar.activation(o[:, :, k, :], r, ACT.Identity)
                    r = rot[t % 2][:, NH * HD:].rearrange("p (h d) -> p h d", d=HD)
                    o = (Ks0, Ks1)[t % 2][:].rearrange("p h (k d) -> p h k d", d=HD)
                    nc.scalar.activation(o[:, :, 0, :], r, ACT.Identity)
                    nc.scalar.activation(o[:, :, 1, :], r, ACT.Identity).then_inc(s_qhi, 1)
                    if t == 1:
                        ln_std(("F0", 1) if b == 0 else ("A1", 0))
                q_operands(T - 1)
                act.wait_ge(s_mt, b + 1)
                evac(mTh[:], ps[:, 4, 0:P], s_mth)
                for gg in range(NKV):
                    for u in range(6):
                        n_u = (b * NKV + gg) * 6 + u
                        act.wait_ge(s_s2, n_u + 1)
                        if n_u >= 3:
                            act.wait_ge(s_pl, n_u - 2)
                        banks = 1 if u == 5 else 2
                        r0 = 2 * (n_u % 3)
                        src = ps[:, r0:r0 + banks, 0:UW[u] // banks]
                        nc.scalar.activation(Pf[n_u % 3][:, 0:UW[u]].rearrange("p (a n) -> p a n", a=banks), src,
                                             ACT.Exp, bias=shift[:], scale=SCALE1).then_inc(s_p, 1)
                for k in range(2):
                    split_hi(n, flat(wo1h[:, 2 * k:2 * k + 2, :]))
                    n += 1
                act.wait_ge(s_o, 2 * NKV * (b + 1))
                tp_hi(("O1", b))
                if b == 0:
                    for k in range(2):
                        split_hi(n + k, flat(w1h[:, 2 * k:2 * k + 2, :]))
            for b in range(B):
                if b == 0:
                    act.wait_ge(s_gwd, 64)
                    evac(gwh[:], gwr[:], s_gw)
                if b == 0:
                    split_hi(n, mwh[0][:])
                tp_hi(("M", b))
                for i in range(E * FE):
                    gi = b * E * FE + i
                    n += 1
                    if gi + 1 < B * E * FE:
                        if gi + 1 >= WSLOTS:
                            act.wait_ge(s_e2, gi - WSLOTS + 2)
                        split_hi(n, mwh[(gi + 1) % WSLOTS][:])
                    act.wait_ge(s_pre, gi + 1)
                    if gi >= 2:
                        act.wait_ge(s_el, gi - 1)
                    func = (ACT.Tanh, ACT.Gelu, ACT.Silu)[i // FE]
                    nc.scalar.activation(ea[gi % 2][:], ps[:, 4 + gi % 2, :], func,
                                         bias=smallc[:, B1C + i:B1C + i + 1]).then_inc(s_ea, 1)
                    act.wait_ge(s_ea, gi + 1)
                    if gi >= 2:
                        act.wait_ge(s_e2, gi - 1)
                    evac(eah[gi % 2][:], ea[gi % 2][:], s_eh)
                    if i == 0:
                        act.wait_ge(s_lgT, b + 1)
                        evac(lgT[:], ps[:, 6, :], s_lgTe)
                    if i == 1:
                        ln_std(("A1", 1) if b == 0 else ("M", 0))
                    if i == 2:
                        act.wait_ge(s_rk, 2 * b + 1)
                        nc.scalar.activation(g[1][:], g[0][:], ACT.Exp).then_inc(s_rt, 1)
            ln_std(("M", 1))

        @block.vector
        def _(dve):
            steps = [0]

            def step(ins):
                steps[0] += 1
                ins.then_inc(s_chain, 1)
                dve.wait_ge(s_chain, steps[0])

            def sub(out, a, hi, sm):
                return nc.vector.tensor_tensor(out, a, f32(hi), ALU.subtract).then_inc(sm, 1)

            def split_lo(n, out, hi):
                cols = chunks[n][2]
                dve.wait_ge(s_whi, n + 1)
                sub(out, raw[n % RING][:, 0:cols], hi, s_wlo)

            def tp_lo(key, scale=None):
                n = TP[key]
                for h in range(HT):
                    dve.wait_ge(s_tphi, 4 * n + h + 1)
                    bank = TPB[key] + h
                    if scale is None:
                        hi, lo = (OTh1, OTl1) if key[0] == "O1" else (XTh, XTl)
                        sub(lo[:, h, :], ps[:, bank, :], hi[:, h, :], s_tplo)
                    else:
                        nc.vector.scalar_tensor_tensor(XTl[:, h, :], ps[:, bank, :], scale[:, h:h + 1],
                                                       f32(XTh[:, h, :]), ALU.mult, ALU.subtract).then_inc(s_tplo, 1)

            def ln_stats(key, z):
                for t in range(T):
                    last = nc.vector.bn_stats(stats[:, t, :], z[:, t, :])
                step(last)
                for t in range(T):
                    last = nc.vector.bn_aggr(mv[:, t, :], stats[:, t, :])
                last.then_inc(s_var, 1)

            def ln_apply(key, z, out):
                dve.wait_ge(s_var, LN[key] + 1)
                dve.wait_ge(s_std, LN[key] + 1)
                step(nc.vector.reciprocal(rstd[:], std[:]))
                for t in range(T):
                    nc.vector.tensor_scalar(out[:, t, :], z[:, t, :], mv[:, t, 0:1], rstd[:, t:t + 1], ALU.subtract,
                                            ALU.mult).then_inc(s_lnout, 1)
                dve.wait_ge(s_lnout, 4 * (LN[key] + 1))

            def add_y(key, bank, x, ready=None):
                for t in range(T):
                    if ready is not None:
                        dve.wait_ge(s_y, ready + t + 1)
                    last = nc.vector.tensor_tensor(x[:, t, :], ps[:, bank + t, :], x[:, t, :], ALU.add)
                last.then_inc(s_yread, 1)
                dve.wait_ge(s_yread, LN[key] + 1)

            def normed_rms(b):
                dve.wait_ge(s_fss, b + 1)
                step(nc.vector.reciprocal(ss[:], rr[:]))
                for t in range(T):
                    nc.vector.tensor_scalar(nx[:, t, :], xs[b][:, t, :], ss[:, t:t + 1], None,
                                            ALU.mult).then_inc(s_fnx, 1)

            flat = lambda t: t[:].rearrange("p a n -> p (a n)")
            split_lo(0, flat(w0l), flat(w0h))
            dve.wait_ge(s_const, 5)
            nc.vector.tensor_copy(identb[:], ident[:]).then_inc(s_const, 1)

            def x_lo(b):
                dve.wait_ge(s_x_in[b], 32)
                for h in range(HT):
                    dve.wait_ge(s_tphi, 4 * b + h + 1)
                    sub(XTl[:, h, :], xT[:, h, :], XTh[:, h, :], s_tplo)

            x_lo(0)
            split_lo(1, wo0l[:], wo0h[:])
            dve.wait_ge(s_const_dma, 16 * N_CONST_DMA)
            for b in range(B):
                q0, v0, o0 = A0BANKS[b]
                step(nc.vector.tensor_tensor(xb0[:], xs[b][:], bo0[:, None, :].to_broadcast([P, T, H]), ALU.add))
                for k, (lo, hi) in enumerate(((QTl, QTh), (KTl, KTh))):
                    dve.wait_ge(s_a0act, 3 * b + k + 1)
                    nc.vector.scalar_tensor_tensor(lo[:], ps[:, q0 + k, :], smallc[:, BQ + k:BQ + k + 1], f32(hi[:]),
                                                   ALU.add, ALU.subtract).then_inc(s_a0lo, 1)
                dve.wait_ge(s_a0vhi, b + 1)
                sub(flat(Vl0), ps[:, v0, :], flat(Vh0), s_a0vlo)
                for q in range(T):
                    dve.wait_ge(s_a0s, T * b + q + 1)
                    step(nc.vector.reduce_max(mx0[:, q:q + 1], ps[:, o0 + q, :], AX.X))
                    nc.vector.tensor_scalar(nm0[:, q:q + 1], mx0[:, q:q + 1], -SCALE0, None,
                                            ALU.mult).then_inc(s_a0nm, 1)
                if b:
                    normed_rms(0)
                for k in range(T):
                    dve.wait_ge(s_a0pthi, T * b + k + 1)
                    sub(PTl[:, k, :], ps[:, q0 + k, :], PTh[:, k, :], s_a0ptlo)
                if b + 1 < B:
                    x_lo(b + 1)
                dve.wait_ge(s_a0othi, b + 1)
                sub(OTl[:], ps[:, o0, :], OTh[:], s_a0otlo)
                if b:
                    split_lo(2, fwl[0][:], fwh[0][:])
                    tp_lo(("F0", 0), smallc[:, LNW:LNW + HT])
                dve.wait_ge(s_a0p, T * (b + 1))
                step(nc.vector.reciprocal(rs0[:], sum0[:]))
                for t in range(T):
                    dve.wait_ge(s_y, 4 * Y["A0", b] + t + 1)
                    last = nc.vector.scalar_tensor_tensor(xs[b][:, t, :], ps[:, q0 + t, :], rs0[:, t:t + 1],
                                                          xb0[:, t, :], ALU.mult, ALU.add)
                last.then_inc(s_yread, 1)
                dve.wait_ge(s_yread, b + 1)
                ln_stats(("A0", b), xs[b])
                if b == 0:
                    ln_apply(("A0", 0), xs[0], xs[0])
            n = 2
            for b in range(B):
                if b:
                    tp_lo(("F0", b), smallc[:, LNW:LNW + HT])
                for i in range(NI):
                    gi = b * NI + i
                    if gi + 1 < B * NI:
                        split_lo(n + 1, fwl[(gi + 1) % WSLOTS][:], fwh[(gi + 1) % WSLOTS][:])
                    n += 1
                    dve.wait_ge(s_fsg, gi + 1)
                    dve.wait_ge(s_fu, gi + 1)
                    nc.vector.tensor_tensor(hh[gi % 2][:], sg[gi % 2][:], ps[:, 6 + gi % 2, :],
                                            ALU.mult).then_inc(s_fh, 1)
                    dve.wait_ge(s_fhi, gi + 1)
                    sub(hlo[gi % 2][:], hh[gi % 2][:], hhi[gi % 2][:], s_flo)
                    if b == 0 and i == 1:
                        ln_apply(("A0", 1), xs[1], xs[1])
                    if b == 0 and i == 5:
                        normed_rms(1)
                    if b == 1 and i == 0:
                        add_y(("F0", 0), 0, xs[0])
                    if b == 1 and i == 1:
                        ln_stats(("F0", 0), xs[0])
                    if b == 1 and i == 4:
                        ln_apply(("F0", 0), xs[0], xs[0])
                    if b == 1 and i == NI - 2:
                        for k in range(2):
                            split_lo(2 + NI * B + k, flat(w1l[:, 2 * k:2 * k + 2, :]),
                                     flat(w1h[:, 2 * k:2 * k + 2, :]))
            for b in range(B):
                n += 2
                tp_lo(("A1", b))
                last_key = ("F0", 1) if b == 0 else ("A1", 0)
                last_x = xs[1] if b == 0 else xs[0]
                if b == 0:
                    dve.wait_ge(s_fdn, NI * B)
                    add_y(last_key, 0, last_x)
                dve.wait_ge(s_a1d, 64)
                dve.wait_ge(s_init, b + 2)
                pb, ob = A1BANKS[b]

                def k_operands(t):
                    u = 5 * (b * T + t) + 4
                    dve.wait_ge(s_tq, u + 1)
                    src = ps[:, ob + u % 4, :].rearrange("p (a q) -> p a q", a=4)
                    for s in range(2):
                        last = nc.vector.tensor_copy(Kop[HR * s:HR * s + HR, s::2, t * P:(t + 1) * P],
                                                     src[HR * s:HR * s + HR])
                    last.then_inc(s_ek, 1)

                for t in range(T):
                    bt = b * T + t
                    dve.wait_ge(s_q, bt + 1)
                    if t >= 2:
                        dve.wait_ge(s_v, 4 * (bt - 1))
                    x, r = qkv[t % 2], rot[t % 2]
                    nc.vector.tensor_tensor(x[:], ps[:, pb + 2 * (t % 2):pb + 2 * (t % 2) + 2, :].rearrange(
                        "p a n -> p (a n)")[:, 0:QKV1], bq1[:], ALU.add).then_inc(s_qe, 1)
                    dve.wait_ge(s_qe, bt + 1)
                    step(nc.vector.tensor_tensor(rope(t2[:]), rope(x[:, 0:QK])[:, :, :, ::-1], table(sinb, t),
                                                 ALU.mult))
                    if t:
                        k_operands(t - 1)
                    dve.wait_ge(s_cos, bt + 1)
                    nc.vector.tensor_tensor(r[:], r[:], t2[:], ALU.add).then_inc(s_rot, 1)
                    dve.wait_ge(s_qhi, bt + 1)
                    dve.wait_ge(s_rot, bt + 1)
                    rq = r[:, 0:NH * HD].rearrange("p (h d) -> p h d", d=HD)
                    o = Qs[t % 2][:].rearrange("p h (k d) -> p h k d", d=HD)
                    nc.vector.tensor_tensor(o[:, :, 1, :], rq, f32(o[:, :, 0, :]), ALU.subtract)
                    rk = r[:, NH * HD:].rearrange("p (h d) -> p h d", d=HD)
                    o = (Ks0, Ks1)[t % 2][:].rearrange("p h (k d) -> p h k d", d=HD)
                    nc.vector.tensor_tensor(o[:, :, 2, :], rk, f32(o[:, :, 0, :]), ALU.subtract).then_inc(s_qlo, 1)
                    if t == 0:
                        if b:
                            dve.wait_ge(s_xb, b)
                            add_y(last_key, 0, last_x, 4 * Y["A1", b - 1])
                        ln_stats(last_key, last_x)
                    if t == 2:
                        ln_apply(last_key, last_x, last_x)
                k_operands(T - 1)
                for p in range(PAIRS):
                    for u in range(3):
                        n_u = (b * PAIRS + p) * 3 + u
                        r0 = 2 * (n_u % 2)
                        dve.wait_ge(s_s1, n_u + 1)
                        if u < 2:
                            q = 3 - u
                            last = nc.vector.reduce_max(mtok[:, :, p, q],
                                                        ps[:, r0:r0 + 2, 0:(q + 1) * P], AX.X)
                        else:
                            for q in range(2):
                                w = (q + 1) * P
                                last = nc.vector.reduce_max(
                                    mtok[:, :, p, q],
                                    ps[:, r0 + q, 0:2 * w].rearrange("p (s k) -> p s k", s=2), AX.X)
                        last.then_inc(s_mx, 1)
                dve.wait_ge(s_mth, b + 1)
                sub(mTl[:], ps[:, 4, 0:P], mTh[:], s_mtl)

                def read_out(gg):
                    for k in range(2):
                        n_o = 2 * (b * NKV + gg) + k
                        dve.wait_ge(s_o, n_o + 1)
                        src = ps[:, 6 + k, 0:8 * VW].rearrange("p (h c) -> p h c", c=VW)
                        nc.vector.reciprocal(orec[:], src[:, :, VW - 1])
                        step(nc.vector.tensor_reduce(osum[:], src[:, :, 0:3 * HD].rearrange(
                            "p h (k d) -> p h d k", k=3), AX.X, ALU.add))
                        G, s = gg // 2, gg % 2
                        dst = Otok[:, 2 * k:2 * k + 2, :].rearrange("p t (g j s d) -> p t g j s d", g=4, j=4, s=2)
                        nc.vector.tensor_tensor(
                            dst[:, :, G, :, s, :], osum[:].rearrange("p (t j) d -> p t j d", t=2),
                            orec[:].rearrange("p (t j) -> p t j", t=2)[:, :, :, None].to_broadcast([P, 2, 4, HD]),
                            ALU.mult).then_inc(s_oe, 1)
                        dve.wait_ge(s_oe, n_o + 1)

                for gg in range(NKV):
                    for u in range(6):
                        n_u = (b * NKV + gg) * 6 + u
                        dve.wait_ge(s_ph, n_u + 1)
                        sl = slice(UO[u], UO[u] + UW[u])
                        nc.vector.tensor_tensor(Pl[gg % 2][:, sl], Pf[n_u % 3][:, 0:UW[u]], Ph[gg % 2][:, sl],
                                                ALU.subtract).then_inc(s_pl, 1)
                    if gg:
                        read_out(gg - 1)
                read_out(NKV - 1)
                for k in range(2):
                    split_lo(n, flat(wo1l[:, 2 * k:2 * k + 2, :]), flat(wo1h[:, 2 * k:2 * k + 2, :]))
                    n += 1
                tp_lo(("O1", b))
                if b == 0:
                    for k in range(2):
                        split_lo(n + k, flat(w1l[:, 2 * k:2 * k + 2, :]), flat(w1h[:, 2 * k:2 * k + 2, :]))
            for b in range(B):
                x = xs[b]
                dve.wait_ge(s_gwd, 64)
                if b == 0:
                    dve.wait_ge(s_gw, 1)
                    sub(flat(gwl), flat(gwr), flat(gwh), s_gw)
                    split_lo(n, mwl[0][:], mwh[0][:])
                tp_lo(("M", b))
                if b == 0:
                    dve.wait_ge(s_xb, B)
                    add_y(("A1", 1), 0, xs[1], 4 * Y["A1", 1])
                    ln_stats(("A1", 1), xs[1])

                col = lambda t, k: t[:, :, k:k + 1]
                bc = lambda a: a.to_broadcast([P, T, E])
                tt = nc.vector.tensor_tensor
                w = g[16]

                def strengths():
                    step(nc.vector.tensor_reduce(asum[:], x[:], AX.X, ALU.add, apply_absolute_value=True))
                    nc.vector.tensor_tensor(wsum[:, 0, :], asum[:], awt[:, 0, :], ALU.mult)
                    step(nc.vector.tensor_tensor(wsum[:, 1, :], asum[:], awt[:, 1, :], ALU.mult))
                    for k in range(2):
                        last = nc.vector.reduce_sum(asum2[:, k:k + 1], wsum[:, k, :], AX.X)
                    last.then_inc(s_as, 1)

                def router_logits():
                    dve.wait_ge(s_rkb, 3 * b + 1)
                    step(nc.vector.tensor_scalar(rat[:, 1:2], ps[:, 6, 1:2], 1e-8, None, ALU.add))
                    step(nc.vector.reciprocal(rat[:, 1:2], rat[:, 1:2]))
                    step(nc.vector.tensor_tensor(rat[:, 0:1], ps[:, 6, 0:1], rat[:, 1:2], ALU.mult))
                    step(nc.vector.scalar_tensor_tensor(lg[:, 0, :], gb[:, 0, :], rat[:, 0:1], gb[:, 1, :], ALU.mult,
                                                        ALU.add))
                    dve.wait_ge(s_lg, b + 1)
                    logits = ps[:, 7, :].rearrange("p (t e) -> p t e", t=T)[:, :, 0:E]
                    step(nc.vector.tensor_tensor(g[2][:], logits, lg[:, 0:1, :].to_broadcast([P, T, E]), ALU.add))
                    step(nc.vector.reduce_max(g[3][:, :, 0:1], g[2][:], AX.X))
                    tt(g[0][:], g[2][:], bc(col(g[3], 0)), ALU.subtract).then_inc(s_rk, 1)

                def top_two():
                    dve.wait_ge(s_rt, b + 1)
                    step(nc.vector.reduce_sum(g[3][:, :, 1:2], g[1][:], AX.X))
                    step(nc.vector.reciprocal(g[3][:, :, 2:3], g[3][:, :, 1:2]))
                    step(tt(g[4][:], g[1][:], bc(col(g[3], 2)), ALU.mult))
                    a, c, d = (col(g[4], k) for k in range(3))
                    tt(col(g[7], 0), a, c, ALU.is_lt)
                    tt(col(g[7], 1), a, d, ALU.is_lt)
                    step(tt(col(g[7], 2), c, d, ALU.is_lt))
                    step(nc.vector.tensor_scalar(g[8][:], g[7][:], -1.0, 1.0, ALU.mult, ALU.add))
                    tt(col(g[9], 0), col(g[7], 0), col(g[7], 1), ALU.add)
                    tt(col(g[9], 1), col(g[8], 0), col(g[7], 2), ALU.add)
                    tt(col(g[9], 2), col(g[8], 1), col(g[8], 2), ALU.add).then_inc(s_rk, 1)
                    tt(col(g[6], 0), a, c, ALU.max)
                    step(tt(col(g[6], 1), a, c, ALU.min))
                    step(tt(col(g[6], 2), col(g[6], 0), d, ALU.min))
                    tt(col(g[5], 0), col(g[6], 0), d, ALU.max)
                    step(tt(col(g[5], 1), col(g[6], 1), col(g[6], 2), ALU.max))
                    step(tt(col(g[10], 0), col(g[5], 0), col(g[5], 1), ALU.add))
                    step(nc.vector.tensor_scalar(col(g[10], 1), col(g[10], 0), 1e-8, None, ALU.add))
                    step(nc.vector.reciprocal(col(g[10], 2), col(g[10], 1)))
                    step(tt(g[11][:, :, 0:2], g[5][:, :, 0:2], col(g[10], 2).to_broadcast([P, T, 2]), ALU.mult))

                def expert_weights():
                    dve.wait_ge(s_rkb, 3 * b + 3)
                    rank = ps[:, 6, 8:8 + E]
                    nc.vector.tensor_scalar(g[12][:, 0, :], rank, 0.0, None, ALU.is_equal)
                    step(nc.vector.tensor_scalar(g[13][:, 0, :], rank, 1.0, None, ALU.is_equal))
                    tt(g[14][:], g[12][:, 0:1, :].to_broadcast([P, T, E]), bc(col(g[11], 0)), ALU.mult)
                    step(tt(g[15][:], g[13][:, 0:1, :].to_broadcast([P, T, E]), bc(col(g[11], 1)), ALU.mult))
                    step(tt(w[:], g[14][:], g[15][:], ALU.add))

                def add_expert(ge):
                    e = ge % E
                    res = zacc if e else xs[ge // E]
                    dve.wait_ge(s_e2, FE * (ge + 1))
                    for t in range(T):
                        last = nc.vector.scalar_tensor_tensor(zacc[:, t, :], ps[:, t, :], w[:, t, e:e + 1],
                                                              res[:, t, :], ALU.mult, ALU.add)
                    last.then_inc(s_acc, 1)
                    dve.wait_ge(s_acc, ge + 1)

                for i in range(E * FE):
                    gi = b * E * FE + i
                    if gi + 1 < B * E * FE:
                        split_lo(n + 1, mwl[(gi + 1) % WSLOTS][:], mwh[(gi + 1) % WSLOTS][:])
                    n += 1
                    dve.wait_ge(s_eh, gi + 1)
                    sub(eal[gi % 2][:], ea[gi % 2][:], eah[gi % 2][:], s_el)
                    if i % FE == 0 and gi:
                        add_expert(gi // FE - 1)
                    if b and i == 0:
                        ln_stats(("M", 0), zacc)
                    if i == 0:
                        strengths()
                    if i == 1:
                        router_logits()
                    if i == 2:
                        top_two()
                    if b and i == 2:
                        ln_apply(("M", 0), zacc, xs[0])
                    if i == 3:
                        expert_weights()
                    if FE <= i < FE + E:
                        for t in range(T):
                            last = nc.vector.scalar_tensor_tensor(zacc[:, t, :], b2b[:, i - FE, :],
                                                                  w[:, t, i - FE:i - FE + 1], zacc[:, t, :],
                                                                  ALU.mult, ALU.add)
                        step(last)
                    if b == 0 and i == FE:
                        ln_apply(("A1", 1), xs[1], xs[1])
            add_expert(B * E - 1)
            ln_stats(("M", 1), zacc)
            ln_apply(("M", 1), zacc, xs[1])

        @block.tensor
        def _(pe):
            mm = nc.tensor.matmul

            def mm3(out, lh, ll, rh, rl, first, last):
                mm(out, lh, rh, start=first, stop=False)
                mm(out, ll, rh, start=False, stop=False)
                return mm(out, lh, rl, start=False, stop=last)

            def transposes(key, src):
                for h in range(HT):
                    for t in range(T):
                        last = nc.tensor.transpose(ps[:, TPB[key] + h, t * P:(t + 1) * P], src[:, t, h * P:(h + 1) * P], ident[:])
                    last.then_inc(s_tp, 1)

            def xt_ready(key, h):
                pe.wait_ge(s_tplo, 4 * TP[key] + h + 1)

            tok = lambda t: slice(t * P, (t + 1) * P)
            pe.wait_ge(s_const, 6)
            for b in range(B):
                q0, v0, o0 = A0BANKS[b]
                pe.wait_ge(s_wlo, 1)
                for k in range(3):
                    for h in range(HT):
                        if k == 0:
                            xt_ready(("A0", b), h)
                        c = slice(k * D0, (k + 1) * D0)
                        last = mm3(ps[:, q0 + k, :], w0h[:, h, c], w0l[:, h, c], XTh[:, h, :], XTl[:, h, :], h == 0,
                                   h == HT - 1)
                    last.then_inc(s_a0qkv, 1)
                pe.wait_ge(s_a0lo, 2 * (b + 1))
                if b:
                    pe.wait_ge(s_yread, b)
                for q in range(T):
                    mm3(ps[:, o0 + q, :], QTh[:, tok(q)], QTl[:, tok(q)], KTh[:], KTl[:], True,
                        True).then_inc(s_a0s, 1)
                pe.wait_ge(s_a0act, 3 * (b + 1))
                if v0 == o0 + T - 1:
                    pe.wait_ge(s_a0p, T * (b + 1))
                for t in range(T):
                    last = nc.tensor.transpose(ps[:, v0, tok(t)], vT[:, tok(t)], ident[:])
                last.then_inc(s_a0vt, 1)
                pe.wait_ge(s_a0p, T * (b + 1))
                pe.wait_ge(s_a0vlo, b + 1)
                for k in range(T):
                    for q in range(T):
                        last = nc.tensor.transpose(ps[:, q0 + k, tok(q)], P0[:, q, tok(k)], ident[:])
                    last.then_inc(s_a0pt, 1)
                for k in range(T):
                    pe.wait_ge(s_a0ptlo, T * b + k + 1)
                    last = mm3(ps[:, o0, :], Vh0[:, k, :], Vl0[:, k, :], PTh[:, k, :], PTl[:, k, :], k == 0,
                               k == T - 1)
                last.then_inc(s_a0ot, 1)
                pe.wait_ge(s_a0otlo, b + 1)
                if b:
                    pe.wait_ge(s_fnx, T)
                    transposes(("F0", 0), nx)
                pe.wait_ge(s_wlo, 2)
                for t in range(T):
                    mm3(ps[:, q0 + t, :], OTh[:, tok(t)], OTl[:, tok(t)], wo0h[:], wo0l[:], True,
                        True).then_inc(s_y, 1)
            n = 2
            for b in range(B):

                def down(gi):
                    pe.wait_ge(s_flo, gi + 1)
                    i = gi % NI
                    if i == 0:
                        pe.wait_ge(s_yread, LN["F0", b])
                    for t in range(T):
                        last = mm3(ps[:, t, :], hhi[gi % 2][:, tok(t)], hlo[gi % 2][:, tok(t)],
                                   fwh[gi % WSLOTS][:, 2 * H:], fwl[gi % WSLOTS][:, 2 * H:], i == 0, i == NI - 1)
                    last.then_inc(s_fdn, 1)

                for i in range(NI):
                    gi = b * NI + i
                    pe.wait_ge(s_wlo, n + 1)
                    n += 1
                    if gi >= 2:
                        pe.wait_ge(s_fsg, gi - 1)
                        pe.wait_ge(s_fh, gi - 1)
                    for k, sm in enumerate((s_fg, s_fu)):
                        for h in range(HT):
                            if i == 0 and k == 0:
                                xt_ready(("F0", b), h)
                            c = slice(k * H + h * P, k * H + (h + 1) * P)
                            last = mm3(ps[:, 4 + 2 * k + gi % 2, :], fwh[gi % WSLOTS][:, c], fwl[gi % WSLOTS][:, c],
                                       XTh[:, h, :], XTl[:, h, :], h == 0, h == HT - 1)
                        last.then_inc(sm, 1)
                    if i:
                        down(gi - 1)
                pe.wait_ge(s_fh, NI * (b + 1))
                if b == 0:
                    pe.wait_ge(s_fnx, 2 * T)
                    transposes(("F0", 1), nx)
                else:
                    pe.wait_ge(s_lnout, 4 * (LN["F0", 0] + 1))
                    transposes(("A1", 0), xs[0])
                down(b * NI + NI - 1)
            for b in range(B):
                n += 2
                pe.wait_ge(s_wlo, n)
                for h in range(HT):
                    xt_ready(("A1", b), h)
                if b == 0:
                    pe.wait_ge(s_yread, LN["A1", b])
                pb, ob = A1BANKS[b]

                def project(t):
                    bt = b * T + t
                    if t >= 2:
                        pe.wait_ge(s_qe, bt - 1)
                    r0 = pb + 2 * (t % 2)
                    for c0, c1, bank in ((0, 512, r0), (512, QKV1, r0 + 1)):
                        for h in range(HT):
                            last = mm3(ps[:, bank, 0:c1 - c0], XTh[:, h, tok(t)], XTl[:, h, tok(t)],
                                       w1h[:, h, c0:c1], w1l[:, h, c0:c1], h == 0, h == HT - 1)
                    last.then_inc(s_q, 1)

                def operands(t):
                    bt = b * T + t
                    pe.wait_ge(s_qlo, bt + 1)
                    if b and t == 0:
                        pe.wait_ge(s_yread, LN["A1", b])
                    for k in range(5):
                        u = 5 * bt + k
                        if u % (5 * T) >= 4:
                            v = u - 4
                            if v % 5 == 4:
                                pe.wait_ge(s_ek, v // 5 + 1)
                            else:
                                pe.wait_ge(s_eq, 4 * (v // 5) + v % 5 + 1)
                        for a in range(4):
                            if k < 4:
                                src = Qs[t % 2][:, 8 * k + 2 * a:8 * k + 2 * a + 2, :]
                            else:
                                src = (Ks0, Ks1)[t % 2][:, 2 * a:2 * a + 2, :]
                            last = nc.tensor.transpose(ps[:, ob + u % 4, tok(a)],
                                                       f32(src.rearrange("p a n -> p (a n)")), ident[:])
                        last.then_inc(s_tq, 1)

                for t in range(T):
                    project(t)
                    if t:
                        operands(t - 1)
                operands(T - 1)
                pe.wait_ge(s_eq, 16 * (b + 1))
                pe.wait_ge(s_ek, T * (b + 1))
                for p in range(PAIRS):
                    G = p // 4
                    for u in range(3):
                        n_u = (b * PAIRS + p) * 3 + u
                        r0 = 2 * (n_u % 2)
                        if n_u % (3 * PAIRS) >= 2:
                            pe.wait_ge(s_mx, n_u - 1)
                        if u < 2:
                            q = 3 - u
                            for s in range(2):
                                mm(ps[:, r0 + s, 0:(q + 1) * P], Qop[:, p, tok(q)], Kop[:, 2 * G + s, 0:(q + 1) * P],
                                   start=True, stop=False)
                                last = mm(ps[:, r0 + s, q * P:(q + 1) * P], identb[:], maskb[:], start=False,
                                          stop=True)
                        else:
                            for q in range(2):
                                w = (q + 1) * P
                                out = ps[:, r0 + q, 0:2 * w].rearrange("p (s k) -> p s k", s=2)
                                mm(out, Qop[:, p, tok(q)], Kop[:, 2 * G:2 * G + 2, 0:w], start=True, stop=False)
                                last = mm(out[:, :, q * P:w], identb[:], maskb[:, None, :].to_broadcast([P, 2, P]),
                                          start=False, stop=True)
                        last.then_inc(s_s1, 1)
                pe.wait_ge(s_mx, 3 * PAIRS * (b + 1))
                nc.tensor.transpose(ps[:, 4, 0:P], mtok[:].rearrange("p s h t -> p (s h t)"), ident[:]).then_inc(s_mt, 1)
                pe.wait_ge(s_mtl, b + 1)
                pe.wait_ge(s_md, 64 * (b + 1))

                def scores(gg):
                    G, s = gg // 2, gg % 2
                    for u in range(6):
                        n_u = (b * NKV + gg) * 6 + u
                        r0 = 2 * (n_u % 3)
                        if n_u % (6 * NKV) >= 3:
                            pe.wait_ge(s_p, n_u - 2)
                        kt = (0, 0, 1, 1, 2, 3)[u]
                        lhsT = Kop[:, 2 * G + s, tok(kt)]
                        if u < 4:
                            for a in range(2):
                                j = 2 * (u % 2) + a
                                mm(ps[:, r0 + a, 0:S - kt * P], lhsT, Qop[:, 4 * G + j, kt * P:S], start=True,
                                   stop=False)
                            for a in range(2):
                                last = mm(ps[:, r0 + a, 0:P], identb[:], maskT[:], start=False, stop=True)
                        elif u == 4:
                            for a in range(2):
                                j = 4 * G + 2 * a
                                mm(ps[:, r0 + a, :].rearrange("p (j q) -> p j q", j=2), lhsT,
                                   Qop[:, j:j + 2, 2 * P:S], start=True, stop=False)
                            for a in range(2):
                                last = mm(ps[:, r0 + a, :].rearrange("p (j q) -> p j q", j=2)[:, :, 0:P], identb[:],
                                          maskT[:, None, :].to_broadcast([P, 2, P]), start=False, stop=True)
                        else:
                            out = ps[:, r0, :].rearrange("p (j q) -> p j q", j=4)
                            mm(out, lhsT, Qop[:, 4 * G:4 * G + 4, 3 * P:S], start=True, stop=False)
                            last = mm(out, identb[:], maskT[:, None, :].to_broadcast([P, 4, P]), start=False,
                                      stop=True)
                        last.then_inc(s_s2, 1)

                def values(gg):
                    gi = b * NKV + gg
                    if gg == 0:
                        pe.wait_ge(s_v, 4 * T * (b + 1))
                    pe.wait_ge(s_pl, 6 * (gi + 1))
                    if gg:
                        pe.wait_ge(s_oe, 2 * gi)
                    for q in range(T):
                        for j in range(4):
                            c = ((q % 2) * 4 + j) * VW
                            out = ps[:, 6 + q // 2, c:c + VW]
                            for kt in range(q + 1):
                                o = (UO[j // 2] + (j % 2) * 512 + q * P, UO[2 + j // 2] + (j % 2) * 384 + (q - 1) * P,
                                     UO[4] + j * 256 + (q - 2) * P, UO[5] + j * P)[kt]
                                for part in (Ph, Pl):
                                    last = mm(out, part[gg % 2][:, o:o + P], Vs[:, kt, gg, :],
                                              start=kt == 0 and part is Ph, stop=kt == q and part is Pl)
                        if q % 2:
                            last.then_inc(s_o, 1)

                for gg in range(NKV):
                    scores(gg)
                    if gg:
                        values(gg - 1)
                values(NKV - 1)
                pe.wait_ge(s_oe, 2 * NKV * (b + 1))
                transposes(("O1", b), Otok)
                if b == 0:
                    pe.wait_ge(s_lnout, 4 * (LN["F0", 1] + 1))
                    transposes(("A1", 1), xs[1])
                else:
                    pe.wait_ge(s_lnout, 4 * (LN["A1", 0] + 1))
                    transposes(("M", 0), xs[0])
                n += 2
                pe.wait_ge(s_wlo, n)
                for h in range(HT):
                    xt_ready(("O1", b), h)
                for t in range(T):
                    for h in range(HT):
                        last = mm3(ps[:, t, :], OTh1[:, h, tok(t)], OTl1[:, h, tok(t)], wo1h[:, h, :], wo1l[:, h, :],
                                   h == 0, h == HT - 1)
                    last.then_inc(s_y, 1)
            for b in range(B):
                pe.wait_ge(s_gw, 2)
                def second(gi):
                    i = gi % (E * FE)
                    pe.wait_ge(s_el, gi + 1)
                    if gi == 0:
                        pe.wait_ge(s_yread, LN["M", 0])
                    if i % FE == 0 and gi >= FE:
                        pe.wait_ge(s_acc, gi // FE)
                    for t in range(T):
                        last = mm3(ps[:, t, :], eah[gi % 2][:, tok(t)], eal[gi % 2][:, tok(t)],
                                   mwh[gi % WSLOTS][:, H:], mwl[gi % WSLOTS][:, H:], i % FE == 0, i % FE == FE - 1)
                    last.then_inc(s_e2, 1)

                for i in range(E * FE):
                    gi = b * E * FE + i
                    pe.wait_ge(s_wlo, n + 1)
                    n += 1
                    if gi >= 2:
                        pe.wait_ge(s_ea, gi - 1)
                    for h in range(HT):
                        if i == 0:
                            xt_ready(("M", b), h)
                        last = mm3(ps[:, 4 + gi % 2, :], mwh[gi % WSLOTS][:, tok(h)], mwl[gi % WSLOTS][:, tok(h)],
                                   XTh[:, h, :], XTl[:, h, :], h == 0, h == HT - 1)
                    last.then_inc(s_pre, 1)
                    if i == 0:
                        for h in range(HT):
                            last = mm3(ps[:, 6, :], gwh[:, h, :], gwl[:, h, :], XTh[:, h, :], XTl[:, h, :], h == 0,
                                       h == HT - 1)
                        last.then_inc(s_lgT, 1)
                    if i == 1:
                        pe.wait_ge(s_lgTe, b + 1)
                        for t in range(T):
                            last = nc.tensor.transpose(ps[:, 7, tok(t)], lgT[:, tok(t)], ident[:])
                        last.then_inc(s_lg, 1)
                    if i:
                        second(gi - 1)
                    if i == 1:
                        pe.wait_ge(s_as, b + 1)
                        mm(ps[:, 6, 0:2], onesf[:], asum2[:], start=True, stop=True).then_inc(s_rkb, 1)
                    if i == 3:
                        pe.wait_ge(s_rk, 2 * (b + 1))
                        mm(ps[:, 6, 8:8 + E], row0[:], g[9][:, 0, :], start=True, stop=True).then_inc(s_rkb, 2)
                if b == 0:
                    pe.wait_ge(s_ea, E * FE)
                    pe.wait_ge(s_rkb, 3)
                    pe.wait_ge(s_acc, 1)
                    pe.wait_ge(s_lnout, 4 * (LN["A1", 1] + 1))
                    transposes(("M", 1), xs[1])
                second(b * E * FE + E * FE - 1)


_IN = ("x", "xT", "smallc", "bo0", "w_qkv0", "w_o0", "w_ffn", "cosb", "sinb", "bq1", "bo1",
       "w_qkv1", "w_o1", "gwr", "awt", "b2", "gb", "w_moe")


def tiles(w):
    return np.ascontiguousarray(w.reshape(-1, P, w.shape[1]).transpose(1, 0, 2)).reshape(P, -1)


def lay_out(a):
    f = np.float32
    x = a["L0_attn_x"]
    heads = np.arange(NH * HD).reshape(NKV // 2, 2, GROUP, HD).transpose(0, 2, 1, 3).reshape(-1)
    cols = np.concatenate([heads, np.arange(NH * HD, QKV1)])
    inv = 1.0 / 10000.0 ** (np.arange(0, HD, 2, dtype=f) / HD)
    ang = np.arange(S, dtype=f)[:, None] * inv[None, :].astype(f)
    cos = np.repeat(np.cos(ang).astype(f), 2, axis=1)
    sin = np.stack([-np.sin(ang), np.sin(ang)], axis=-1).astype(f).reshape(S, HD)
    by_tile = lambda v: np.ascontiguousarray(v.reshape(T, P, -1).transpose(1, 0, 2))
    smallc = np.zeros((P, 64), f)
    smallc[:, 0:3] = a["L0_attn_bqkv"].reshape(3, P).T
    smallc[:, 3:7] = a["L0_ffn_ln_w"].reshape(HT, P).T
    smallc[:, 8:20] = a["L1_ffn_b1"].reshape(E * FE, P).T
    gate, up, down = (a["L0_ffn_" + k] for k in ("gate_w", "up_w", "down_w"))
    w_ffn = np.concatenate([
        gate.reshape(NI, P, HT, P).transpose(0, 3, 2, 1).reshape(NI, P, H),
        up.reshape(NI, P, HT, P).transpose(0, 3, 2, 1).reshape(NI, P, H),
        down.T.reshape(NI, P, H)], axis=2)
    w_qkv1 = tiles(a["L1_attn_w_qkv"][cols].T).reshape(P, 2, CHUNK).transpose(1, 0, 2)
    w_o1 = tiles(a["L1_attn_w_o"].T[heads]).reshape(P, 2, 2 * H).transpose(1, 0, 2)
    w1, w2 = a["L1_ffn_w1"], a["L1_ffn_w2"]
    w_moe = np.concatenate([
        w1.reshape(E, HT, P, FE, P).transpose(0, 3, 2, 1, 4).reshape(E * FE, P, H),
        w2.reshape(E * FE, P, H)], axis=2)
    gwr = np.zeros((P, HT, P), f)
    gwr[:, :, 0:E] = a["L1_ffn_gate_w"][0:H].reshape(HT, P, E).transpose(1, 0, 2)
    text = (np.arange(S) >= VISION).astype(f)
    awt = np.stack([text / ((S - VISION) * H), (1 - text) / (VISION * H)]).astype(f)
    return {
        "x": x.reshape(B, T, P, H).transpose(0, 2, 1, 3),
        "xT": x.transpose(0, 2, 1).reshape(B, HT, P, S).transpose(0, 2, 1, 3),
        "smallc": smallc,
        "bo0": a["L0_attn_bo"], "w_qkv0": tiles(a["L0_attn_Wqkv"]), "w_o0": a["L0_attn_Wo"], "w_ffn": w_ffn,
        "cosb": by_tile(cos), "sinb": by_tile(sin),
        "bq1": a["L1_attn_b_qkv"][cols], "bo1": a["L1_attn_b_o"], "w_qkv1": w_qkv1, "w_o1": w_o1,
        "gwr": gwr, "awt": awt.reshape(2, T, P).transpose(2, 0, 1), "b2": a["L1_ffn_b2"],
        "gb": np.stack([a["L1_ffn_gate_w"][H], a["L1_ffn_gate_b"]]), "w_moe": w_moe,
    }


def kernel(**inputs):
    import concourse.bacc as bacc
    from concourse.bass_utils import run_bass_kernel_spmd

    nc = bacc.Bacc("TRN2", target_bir_lowering=False, num_devices=1)
    arrays = {n: np.ascontiguousarray(v) for n, v in lay_out({k: np.asarray(v) for k, v in inputs.items()}).items()}
    dram = {n: nc.dram_tensor(f"in_{n}", arrays[n].shape, mybir.dt.from_np(arrays[n].dtype),
                              kind="ExternalInput").ap() for n in _IN}
    dram["out"] = nc.dram_tensor("out_0", (B, P, T, H), F32, kind="ExternalOutput").ap()
    post_ln_layers(nc, dram)
    r = run_bass_kernel_spmd(nc, [{f"in_{n}": arrays[n] for n in _IN}], core_ids=[0])
    return r.results[0]["out_0"].transpose(0, 2, 1, 3).reshape(B, S, H)
```

```python
from contextlib import ExitStack

import numpy as np

import concourse.bass as bass
from concourse import mybir
from concourse.alu_op_type import AluOpType as ALU

ACT = mybir.ActivationFunctionType
F32 = mybir.dt.float32
F32R = mybir.dt.float32r
BF16 = mybir.dt.bfloat16
F16 = mybir.dt.float16
AX = mybir.AxisListType

P = 128
B = 2
S = 512
H = 512
T = S // P
HT = H // P
D0 = H // 4
F = 1792
NI = F // P
NH, NKV, HD = 32, 8, 16
GROUP = NH // NKV
PAIRS = NH // 2
HP = PAIRS // 2
HR = 64
E = 3
FE = H // P
VW = 3 * HD + 1
QK = (NH + NKV) * HD
QKV1 = QK + NKV * HD
LN_EPS = 1e-5
RMS_EPS = 1e-5
SCALE0 = float(D0) ** -0.5
SCALE1 = float(HD) ** -0.5
SHIFT1 = 14 * float(np.log(2.0))
MASKED = -1e30
RING = 4
CHUNK = 3 * H
VISION = int(S * 0.3)
UW = (1024, 1024, 768, 768, 1024, 512)
UO = tuple(sum(UW[:u]) for u in range(6))
W1_AT = (NI - 2, NI - 1)
PRING = 4
OUT_AT = 1
READ_AT = 2
EARLY = 4
EARLY_A = 2
WSLOTS = 3
FSTEPS = 2 * WSLOTS
assert (NI - 2) % FSTEPS == 0


def max_unit(p, u):
    if p < EARLY:
        return p if u == 2 else EARLY + 2 * p + u
    return 3 * p + u


def split_chunks():
    chunks = [("w_qkv0", None, HT * 3 * D0), ("w_o0", None, H)]
    for b in range(B):
        chunks += [("w_ffn", i, 3 * H) for i in range(NI)]
    for b in range(B):
        chunks += [("w_qkv1", i, CHUNK) for i in range(2)] + [("w_o1", i, 2 * H) for i in range(2)]
    for b in range(B):
        chunks += [("w_moe", i, 2 * H) for i in range(E * FE)]
    return chunks


def post_ln_layers(nc, dram):
    chunks = split_chunks()
    FIRST = {}
    for n, (name, i, _) in enumerate(chunks):
        FIRST.setdefault((name, i), []).append(n)
    ctx = ExitStack()
    with ctx:
        offset = [(nc.sbuf_base + 63) // 64 * 64]
        limit = nc.sbuf_usable_end

        def at(name, shape, dt, off):
            return nc.alloc_sbuf_tensor_at(name, shape, dt, offset=off)

        def size(shape, dt):
            n = int(np.prod(shape[1:])) * (2 if dt in (BF16, F16) else 4)
            return (n + 63) // 64 * 64

        def sb(name, shape, dt):
            t = at(name, shape, dt, offset[0])
            offset[0] += size(shape, dt)
            assert offset[0] <= limit, (name, offset[0], limit)
            return t

        def region(base, items):
            out = []
            for name, shape, dt in items:
                out.append(at(name, shape, dt, base))
                base += size(shape, dt)
            assert base <= limit, (items[-1][0], base, limit)
            return out, base

        def sem(name):
            return ctx.enter_context(nc.semaphore(name))

        xs = [sb(f"xs{b}", [P, T, H], F32) for b in range(B)]
        XTh = sb("XTh", [P, HT, S], F32R)
        XTl = sb("XTl", [P, HT, S], F32R)
        ident = sb("ident", [P, P], F32)
        identb = sb("identb", [P, P], BF16)
        maskb = sb("maskb", [P, P], BF16)
        maskT = sb("maskT", [P, P], BF16)
        onesf = sb("onesf", [P, P], F32)
        row0 = sb("row0", [P, P], F32)
        smallc = sb("smallc", [P, 64], F32)
        mv = sb("mv", [P, T, 2], F32)
        stats = sb("stats", [P, T, 6], F32)
        std = sb("std", [P, T], F32)
        rstd = sb("rstd", [P, T], F32)
        eps = sb("eps", [P, 1], F32)
        shift = sb("shift", [P, 1], F32)
        warm = sb("warm", [P, 1], F32)
        cosb = sb("cosb", [P, T, HD], F32)
        sinb = sb("sinb", [P, T, HD], F32)
        bq1 = sb("bq1", [P, QKV1], F32)
        bo1 = sb("bo1", [P, H], F32)
        raw = [sb(f"raw{i}", [P, CHUNK], F32) for i in range(RING)]
        base = offset[0]

        (w0h, w0l, wo0h, wo0l, QTh, QTl, KTh, KTl, vT, Vh0, Vl0, P0, PTh, PTl, OTh, OTl, xT, mx0, nm0, sum0, rs0,
         xb0, bo0), a0_end = region(base, [
            ("w0h", [P, HT, 3 * D0], F32R), ("w0l", [P, HT, 3 * D0], F32R),
            ("wo0h", [P, H], F32R), ("wo0l", [P, H], F32R),
            ("QTh", [P, S], F32R), ("QTl", [P, S], F32R), ("KTh", [P, S], F32R), ("KTl", [P, S], F32R),
            ("vT", [P, S], F32), ("Vh0", [P, T, D0], F32R), ("Vl0", [P, T, D0], F32R),
            ("P0", [P, T, S], F32), ("PTh", [P, T, S], F32R), ("PTl", [P, T, S], F32R),
            ("OTh", [P, S], F32R), ("OTl", [P, S], F32R), ("xT", [P, HT, S], F32),
            ("mx0", [P, T], F32), ("nm0", [P, T], F32), ("sum0", [P, T], F32), ("rs0", [P, T], F32),
            ("xb0", [P, T, H], F32), ("bo0", [P, H], F32)])
        (nx, ss, rr), f_end = region(a0_end, [("nx", [P, T, H], F32), ("ss", [P, T], F32), ("rr", [P, T], F32)])
        fwh, f_end = region(f_end, [(f"fwh{i}", [P, 3 * H], F32R) for i in range(WSLOTS)])
        fwl, f_end = region(f_end, [(f"fwl{i}", [P, 3 * H], F32R) for i in range(WSLOTS)])
        sg, f_end = region(f_end, [(f"sg{i}", [P, S], F32) for i in range(2)])
        hh, f_end = region(f_end, [(f"hh{i}", [P, S], F32) for i in range(2)])
        hhi, f_end = region(f_end, [(f"hhi{i}", [P, S], F32R) for i in range(2)])
        hlo, f_end = region(f_end, [(f"hlo{i}", [P, S], F32R) for i in range(2)])
        PW = 5120
        (Ph0, Ph1, Pl0, Pl1), p_end = region(base, [
            ("Ph0", [P, PW], F16), ("Ph1", [P, PW], F16), ("Pl0", [P, PW], F16), ("Pl1", [P, PW], F16)])
        Ph, Pl = [Ph0, Ph1], [Pl0, Pl1]
        (w1h, w1l, qkv0, qkv1, rot0, rot1, t2), end = region(base, [
            ("w1h", [P, HT, QKV1], F32R), ("w1l", [P, HT, QKV1], F32R), ("qkv0", [P, QKV1], F32),
            ("qkv1", [P, QKV1], F32), ("rot0", [P, QK], F32), ("rot1", [P, QK], F32), ("t2", [P, QK], F32)])
        qkv, rot = [qkv0, qkv1], [rot0, rot1]
        assert end <= p_end
        Pf, pf_end = region(p_end, [(f"Pf{i}", [P, 1024], F32) for i in range(PRING)])
        (Qs0, Ks0, Ks1), end = region(p_end, [
            ("Qs0", [P, NH, HR], F32R), ("Ks0", [P, NKV, HR], F32R), ("Ks1", [P, NKV, HR], F32R)])
        assert end <= pf_end <= a0_end
        (Qop, Kop, Vs, Otok, mtok, mTh0, mTh1, mTl0, mTl1, osum, orec, vr, OTh1, OTl1), a_end = region(pf_end, [
            ("Qop", [P, PAIRS, S], F32R), ("Kop", [P, NKV, S], F32R), ("Vs", [P, T, NKV, VW], BF16),
            ("Otok", [P, T, H], F32), ("mtok", [P, 2, 2, HP, T], F32),
            ("mTh0", [2 * HP * T, P], F32R), ("mTh1", [2 * HP * T, P], F32R), ("mTl0", [2 * HP * T, P], F32R),
            ("mTl1", [2 * HP * T, P], F32R), ("osum", [P, 16, HD], F32), ("orec", [P, 16], F32),
            ("vr", [P, NKV * HD], F32),
            ("OTh1", [P, HT, S], F32R), ("OTl1", [P, HT, S], F32R)])
        mTh, mTl = [mTh0, mTh1], [mTl0, mTl1]
        Qs = [Qs0, at("Qs1", [P, NH, HR], F32R, pf_end + size([P, PAIRS, S], F32R) + size([P, NKV, S], F32R)
                      + size([P, T, NKV, VW], BF16))]
        (wo1h, wo1l), _ = region(pf_end, [("wo1h", [P, HT, H], F32R), ("wo1l", [P, HT, H], F32R)])
        mwh, m_end = region(base, [(f"mwh{i}", [P, 2 * H], F32R) for i in range(WSLOTS)])
        mwl, m_end = region(m_end, [(f"mwl{i}", [P, 2 * H], F32R) for i in range(WSLOTS)])
        (gwr, gwh, gwl, lgT, lg, asum, awt, asum2, rat, gb, wsum), m_end = region(m_end, [
            ("gwr", [P, HT, P], F32), ("gwh", [P, HT, P], F32R), ("gwl", [P, HT, P], F32R), ("lgT", [P, S], F32),
            ("lg", [P, T, E], F32), ("asum", [P, T], F32), ("awt", [P, 2, T], F32), ("asum2", [P, 2], F32),
            ("rat", [P, 2], F32), ("gb", [P, 2, E], F32), ("wsum", [P, 2, T], F32)])
        g, m_end = region(m_end, [(f"g{i}", [P, T, E], F32) for i in range(17)])
        assert m_end <= p_end
        ea, m_end = region(p_end, [(f"ea{i}", [P, S], F32) for i in range(2)])
        eah, m_end = region(m_end, [(f"eah{i}", [P, S], F32R) for i in range(2)])
        eal, m_end = region(m_end, [(f"eal{i}", [P, S], F32R) for i in range(2)])
        assert m_end <= pf_end
        (b2b, zacc), m_end = region(pf_end + PAIRS * S * 4, [("b2b", [P, E, H], F32), ("zacc", [P, T, H], F32)])
        assert m_end <= pf_end + (PAIRS + NKV) * S * 4

        ps = ctx.enter_context(nc.psum_tensor("ps", [P, 8, 512], F32))

        A0BANKS = ((4, 7, 0), (0, 3, 4))
        A1P, A1O = 4, 0

        BQ, LNW, B1C = 0, 3, 8

        s_const_dma = sem("const_dma")
        s_const = sem("const_made")
        s_xT_in = [sem(f"xT_in{b}") for b in range(B)]
        s_x_in = [sem(f"x_in{b}") for b in range(B)]
        s_raw = [sem(f"raw_landed{i}") for i in range(RING)]
        s_whi = sem("weights_hi")
        s_wlo = sem("weights_lo")
        s_yread = sem("y_read")
        s_tp = sem("transposed")
        s_tphi = sem("xT_hi")
        s_tplo = sem("xT_lo")
        s_y = sem("y_full")
        s_var = sem("ln_var")
        s_std = sem("ln_std")
        s_chain = sem("dve_step")
        s_achain = sem("act_step")
        s_pchain = sem("pool_step")
        s_lnout = sem("ln_out")
        s_a0qkv, s_a0act, s_a0lo = sem("a0_qkv_full"), sem("a0_qkv_hi"), sem("a0_qk_lo")
        s_a0vt, s_a0vhi, s_a0vlo = sem("a0_v_transposed"), sem("a0_v_hi"), sem("a0_v_lo")
        s_a0s, s_a0nm, s_a0p = sem("a0_scores"), sem("a0_negmax"), sem("a0_probs")
        s_a0pt, s_a0pthi, s_a0ptlo = sem("a0_pT"), sem("a0_pT_hi"), sem("a0_pT_lo")
        s_a0ot, s_a0othi, s_a0otlo = sem("a0_oT"), sem("a0_oT_hi"), sem("a0_oT_lo")
        s_fss, s_fnx = sem("f_rms"), sem("f_nx")
        s_fg, s_fu, s_fsg, s_fh = sem("f_gate_full"), sem("f_up_full"), sem("f_silu"), sem("f_h")
        s_fhi, s_flo, s_fdn = sem("f_h_hi"), sem("f_h_lo"), sem("f_down")
        s_init = sem("a1_operands_init")
        s_q, s_qe = sem("a1_qkv_full"), sem("a1_qkv_read")
        s_rot, s_qhi, s_qlo, s_v = sem("a1_rotated"), sem("a1_qk_hi"), sem("a1_qk_lo"), sem("a1_v_parts")
        s_tq, s_eq, s_ek = sem("a1_qk_transposed"), sem("a1_q_operand"), sem("a1_k_operand")
        s_s1, s_mx = sem("a1_scores_for_max"), sem("a1_max")
        s_mt, s_mth, s_mtl = sem("a1_maxT"), sem("a1_maxT_hi"), sem("a1_maxT_lo")
        s_md = [sem(f"a1_max_rows{half}") for half in range(2)]
        s_s2, s_p, s_ph, s_pl = sem("a1_scores"), sem("a1_probs"), sem("a1_p_hi"), sem("a1_p_lo")
        s_o, s_oe, s_ot = sem("a1_out"), sem("a1_out_read"), sem("a1_out_tokens")
        s_cos, s_xb, s_xb0 = sem("a1_x_cos"), sem("a1_residual_bias"), sem("a0_residual_bias")
        s_gw, s_lgT, s_lgTe, s_lg, s_as, s_rt, s_rk, s_rkb = (
            sem("m_gate_w"), sem("m_logitsT"), sem("m_logitsT_read"), sem("m_logits"), sem("m_abs"), sem("m_ratio"),
            sem("m_rank"), sem("m_rank_bc"))
        s_pre, s_ea, s_eh, s_el, s_e2, s_acc = (sem("m_pre"), sem("m_act"), sem("m_act_hi"), sem("m_act_lo"),
                                                sem("m_expert_out"), sem("m_acc"))
        s_last = sem("m_last_output")
        s_gwd = sem("m_const_dma")
        s_a1d = sem("a1_const_dma")
        s_out = sem("out_written")

        N_CONST_DMA = 2

        def f32(ap):
            return ap.bitcast(F32)

        def rope(ap):
            return ap.rearrange("p (h i c) -> p h i c", h=NH + NKV, c=2)

        def table(t, k):
            return t[:, k, None, :].to_broadcast([P, NH + NKV, HD]).rearrange("p h (i c) -> p h i c", c=2)

        def heads_of(G, s):
            o = Otok[:].rearrange("p t (g j s d) -> p t g j s d", g=4, j=4, s=2)
            return o[:, :, G, :, s, :]

        def each_group_pair(engine, body, peel):
            if peel:
                body(0)
            with engine.Fori(int(peel), NKV // 2) as G:
                body(G)

        TP = {("A0", 0): 0, ("A0", 1): 1, ("F0", 0): 2, ("F0", 1): 3, ("A1", 0): 4, ("A1", 1): 5, ("O1", 0): 6,
              ("M", 0): 7, ("O1", 1): 8, ("M", 1): 9}
        TPP = {key: k - 2 for key, k in TP.items()}
        LN = {("A0", 0): 0, ("A0", 1): 1, ("F0", 0): 2, ("F0", 1): 3, ("A1", 0): 4, ("A1", 1): 5, ("M", 0): 6,
              ("M", 1): 7}
        Y = {("A0", 0): 0, ("A0", 1): 1, ("A1", 0): 2, ("A1", 1): 3}
        TPB = {("F0", 0): 4, ("F0", 1): 4, ("A1", 0): 4, ("O1", 0): 4, ("A1", 1): 0, ("O1", 1): 4, ("M", 0): 0,
               ("M", 1): 4}

        block = ctx.enter_context(nc.Block())

        @block.sync
        def _(sp):
            def load(n):
                name, i, cols = chunks[n]
                if n >= RING:
                    sp.wait_ge(s_wlo, n - RING + 1)
                src = dram[name] if i is None else dram[name][i]
                sp.dma_start(raw[n % RING][:, 0:cols], src).then_inc(s_raw[n % RING], 16)

            load(0)
            for b in range(B):
                if b:
                    sp.wait_ge(s_tplo, HT * b)
                sp.dma_start(xT[:], dram["xT"][b]).then_inc(s_xT_in[b], 16)
                if b == 0:
                    sp.wait_ge(s_xT_in[0], 16)
                    sp.dma_start(smallc[:], dram["smallc"]).then_inc(s_const_dma, 16)
                    load(1)
                sp.dma_start(xs[b][:], dram["x"][b]).then_inc(s_x_in[b], 16)
                if b == 0:
                    sp.dma_start(bo0[:], dram["bo0"].partition_broadcast(P)).then_inc(s_const_dma, 16)
                    for dst, name, bc in ((cosb, "cosb", False), (sinb, "sinb", False), (bq1, "bq1", True),
                                          (bo1, "bo1", True)):
                        src = dram[name].partition_broadcast(P) if bc else dram[name]
                        sp.dma_start(dst[:], src).then_inc(s_a1d, 16)
                    load(2)
                    load(3)
            n = 4
            while chunks[n][0] == "w_ffn":
                load(n)
                n += 1
            for b in range(B):
                for _ in range(2):
                    load(n)
                    n += 1
                load(n)
                load(n + 1)
                n += 2
                for half in range(2):
                    sp.wait_ge(s_mth, 2 * b + half + 1)
                    sp.wait_ge(s_mtl, 2 * b + half + 1)
                    for k, mt in enumerate((mTh, mTl)):
                        for s in range(2):
                            row = HR * s + 3 * HD + k
                            dst = f32(Qop[row:row + 1, HP * half:HP * (half + 1), :]).rearrange(
                                "o p (t q) -> o (p t) q", q=P)
                            src = f32(mt[half][HP * T * s:HP * T * (s + 1), :])
                            sp.dma_start(dst, src).then_inc(s_md[half], 16)
            sp.wait_ge(s_o, 2 * NKV * B)
            for dst, name, bc in ((gwr, "gwr", False), (awt, "awt", False)):
                sp.dma_start(dst[:], dram[name]).then_inc(s_gwd, 16)
            sp.dma_start(b2b[:], dram["b2"].partition_broadcast(P)).then_inc(s_gwd, 16)
            sp.dma_start(gb[:], dram["gb"].partition_broadcast(P)).then_inc(s_gwd, 16)
            while n < len(chunks):
                load(n)
                n += 1
            for b in range(B):
                for t in range(T):
                    sp.wait_ge(s_lnout, 4 * LN["M", b] + t + 1)
                    sp.dma_start(dram["out"][b, :, t, :], xs[b][:, t, :]).then_inc(s_out, 16)
            sp.wait_ge(s_out, 16 * B * T)

        @block.gpsimd
        def _(pool):
            nc.gpsimd.memset(eps[:], LN_EPS)
            nc.gpsimd.memset(shift[:], SHIFT1)
            nc.gpsimd.memset(onesf[:], 1.0).then_inc(s_const, 1)
            nc.gpsimd.memset(ident[:], 0.0).then_inc(s_pchain, 1)
            nc.gpsimd.memset(row0[:], 0.0).then_inc(s_pchain, 1)
            nc.gpsimd.memset(maskb[:], 0.0).then_inc(s_pchain, 1)
            nc.gpsimd.memset(maskT[:], 0.0).then_inc(s_pchain, 1)
            pool.wait_ge(s_pchain, 2)
            nc.gpsimd.affine_select(out=ident[:], in_=ident[:], compare_op=ALU.not_equal, fill=1.0, base=0,
                                    pattern=[[-1, P]], channel_multiplier=1).then_inc(s_const, 1)
            nc.gpsimd.affine_select(out=row0[:], in_=row0[:], compare_op=ALU.not_equal, fill=1.0, base=0,
                                    pattern=[[0, P]], channel_multiplier=1).then_inc(s_const, 1)

            pool.wait_ge(s_pchain, 3)
            nc.gpsimd.affine_select(out=maskb[:], in_=maskb[:], compare_op=ALU.is_ge, fill=MASKED, base=0,
                                    pattern=[[-1, P]], channel_multiplier=1).then_inc(s_const, 1)
            pool.wait_ge(s_pchain, 4)
            nc.gpsimd.affine_select(out=maskT[:], in_=maskT[:], compare_op=ALU.is_ge, fill=MASKED, base=0,
                                    pattern=[[1, P]], channel_multiplier=-1).then_inc(s_const, 1)
            pool.wait_ge(s_const_dma, 16 * N_CONST_DMA)
            for b in range(B):
                pool.wait_ge(s_x_in[b], 16)
                if b:
                    pool.wait_ge(s_yread, b)
                nc.gpsimd.tensor_tensor(xb0[:], xs[b][:], bo0[:, None, :].to_broadcast([P, T, H]),
                                        ALU.add).then_inc(s_xb0, 1)
            for b in range(B):
                if b == 0:
                    pool.wait_ge(s_fdn, NI * B)
                    nc.gpsimd.memset(f32(Kop[:]), 0.0)
                    nc.gpsimd.memset(Vs[:, :, :, VW - 1:VW], 1.0).then_inc(s_init, 1)
                if b:
                    pool.wait_ge(s_o, 2 * NKV * b)
                    pool.wait_ge(s_pl, 6 * NKV * b)
                    pool.wait_ge(s_tp, 4 * (TPP["O1", b - 1] + 1))
                for q in Qs:
                    nc.gpsimd.memset(f32(q[:, :, 3 * HD:HR]), 0.0)
                for k in (Ks0, Ks1):
                    nc.gpsimd.memset(f32(k[:, :, 3 * HD + 2:HR]), 0.0)
                    last = nc.gpsimd.memset(f32(k[:, :, 3 * HD:3 * HD + 2]), -1.0)
                last.then_inc(s_init, 1)
                for t in range(T):
                    bt = b * T + t
                    pool.wait_ge(s_qe, bt + 1)
                    if t >= 2:
                        pool.wait_ge(s_qhi, bt - 1)
                        pool.wait_ge(s_qlo, bt - 1)
                    x = qkv[t % 2]
                    nc.gpsimd.tensor_tensor(rope(rot[t % 2][:]), rope(x[:, 0:QK]), table(cosb, t),
                                            ALU.mult).then_inc(s_cos, 1)
                    v = x[:, QK:].rearrange("p (g d) -> p g d", d=HD)
                    r3 = vr[:].rearrange("p (g d) -> p g d", d=HD)
                    part = lambda k: Vs[:, t, :, k * HD:(k + 1) * HD]
                    for k, (op, src) in enumerate(((None, v), ((v, 0), r3), (None, r3), ((r3, 1), part(2)))):
                        if k:
                            pool.wait_ge(s_v, 4 * bt + k)
                        if op is None:
                            nc.gpsimd.tensor_copy(part(k // 2), src).then_inc(s_v, 1)
                        else:
                            nc.gpsimd.tensor_tensor(src, op[0], part(op[1]), ALU.subtract).then_inc(s_v, 1)
                pool.wait_ge(s_tplo, 4 * (TP["A1", b] + 1))
                pool.wait_ge(s_a1d, 64)
                nc.gpsimd.tensor_tensor(xs[b][:], xs[b][:], bo1[:, None, :].to_broadcast([P, T, H]),
                                        ALU.add).then_inc(s_xb, 1)

                def probs_hi(G):
                    for s in range(2):
                        if b or G:
                            pool.wait_ge(s_o, 2 * (b * NKV + s - 1) + 4 * G)
                        for u in range(6):
                            k = 6 * s + u
                            cols = UW[u]
                            pool.wait_ge(s_p, b * NKV * 6 + k + 1 + 12 * G)
                            nc.gpsimd.affine_select(out=Ph[s][:, UO[u]:UO[u] + cols], in_=Pf[k % PRING][:, 0:cols],
                                                    compare_op=ALU.is_equal, fill=0.0, base=0, pattern=[[0, cols]],
                                                    channel_multiplier=0).then_inc(s_ph, 1)
                            if u == OUT_AT and G:
                                outputs(G - 1, s)

                def outputs(G, s):
                    pool.wait_ge(s_oe, b * NKV + s + 1 + 2 * G)
                    nc.gpsimd.tensor_tensor(heads_of(G, s), osum[:].rearrange("p (t j) d -> p t j d", t=T),
                                            orec[:].rearrange("p (t j) -> p t j", t=T)[:, :, :, None].to_broadcast(
                                                [P, T, 4, HD]), ALU.mult).then_inc(s_ot, 1)

                for G in range(NKV // 2):
                    probs_hi(G)
                outputs(NKV // 2 - 1, 0)

        @block.scalar
        def _(act):
            def evac(out, in_, sm, func=ACT.Identity, **kw):
                return nc.scalar.activation(out, in_, func, **kw).then_inc(sm, 1)

            def tp_hi(key, scale=None):
                for h in range(HT):
                    act.wait_ge(s_tp, 4 * TPP[key] + h + 1)
                    kw = {} if scale is None else {"scale": scale[:, h:h + 1]}
                    dst = OTh1 if key[0] == "O1" else XTh
                    evac(dst[:, h, :], ps[:, TPB[key] + h, :], s_tphi, **kw)

            def ln_std(key):
                act.wait_ge(s_var, LN[key] + 1)
                nc.scalar.activation(std[:], mv[:, :, 1], ACT.Sqrt, bias=eps[:]).then_inc(s_std, 1)

            def split_hi(n, out):
                cols = chunks[n][2]
                act.wait_ge(s_raw[n % RING], 16 * (n // RING + 1))
                evac(out, raw[n % RING][:, 0:cols], s_whi)

            flat = lambda t: t.rearrange("p a n -> p (a n)")
            tok = lambda t: slice(t * P, (t + 1) * P)
            split_hi(0, flat(w0h[:]))

            def rms(b):
                act.wait_ge(s_lnout, 4 * (LN["A0", b] + 1))
                if b:
                    act.wait_ge(s_tp, 4 * b)
                for t in range(T):
                    last = nc.scalar.activation(nx[:, t, :], xs[b][:, t, :], ACT.Square, accum_out=ss[:, t:t + 1])
                last.then_inc(s_achain, 1)
                act.wait_ge(s_achain, b + 1)
                nc.scalar.activation(rr[:], ss[:], ACT.Sqrt, bias=eps[:], scale=1.0 / H).then_inc(s_fss, 1)

            def x_hi(b):
                act.wait_ge(s_xT_in[b], 16)
                if b:
                    act.wait_ge(s_a0qkv, 3 * b)
                for h in range(HT):
                    evac(XTh[:, h, :], xT[:, h, :], s_tphi)

            x_hi(0)
            split_hi(1, wo0h[:])
            act.wait_ge(s_const, 5)
            act.wait_ge(s_const_dma, 16 * N_CONST_DMA)
            for b in range(B):
                q0, v0, o0 = A0BANKS[b]
                for k, out in enumerate((QTh, KTh, vT)):
                    act.wait_ge(s_a0qkv, 3 * b + k + 1)
                    evac(out[:], ps[:, q0 + k, :], s_a0act, bias=smallc[:, BQ + k:BQ + k + 1])
                if b:
                    rms(0)
                for q in range(T):
                    act.wait_ge(s_a0nm, T * b + q + 1)
                    nc.scalar.activation(P0[:, q, :], ps[:, o0 + q, :], ACT.Exp, bias=nm0[:, q:q + 1], scale=SCALE0,
                                         accum_out=sum0[:, q:q + 1]).then_inc(s_a0p, 1)
                act.wait_ge(s_a0vt, b + 1)
                evac(Vh0[:].rearrange("p t d -> p (t d)"), ps[:, v0, :], s_a0vhi)
                for k in range(T):
                    act.wait_ge(s_a0pt, T * b + k + 1)
                    evac(PTh[:, k, :], ps[:, q0 + k, :], s_a0pthi)
                if b + 1 < B:
                    x_hi(b + 1)
                else:
                    split_hi(2, fwh[0][:])
                act.wait_ge(s_a0ot, b + 1)
                evac(OTh[:], ps[:, o0, :], s_a0othi)
                if b == 0:
                    ln_std(("A0", 0))
            n = 2
            for b in range(B):
                tp_hi(("F0", b), smallc[:, LNW:LNW + HT])
                for i in range(NI):
                    gi = b * NI + i
                    n += 1
                    if gi + 1 < B * NI:
                        if gi + 1 >= WSLOTS:
                            act.wait_ge(s_fdn, gi - WSLOTS + 2)
                        split_hi(n, fwh[(gi + 1) % WSLOTS][:])
                    act.wait_ge(s_fg, gi + 1)
                    if gi >= 2:
                        act.wait_ge(s_fh, gi - 1)
                    nc.scalar.activation(sg[gi % 2][:], ps[:, 4 + gi % 2, :], ACT.Silu).then_inc(s_fsg, 1)
                    act.wait_ge(s_fh, gi + 1)
                    if gi >= 2:
                        act.wait_ge(s_fdn, gi - 1)
                    evac(hhi[gi % 2][:], hh[gi % 2][:], s_fhi)
                    if b == 0 and i == 1:
                        ln_std(("A0", 1))
                    if b == 0 and i == 4:
                        rms(1)
                    if b == 1 and i == 3:
                        ln_std(("F0", 0))
                    if b == 1 and i in W1_AT:
                        k = W1_AT.index(i)
                        split_hi(2 + NI * B + k, flat(w1h[:, 2 * k:2 * k + 2, :]))
            for b in range(B):
                n += 2
                if b == 0:
                    tp_hi(("A1", 0))
                act.wait_ge(s_init, b + 2)

                def q_operands(t):
                    for k in range(4):
                        u = 5 * (b * T + t) + k
                        act.wait_ge(s_tq, u + 1)
                        evac(Qop[:, 4 * k:4 * k + 4, t * P:(t + 1) * P],
                             ps[:, ob + u % 4, :].rearrange("p (a q) -> p a q", a=4), s_eq)

                ob = A1O
                for t in range(T):
                    bt = b * T + t
                    if t:
                        q_operands(t - 1)
                    if t == 1:
                        ln_std(("F0", 1) if b == 0 else ("A1", 0))
                    act.wait_ge(s_rot, bt + 1)
                    r = rot[t % 2][:, 0:NH * HD].rearrange("p (h d) -> p h d", d=HD)
                    o = Qs[t % 2][:].rearrange("p h (k d) -> p h k d", d=HD)
                    for k in (0, 2):
                        nc.scalar.activation(o[:, :, k, :], r, ACT.Identity)
                    r = rot[t % 2][:, NH * HD:].rearrange("p (h d) -> p h d", d=HD)
                    o = (Ks0, Ks1)[t % 2][:].rearrange("p h (k d) -> p h k d", d=HD)
                    nc.scalar.activation(o[:, :, 0, :], r, ACT.Identity)
                    nc.scalar.activation(o[:, :, 1, :], r, ACT.Identity).then_inc(s_qhi, 1)
                q_operands(T - 1)
                for half in range(2):
                    act.wait_ge(s_mt, 2 * b + half + 1)
                    evac(mTh[half][:], ps[0:2 * HP * T, 4, tok(half)], s_mth)

                def probs(G):
                    first = b == 0 and isinstance(G, int)
                    for k in range(12):
                        u = k % 6
                        act.wait_ge(s_s2, b * NKV * 6 + k + 1 + 12 * G)
                        if not first or k >= PRING:
                            act.wait_ge(s_pl, b * NKV * 6 + k - PRING + 1 + 12 * G)
                        banks = 1 if u == 5 else 2
                        r0 = 2 * (k % 3)
                        src = ps[:, r0:r0 + banks, 0:UW[u] // banks]
                        nc.scalar.activation(Pf[k % PRING][:, 0:UW[u]].rearrange("p (a n) -> p a n", a=banks), src,
                                             ACT.Exp, bias=shift[:], scale=SCALE1).then_inc(s_p, 1)

                each_group_pair(act, probs, b == 0)
                for k in range(2):
                    split_hi(n, flat(wo1h[:, 2 * k:2 * k + 2, :]))
                    n += 1
                tp_hi(("A1", 1) if b == 0 else ("M", 0))
                act.wait_ge(s_o, 2 * NKV * (b + 1))
                if b == 0:
                    for k in range(2):
                        split_hi(n + k, flat(w1h[:, 2 * k:2 * k + 2, :]))
                tp_hi(("O1", b))
            for b in range(B):
                if b == 0:
                    act.wait_ge(s_gwd, 64)
                    evac(gwh[:], gwr[:], s_gw)
                if b == 0:
                    split_hi(n, mwh[0][:])
                else:
                    tp_hi(("M", b))
                for i in range(E * FE):
                    gi = b * E * FE + i
                    n += 1
                    if gi + 1 < B * E * FE:
                        if gi + 1 >= WSLOTS:
                            act.wait_ge(s_e2, gi - WSLOTS + 2)
                        split_hi(n, mwh[(gi + 1) % WSLOTS][:])
                    act.wait_ge(s_pre, gi + 1)
                    if gi >= 2:
                        act.wait_ge(s_el, gi - 1)
                    func = (ACT.Tanh, ACT.Gelu, ACT.Silu)[i // FE]
                    nc.scalar.activation(ea[gi % 2][:], ps[:, 4 + gi % 2, :], func,
                                         bias=smallc[:, B1C + i:B1C + i + 1]).then_inc(s_ea, 1)
                    act.wait_ge(s_ea, gi + 1)
                    if gi >= 2:
                        act.wait_ge(s_e2, gi - 1)
                    evac(eah[gi % 2][:], ea[gi % 2][:], s_eh)
                    if i == 0:
                        act.wait_ge(s_lgT, b + 1)
                        evac(lgT[:], ps[:, 6, :], s_lgTe)
                    if i == 2:
                        act.wait_ge(s_rk, 2 * b + 1)
                        nc.scalar.activation(g[1][:], g[0][:], ACT.Exp).then_inc(s_rt, 1)
                        ln_std(("A1", 1) if b == 0 else ("M", 0))
            nc.scalar.activation(warm[:], eps[:], ACT.Sqrt, bias=eps[:])
            ln_std(("M", 1))

        @block.vector
        def _(dve):
            steps = [0]

            def step(ins):
                steps[0] += 1
                ins.then_inc(s_chain, 1)
                dve.wait_ge(s_chain, steps[0])

            def sub(out, a, hi, sm):
                return nc.vector.tensor_tensor(out, a, f32(hi), ALU.subtract).then_inc(sm, 1)

            def split_lo(n, out, hi):
                cols = chunks[n][2]
                dve.wait_ge(s_whi, n + 1)
                sub(out, raw[n % RING][:, 0:cols], hi, s_wlo)

            def tp_lo(key, scale=None):
                n = TP[key]
                for h in range(HT):
                    dve.wait_ge(s_tphi, 4 * n + h + 1)
                    bank = TPB[key] + h
                    if scale is None:
                        hi, lo = (OTh1, OTl1) if key[0] == "O1" else (XTh, XTl)
                        sub(lo[:, h, :], ps[:, bank, :], hi[:, h, :], s_tplo)
                    else:
                        nc.vector.scalar_tensor_tensor(XTl[:, h, :], ps[:, bank, :], scale[:, h:h + 1],
                                                       f32(XTh[:, h, :]), ALU.mult, ALU.subtract).then_inc(s_tplo, 1)

            def ln_stats(key, z):
                for t in range(T):
                    last = nc.vector.bn_stats(stats[:, t, :], z[:, t, :])
                step(last)
                for t in range(T):
                    last = nc.vector.bn_aggr(mv[:, t, :], stats[:, t, :])
                last.then_inc(s_var, 1)

            def ln_apply(key, z, out):
                dve.wait_ge(s_var, LN[key] + 1)
                dve.wait_ge(s_std, LN[key] + 1)
                step(nc.vector.reciprocal(rstd[:], std[:]))
                for t in range(T):
                    nc.vector.tensor_scalar(out[:, t, :], z[:, t, :], mv[:, t, 0:1], rstd[:, t:t + 1], ALU.subtract,
                                            ALU.mult).then_inc(s_lnout, 1)
                dve.wait_ge(s_lnout, 4 * (LN[key] + 1))

            def add_y(key, bank, x, ready=None):
                for t in range(T):
                    if ready is not None:
                        dve.wait_ge(s_y, ready + t + 1)
                    last = nc.vector.tensor_tensor(x[:, t, :], ps[:, bank + t, :], x[:, t, :], ALU.add)
                last.then_inc(s_yread, 1)
                dve.wait_ge(s_yread, LN[key] + 1)

            def normed_rms(b):
                dve.wait_ge(s_fss, b + 1)
                step(nc.vector.reciprocal(ss[:], rr[:]))
                for t in range(T):
                    nc.vector.tensor_scalar(nx[:, t, :], xs[b][:, t, :], ss[:, t:t + 1], None,
                                            ALU.mult).then_inc(s_fnx, 1)

            flat = lambda t: t[:].rearrange("p a n -> p (a n)")
            split_lo(0, flat(w0l), flat(w0h))
            dve.wait_ge(s_const, 5)
            nc.vector.tensor_copy(identb[:], ident[:]).then_inc(s_const, 1)

            def x_lo(b):
                dve.wait_ge(s_xT_in[b], 16)
                for h in range(HT):
                    dve.wait_ge(s_tphi, 4 * b + h + 1)
                    sub(XTl[:, h, :], xT[:, h, :], XTh[:, h, :], s_tplo)

            x_lo(0)
            split_lo(1, wo0l[:], wo0h[:])
            dve.wait_ge(s_const_dma, 16 * N_CONST_DMA)
            for b in range(B):
                q0, v0, o0 = A0BANKS[b]
                for k, (lo, hi) in enumerate(((QTl, QTh), (KTl, KTh))):
                    dve.wait_ge(s_a0act, 3 * b + k + 1)
                    nc.vector.scalar_tensor_tensor(lo[:], ps[:, q0 + k, :], smallc[:, BQ + k:BQ + k + 1], f32(hi[:]),
                                                   ALU.add, ALU.subtract).then_inc(s_a0lo, 1)
                for q in range(T):
                    dve.wait_ge(s_a0s, T * b + q + 1)
                    step(nc.vector.reduce_max(mx0[:, q:q + 1], ps[:, o0 + q, :], AX.X))
                    nc.vector.tensor_scalar(nm0[:, q:q + 1], mx0[:, q:q + 1], -SCALE0, None,
                                            ALU.mult).then_inc(s_a0nm, 1)
                if b:
                    normed_rms(0)
                dve.wait_ge(s_a0vhi, b + 1)
                sub(flat(Vl0), ps[:, v0, :], flat(Vh0), s_a0vlo)
                for k in range(T):
                    dve.wait_ge(s_a0pthi, T * b + k + 1)
                    sub(PTl[:, k, :], ps[:, q0 + k, :], PTh[:, k, :], s_a0ptlo)
                if b + 1 < B:
                    x_lo(b + 1)
                else:
                    split_lo(2, fwl[0][:], fwh[0][:])
                dve.wait_ge(s_a0othi, b + 1)
                sub(OTl[:], ps[:, o0, :], OTh[:], s_a0otlo)
                if b:
                    tp_lo(("F0", 0), smallc[:, LNW:LNW + HT])
                dve.wait_ge(s_a0p, T * (b + 1))
                dve.wait_ge(s_xb0, b + 1)
                step(nc.vector.reciprocal(rs0[:], sum0[:]))
                for t in range(T):
                    dve.wait_ge(s_y, 4 * Y["A0", b] + t + 1)
                    last = nc.vector.scalar_tensor_tensor(xs[b][:, t, :], ps[:, q0 + t, :], rs0[:, t:t + 1],
                                                          xb0[:, t, :], ALU.mult, ALU.add)
                last.then_inc(s_yread, 1)
                dve.wait_ge(s_yread, b + 1)
                if b == 0:
                    ln_stats(("A0", 0), xs[0])
                    ln_apply(("A0", 0), xs[0], xs[0])
            n = 2
            for b in range(B):
                if b:
                    tp_lo(("F0", b), smallc[:, LNW:LNW + HT])
                for i in range(NI):
                    gi = b * NI + i
                    if gi + 1 < B * NI:
                        split_lo(n + 1, fwl[(gi + 1) % WSLOTS][:], fwh[(gi + 1) % WSLOTS][:])
                    n += 1
                    dve.wait_ge(s_fsg, gi + 1)
                    dve.wait_ge(s_fu, gi + 1)
                    nc.vector.tensor_tensor(hh[gi % 2][:], sg[gi % 2][:], ps[:, 6 + gi % 2, :],
                                            ALU.mult).then_inc(s_fh, 1)
                    dve.wait_ge(s_fhi, gi + 1)
                    sub(hlo[gi % 2][:], hh[gi % 2][:], hhi[gi % 2][:], s_flo)
                    if b == 0 and i == 0:
                        ln_stats(("A0", 1), xs[1])
                    if b == 0 and i == 2:
                        ln_apply(("A0", 1), xs[1], xs[1])
                    if b == 0 and i == 5:
                        normed_rms(1)
                    if b == 1 and i == 0:
                        add_y(("F0", 0), 0, xs[0])
                    if b == 1 and i == 1:
                        ln_stats(("F0", 0), xs[0])
                    if b == 1 and i == 4:
                        ln_apply(("F0", 0), xs[0], xs[0])
                    if b == 1 and i in W1_AT:
                        k = W1_AT.index(i)
                        split_lo(2 + NI * B + k, flat(w1l[:, 2 * k:2 * k + 2, :]),
                                 flat(w1h[:, 2 * k:2 * k + 2, :]))
            for b in range(B):
                n += 2
                if b == 0:
                    tp_lo(("A1", 0))
                last_key = ("F0", 1) if b == 0 else ("A1", 0)
                last_x = xs[1] if b == 0 else xs[0]
                if b == 0:
                    dve.wait_ge(s_fdn, NI * B)
                    add_y(last_key, 0, last_x)
                else:
                    dve.wait_ge(s_xb, b)
                    add_y(last_key, 0, last_x, 4 * Y["A1", b - 1])
                dve.wait_ge(s_a1d, 64)
                dve.wait_ge(s_init, b + 2)
                pb, ob = A1P, A1O

                def k_operands(t):
                    u = 5 * (b * T + t) + 4
                    dve.wait_ge(s_tq, u + 1)
                    src = ps[:, ob + u % 4, :].rearrange("p (a q) -> p a q", a=4)
                    for s in range(2):
                        last = nc.vector.tensor_copy(Kop[HR * s:HR * s + HR, s::2, t * P:(t + 1) * P],
                                                     src[HR * s:HR * s + HR])
                    last.then_inc(s_ek, 1)

                def maxima(p, u):
                    n_u = 3 * PAIRS * b + max_unit(p, u)
                    r0 = (A1P if u == 2 and p < EARLY else 0) + 2 * (n_u % 2)
                    dve.wait_ge(s_s1, n_u + 1)
                    if u < 2:
                        q = 3 - u
                        last = nc.vector.reduce_max(mtok[:, p // HP, :, p % HP, q], ps[:, r0:r0 + 2, 0:(q + 1) * P],
                                                    AX.X)
                    else:
                        for q in range(2):
                            w = (q + 1) * P
                            last = nc.vector.reduce_max(mtok[:, p // HP, :, p % HP, q],
                                                        ps[:, r0 + q, 0:2 * w].rearrange("p (s k) -> p s k", s=2),
                                                        AX.X)
                    last.then_inc(s_mx, 1)

                for t in range(T):
                    bt = b * T + t
                    dve.wait_ge(s_q, bt + 1)
                    if t >= 2:
                        dve.wait_ge(s_v, 4 * (bt - 1))
                    x, r = qkv[t % 2], rot[t % 2]
                    nc.vector.tensor_tensor(x[:], ps[:, pb + 2 * (t % 2):pb + 2 * (t % 2) + 2, :].rearrange(
                        "p a n -> p (a n)")[:, 0:QKV1], bq1[:], ALU.add).then_inc(s_qe, 1)
                    dve.wait_ge(s_qe, bt + 1)
                    step(nc.vector.tensor_tensor(rope(t2[:]), rope(x[:, 0:QK])[:, :, :, ::-1], table(sinb, t),
                                                 ALU.mult))
                    if t:
                        k_operands(t - 1)
                    dve.wait_ge(s_cos, bt + 1)
                    nc.vector.tensor_tensor(r[:], r[:], t2[:], ALU.add).then_inc(s_rot, 1)
                    if t == 2:
                        ln_apply(last_key, last_x, last_x)
                    if t == T - 1:
                        for p in range(0, EARLY_A):
                            maxima(p, 2)
                    dve.wait_ge(s_qhi, bt + 1)
                    dve.wait_ge(s_rot, bt + 1)
                    rq = r[:, 0:NH * HD].rearrange("p (h d) -> p h d", d=HD)
                    o = Qs[t % 2][:].rearrange("p h (k d) -> p h k d", d=HD)
                    nc.vector.tensor_tensor(o[:, :, 1, :], rq, f32(o[:, :, 0, :]), ALU.subtract)
                    rk = r[:, NH * HD:].rearrange("p (h d) -> p h d", d=HD)
                    o = (Ks0, Ks1)[t % 2][:].rearrange("p h (k d) -> p h k d", d=HD)
                    nc.vector.tensor_tensor(o[:, :, 2, :], rk, f32(o[:, :, 0, :]), ALU.subtract).then_inc(s_qlo, 1)
                    if t == 0:
                        ln_stats(last_key, last_x)
                for p in range(EARLY_A, EARLY):
                    maxima(p, 2)
                k_operands(T - 1)
                for p in range(PAIRS):
                    for u in range(2 if p < EARLY else 3):
                        maxima(p, u)
                    if p in (HP + 1, PAIRS - 1):
                        half = int(p > HP + 1)
                        dve.wait_ge(s_mth, 2 * b + half + 1)
                        sub(mTl[half][:], ps[0:2 * HP * T, 4, half * P:(half + 1) * P], mTh[half][:], s_mtl)

                def read_out(gg):
                    gi = b * NKV + gg
                    if gi:
                        dve.wait_ge(s_ot, gi)
                    src = ps[:, 6:8, 0:8 * VW].rearrange("p b (h c) -> p b h c", c=VW)
                    for k in range(2):
                        dve.wait_ge(s_o, 2 * gi + k + 1)
                        if k:
                            nc.vector.reciprocal(orec[:].rearrange("p (b h) -> p b h", b=2), src[:, :, :, VW - 1])
                        last = nc.vector.tensor_reduce(osum[:, 8 * k:8 * k + 8, :],
                                                       src[:, k, :, 0:3 * HD].rearrange("p h (k d) -> p h d k", k=3),
                                                       AX.X, ALU.add)
                    last.then_inc(s_oe, 1)
                    if gg == NKV - 1:
                        dve.wait_ge(s_oe, gi + 1)
                        nc.vector.tensor_tensor(
                            heads_of(gg // 2, gg % 2), osum[:].rearrange("p (t j) d -> p t j d", t=T),
                            orec[:].rearrange("p (t j) -> p t j", t=T)[:, :, :, None].to_broadcast([P, T, 4, HD]),
                            ALU.mult).then_inc(s_ot, 1)

                for gg in range(NKV):
                    for u in range(6):
                        n_u = (b * NKV + gg) * 6 + u
                        dve.wait_ge(s_ph, n_u + 1)
                        sl = slice(UO[u], UO[u] + UW[u])
                        nc.vector.tensor_tensor(Pl[gg % 2][:, sl], Pf[n_u % PRING][:, 0:UW[u]], Ph[gg % 2][:, sl],
                                                ALU.subtract).then_inc(s_pl, 1)
                        if gg and u == READ_AT:
                            read_out(gg - 1)
                for k in range(2):
                    split_lo(n, flat(wo1l[:, 2 * k:2 * k + 2, :]), flat(wo1h[:, 2 * k:2 * k + 2, :]))
                    n += 1
                read_out(NKV - 1)
                tp_lo(("A1", 1) if b == 0 else ("M", 0))
                tp_lo(("O1", b))
                if b == 0:
                    for k in range(2):
                        split_lo(n + k, flat(w1l[:, 2 * k:2 * k + 2, :]), flat(w1h[:, 2 * k:2 * k + 2, :]))
            for b in range(B):
                x = xs[b]
                dve.wait_ge(s_gwd, 64)
                if b == 0:
                    dve.wait_ge(s_gw, 1)
                    sub(flat(gwl), flat(gwr), flat(gwh), s_gw)
                    split_lo(n, mwl[0][:], mwh[0][:])
                    dve.wait_ge(s_xb, B)
                    add_y(("A1", 1), 0, xs[1], 4 * Y["A1", 1])
                    ln_stats(("A1", 1), xs[1])
                else:
                    tp_lo(("M", b))

                col = lambda t, k: t[:, :, k:k + 1]
                bc = lambda a: a.to_broadcast([P, T, E])
                tt = nc.vector.tensor_tensor
                w = g[16]

                def strengths():
                    step(nc.vector.tensor_reduce(asum[:], x[:], AX.X, ALU.add, apply_absolute_value=True))
                    nc.vector.tensor_tensor(wsum[:, 0, :], asum[:], awt[:, 0, :], ALU.mult)
                    step(nc.vector.tensor_tensor(wsum[:, 1, :], asum[:], awt[:, 1, :], ALU.mult))
                    for k in range(2):
                        last = nc.vector.reduce_sum(asum2[:, k:k + 1], wsum[:, k, :], AX.X)
                    last.then_inc(s_as, 1)

                def router_logits():
                    dve.wait_ge(s_rkb, 3 * b + 1)
                    step(nc.vector.tensor_scalar(rat[:, 1:2], ps[:, 6, 1:2], 1e-8, None, ALU.add))
                    step(nc.vector.reciprocal(rat[:, 1:2], rat[:, 1:2]))
                    step(nc.vector.tensor_tensor(rat[:, 0:1], ps[:, 6, 0:1], rat[:, 1:2], ALU.mult))
                    step(nc.vector.scalar_tensor_tensor(lg[:, 0, :], gb[:, 0, :], rat[:, 0:1], gb[:, 1, :], ALU.mult,
                                                        ALU.add))
                    dve.wait_ge(s_lg, b + 1)
                    logits = ps[:, 7, :].rearrange("p (t e) -> p t e", t=T)[:, :, 0:E]
                    step(nc.vector.tensor_tensor(g[2][:], logits, lg[:, 0:1, :].to_broadcast([P, T, E]), ALU.add))
                    step(nc.vector.reduce_max(g[3][:, :, 0:1], g[2][:], AX.X))
                    tt(g[0][:], g[2][:], bc(col(g[3], 0)), ALU.subtract).then_inc(s_rk, 1)

                def top_two():
                    dve.wait_ge(s_rt, b + 1)
                    step(nc.vector.reduce_sum(g[3][:, :, 1:2], g[1][:], AX.X))
                    step(nc.vector.reciprocal(g[3][:, :, 2:3], g[3][:, :, 1:2]))
                    step(tt(g[4][:], g[1][:], bc(col(g[3], 2)), ALU.mult))
                    a, c, d = (col(g[4], k) for k in range(3))
                    tt(col(g[7], 0), a, c, ALU.is_lt)
                    tt(col(g[7], 1), a, d, ALU.is_lt)
                    step(tt(col(g[7], 2), c, d, ALU.is_lt))
                    step(nc.vector.tensor_scalar(g[8][:], g[7][:], -1.0, 1.0, ALU.mult, ALU.add))
                    tt(col(g[9], 0), col(g[7], 0), col(g[7], 1), ALU.add)
                    tt(col(g[9], 1), col(g[8], 0), col(g[7], 2), ALU.add)
                    tt(col(g[9], 2), col(g[8], 1), col(g[8], 2), ALU.add).then_inc(s_rk, 1)
                    tt(col(g[6], 0), a, c, ALU.max)
                    step(tt(col(g[6], 1), a, c, ALU.min))
                    step(tt(col(g[6], 2), col(g[6], 0), d, ALU.min))
                    tt(col(g[5], 0), col(g[6], 0), d, ALU.max)
                    step(tt(col(g[5], 1), col(g[6], 1), col(g[6], 2), ALU.max))
                    step(tt(col(g[10], 0), col(g[5], 0), col(g[5], 1), ALU.add))
                    step(nc.vector.tensor_scalar(col(g[10], 1), col(g[10], 0), 1e-8, None, ALU.add))
                    step(nc.vector.reciprocal(col(g[10], 2), col(g[10], 1)))
                    step(tt(g[11][:, :, 0:2], g[5][:, :, 0:2], col(g[10], 2).to_broadcast([P, T, 2]), ALU.mult))

                def expert_weights():
                    dve.wait_ge(s_rkb, 3 * b + 3)
                    rank = ps[:, 6, 8:8 + E]
                    nc.vector.tensor_scalar(g[12][:, 0, :], rank, 0.0, None, ALU.is_equal)
                    step(nc.vector.tensor_scalar(g[13][:, 0, :], rank, 1.0, None, ALU.is_equal))
                    tt(g[14][:], g[12][:, 0:1, :].to_broadcast([P, T, E]), bc(col(g[11], 0)), ALU.mult)
                    step(tt(g[15][:], g[13][:, 0:1, :].to_broadcast([P, T, E]), bc(col(g[11], 1)), ALU.mult))
                    step(tt(w[:], g[14][:], g[15][:], ALU.add))

                def add_expert(ge):
                    e = ge % E
                    res = zacc if e else xs[ge // E]
                    dve.wait_ge(s_e2, FE * (ge + 1))
                    for t in range(T):
                        last = nc.vector.scalar_tensor_tensor(zacc[:, t, :], ps[:, t, :], w[:, t, e:e + 1],
                                                              res[:, t, :], ALU.mult, ALU.add)
                    last.then_inc(s_acc, 1)
                    dve.wait_ge(s_acc, ge + 1)

                for i in range(E * FE):
                    gi = b * E * FE + i
                    if gi + 1 < B * E * FE:
                        split_lo(n + 1, mwl[(gi + 1) % WSLOTS][:], mwh[(gi + 1) % WSLOTS][:])
                    n += 1
                    dve.wait_ge(s_eh, gi + 1)
                    sub(eal[gi % 2][:], ea[gi % 2][:], eah[gi % 2][:], s_el)
                    if i % FE == 0 and gi:
                        add_expert(gi // FE - 1)
                    if i == 0:
                        strengths()
                    if i == 1:
                        router_logits()
                    if b and i == 1:
                        ln_stats(("M", 0), zacc)
                    if i == 2:
                        top_two()
                    if b and i == 3:
                        ln_apply(("M", 0), zacc, xs[0])
                    if i == 3:
                        expert_weights()
                    if FE < i <= FE + E:
                        for t in range(T):
                            last = nc.vector.scalar_tensor_tensor(zacc[:, t, :], b2b[:, i - FE - 1, :],
                                                                  w[:, t, i - FE - 1:i - FE], zacc[:, t, :],
                                                                  ALU.mult, ALU.add)
                        step(last)
                    if b == 0 and i == 2 * FE + 1:
                        ln_apply(("A1", 1), xs[1], xs[1])
            for t in range(T):
                dve.wait_ge(s_last, t + 1)
                step(nc.vector.scalar_tensor_tensor(zacc[:, t, :], ps[:, t, :], w[:, t, E - 1:E], zacc[:, t, :],
                                                    ALU.mult, ALU.add))
                last = nc.vector.bn_stats(stats[:, t, :], zacc[:, t, :])
            step(last)
            for t in range(T):
                last = nc.vector.bn_aggr(mv[:, t, :], stats[:, t, :])
            last.then_inc(s_var, 1)
            ln_apply(("M", 1), zacc, xs[1])

        @block.tensor
        def _(pe):
            mm = nc.tensor.matmul

            def mm3(out, lh, ll, rh, rl, first, last):
                mm(out, lh, rh, start=first, stop=False)
                mm(out, ll, rh, start=False, stop=False)
                return mm(out, lh, rl, start=False, stop=last)

            def transposes(key, src):
                for h in range(HT):
                    for t in range(T):
                        last = nc.tensor.transpose(ps[:, TPB[key] + h, t * P:(t + 1) * P],
                                                   src[:, t, h * P:(h + 1) * P], ident[:])
                    last.then_inc(s_tp, 1)

            def xt_ready(key, h):
                pe.wait_ge(s_tplo, 4 * TP[key] + h + 1)

            tok = lambda t: slice(t * P, (t + 1) * P)
            pe.wait_ge(s_const, 6)
            for b in range(B):
                q0, v0, o0 = A0BANKS[b]
                pe.wait_ge(s_wlo, 1)
                for k in range(3):
                    for h in range(HT):
                        if k == 0:
                            xt_ready(("A0", b), h)
                        c = slice(k * D0, (k + 1) * D0)
                        last = mm3(ps[:, q0 + k, :], w0h[:, h, c], w0l[:, h, c], XTh[:, h, :], XTl[:, h, :], h == 0,
                                   h == HT - 1)
                    last.then_inc(s_a0qkv, 1)
                pe.wait_ge(s_a0lo, 2 * (b + 1))
                if b:
                    pe.wait_ge(s_yread, b)
                for q in range(T):
                    mm3(ps[:, o0 + q, :], QTh[:, tok(q)], QTl[:, tok(q)], KTh[:], KTl[:], True,
                        True).then_inc(s_a0s, 1)
                pe.wait_ge(s_a0act, 3 * (b + 1))
                if v0 == o0 + T - 1:
                    pe.wait_ge(s_a0p, T * (b + 1))
                for t in range(T):
                    last = nc.tensor.transpose(ps[:, v0, tok(t)], vT[:, tok(t)], ident[:])
                last.then_inc(s_a0vt, 1)
                for q in range(T):
                    pe.wait_ge(s_a0p, T * b + q + 1)
                    for k in range(T - 1):
                        last = nc.tensor.transpose(ps[:, q0 + k, tok(q)], P0[:, q, tok(k)], ident[:])
                        if q == T - 1:
                            last.then_inc(s_a0pt, 1)
                pe.wait_ge(s_a0vlo, b + 1)
                for q in range(T):
                    last = nc.tensor.transpose(ps[:, q0 + T - 1, tok(q)], P0[:, q, tok(T - 1)], ident[:])
                last.then_inc(s_a0pt, 1)
                for k in range(T):
                    pe.wait_ge(s_a0ptlo, T * b + k + 1)
                    last = mm3(ps[:, o0, :], Vh0[:, k, :], Vl0[:, k, :], PTh[:, k, :], PTl[:, k, :], k == 0,
                               k == T - 1)
                last.then_inc(s_a0ot, 1)
                pe.wait_ge(s_a0otlo, b + 1)
                if b:
                    pe.wait_ge(s_fnx, T)
                    transposes(("F0", 0), nx)
                pe.wait_ge(s_wlo, 2)
                for t in range(T):
                    mm3(ps[:, q0 + t, :], OTh[:, tok(t)], OTl[:, tok(t)], wo0h[:], wo0l[:], True,
                        True).then_inc(s_y, 1)
            n = 2
            for b in range(B):

                def down(gi, more=0):
                    pe.wait_ge(s_flo, gi + 1 + more)
                    i = gi % NI
                    if i == 0:
                        pe.wait_ge(s_yread, LN["F0", b])
                    for t in range(T):
                        last = mm3(ps[:, t, :], hhi[gi % 2][:, tok(t)], hlo[gi % 2][:, tok(t)],
                                   fwh[gi % WSLOTS][:, 2 * H:], fwl[gi % WSLOTS][:, 2 * H:], i == 0, i == NI - 1)
                    last.then_inc(s_fdn, 1)

                def gate_up(gi, more=0):
                    pe.wait_ge(s_wlo, n + gi + 1 + more)
                    if gi >= 2:
                        pe.wait_ge(s_fsg, gi - 1 + more)
                        pe.wait_ge(s_fh, gi - 1 + more)
                    for k, sm in enumerate((s_fg, s_fu)):
                        for h in range(HT):
                            if gi % NI == 0 and k == 0:
                                xt_ready(("F0", b), h)
                            c = slice(k * H + h * P, k * H + (h + 1) * P)
                            last = mm3(ps[:, 4 + 2 * k + gi % 2, :], fwh[gi % WSLOTS][:, c], fwl[gi % WSLOTS][:, c],
                                       XTh[:, h, :], XTl[:, h, :], h == 0, h == HT - 1)
                        last.then_inc(sm, 1)

                gate_up(b * NI)
                gate_up(b * NI + 1)
                down(b * NI)
                with pe.Fori(0, (NI - 2) // FSTEPS) as r:
                    for k in range(2, 2 + FSTEPS):
                        gate_up(b * NI + k, FSTEPS * r)
                        down(b * NI + k - 1, FSTEPS * r)
                pe.wait_ge(s_fh, NI * (b + 1))
                if b == 0:
                    pe.wait_ge(s_fnx, 2 * T)
                    transposes(("F0", 1), nx)
                else:
                    pe.wait_ge(s_lnout, 4 * (LN["F0", 0] + 1))
                    transposes(("A1", 0), xs[0])
                down(b * NI + NI - 1)
            n += B * NI
            for b in range(B):
                n += 2
                pe.wait_ge(s_wlo, n)
                for h in range(HT):
                    xt_ready(("A1", b), h)
                pb, ob = A1P, A1O

                def project(t):
                    bt = b * T + t
                    if t >= 2:
                        pe.wait_ge(s_qe, bt - 1)
                    r0 = pb + 2 * (t % 2)
                    for c0, c1, bank in ((0, 512, r0), (512, QKV1, r0 + 1)):
                        for h in range(HT):
                            last = mm3(ps[:, bank, 0:c1 - c0], XTh[:, h, tok(t)], XTl[:, h, tok(t)],
                                       w1h[:, h, c0:c1], w1l[:, h, c0:c1], h == 0, h == HT - 1)
                    last.then_inc(s_q, 1)

                def operands(t):
                    bt = b * T + t
                    pe.wait_ge(s_qlo, bt + 1)
                    if t == 0:
                        pe.wait_ge(s_yread, LN["A1", b])
                    for k in range(5):
                        u = 5 * bt + k
                        if u % (5 * T) >= 4:
                            v = u - 4
                            if v % 5 == 4:
                                pe.wait_ge(s_ek, v // 5 + 1)
                            else:
                                pe.wait_ge(s_eq, 4 * (v // 5) + v % 5 + 1)
                        for a in range(4):
                            if k < 4:
                                src = Qs[t % 2][:, 8 * k + 2 * a:8 * k + 2 * a + 2, :]
                            else:
                                src = (Ks0, Ks1)[t % 2][:, 2 * a:2 * a + 2, :]
                            last = nc.tensor.transpose(ps[:, ob + u % 4, tok(a)],
                                                       f32(src.rearrange("p a n -> p (a n)")), ident[:])
                        last.then_inc(s_tq, 1)

                for t in range(T):
                    project(t)
                    if t:
                        operands(t - 1)

                def max_scores(p, u):
                    G = p // 4
                    n_u = 3 * PAIRS * b + max_unit(p, u)
                    r0 = (A1P if u == 2 and p < EARLY else 0) + 2 * (n_u % 2)
                    if n_u % (3 * PAIRS) >= 2:
                        pe.wait_ge(s_mx, n_u - 1)
                    if u < 2:
                        q = 3 - u
                        for s in range(2):
                            mm(ps[:, r0 + s, 0:(q + 1) * P], Qop[:, p, tok(q)], Kop[:, 2 * G + s, 0:(q + 1) * P],
                               start=True, stop=False)
                            last = mm(ps[:, r0 + s, q * P:(q + 1) * P], identb[:], maskb[:], start=False, stop=True)
                    else:
                        for q in range(2):
                            w = (q + 1) * P
                            out = ps[:, r0 + q, 0:2 * w].rearrange("p (s k) -> p s k", s=2)
                            mm(out, Qop[:, p, tok(q)], Kop[:, 2 * G:2 * G + 2, 0:w], start=True, stop=False)
                            last = mm(out[:, :, q * P:w], identb[:], maskb[:, None, :].to_broadcast([P, 2, P]),
                                      start=False, stop=True)
                    last.then_inc(s_s1, 1)

                pe.wait_ge(s_eq, 16 * b + 8)
                pe.wait_ge(s_ek, T * b + 2)
                pe.wait_ge(s_qe, T * (b + 1))
                for p in range(EARLY):
                    max_scores(p, 2)
                operands(T - 1)
                pe.wait_ge(s_eq, 16 * (b + 1))
                pe.wait_ge(s_ek, T * (b + 1))
                for p in range(PAIRS):
                    for u in range(2 if p < EARLY else 3):
                        max_scores(p, u)
                    if p in (HP, PAIRS - 1):
                        half = int(p > HP)
                        pe.wait_ge(s_mx, 3 * (b * PAIRS + HP * (half + 1)))
                        nc.tensor.transpose(ps[0:2 * HP * T, 4, tok(half)],
                                            mtok[:, half].rearrange("p s h t -> p (s h t)"), ident[:]).then_inc(s_mt, 1)

                def scores(gg, u):
                    G, s = gg // 2, gg % 2
                    n_u = (b * NKV + gg) * 6 + u
                    r0 = 2 * (n_u % 3)
                    if n_u % (6 * NKV) >= 3:
                        pe.wait_ge(s_p, n_u - 2)
                    kt = (0, 0, 1, 1, 2, 3)[u]
                    lhsT = Kop[:, 2 * G + s, tok(kt)]
                    if u < 4:
                        for a in range(2):
                            j = 2 * (u % 2) + a
                            mm(ps[:, r0 + a, 0:S - kt * P], lhsT, Qop[:, 4 * G + j, kt * P:S], start=True,
                               stop=False)
                        for a in range(2):
                            last = mm(ps[:, r0 + a, 0:P], identb[:], maskT[:], start=False, stop=True)
                    elif u == 4:
                        for a in range(2):
                            j = 4 * G + 2 * a
                            mm(ps[:, r0 + a, :].rearrange("p (j q) -> p j q", j=2), lhsT,
                               Qop[:, j:j + 2, 2 * P:S], start=True, stop=False)
                        for a in range(2):
                            last = mm(ps[:, r0 + a, :].rearrange("p (j q) -> p j q", j=2)[:, :, 0:P], identb[:],
                                      maskT[:, None, :].to_broadcast([P, 2, P]), start=False, stop=True)
                    else:
                        out = ps[:, r0, :].rearrange("p (j q) -> p j q", j=4)
                        mm(out, lhsT, Qop[:, 4 * G:4 * G + 4, 3 * P:S], start=True, stop=False)
                        last = mm(out, identb[:], maskT[:, None, :].to_broadcast([P, 4, P]), start=False,
                                  stop=True)
                    last.then_inc(s_s2, 1)

                def values(gg, q):
                    gi = b * NKV + gg
                    if q == 0:
                        if gg:
                            pe.wait_ge(s_oe, gi)
                        else:
                            pe.wait_ge(s_v, 4 * T * (b + 1))
                    pe.wait_ge(s_pl, 6 * gi + (2, 4, 5, 6)[q])
                    for j in range(4):
                        c = ((q % 2) * 4 + j) * VW
                        out = ps[:, 6 + q // 2, c:c + VW]
                        for kt in range(q + 1):
                            o = (UO[j // 2] + (j % 2) * 512 + q * P, UO[2 + j // 2] + (j % 2) * 384 + (q - 1) * P,
                                 UO[4] + j * 256 + (q - 2) * P, UO[5] + j * P)[kt]
                            for part in (Ph, Pl):
                                last = mm(out, part[gg % 2][:, o:o + P], Vs[:, kt, gg, :],
                                          start=kt == 0 and part is Ph, stop=kt == q and part is Pl)
                    if q % 2:
                        last.then_inc(s_o, 1)

                for gg in range(NKV):
                    if gg == 0:
                        pe.wait_ge(s_mx, 3 * PAIRS * (b + 1))
                    if gg % (NKV // 2) == 0:
                        half = gg // (NKV // 2)
                        pe.wait_ge(s_md[half], 64 * (b + 1))
                    for u in range(6):
                        if gg == 0 and u == 2:
                            pe.wait_ge(s_mtl, 2 * b + 2)
                        scores(gg, u)
                        if gg and u in (1, 2, 3, 4):
                            values(gg - 1, u - 1)
                pe.wait_ge(s_p, 6 * NKV * (b + 1))
                if b == 0:
                    pe.wait_ge(s_lnout, 4 * (LN["F0", 1] + 1))
                    transposes(("A1", 1), xs[1])
                else:
                    pe.wait_ge(s_lnout, 4 * (LN["A1", 0] + 1))
                    transposes(("M", 0), xs[0])
                for q in range(T):
                    values(NKV - 1, q)
                pe.wait_ge(s_ot, NKV * (b + 1))
                transposes(("O1", b), Otok)
                n += 2
                pe.wait_ge(s_wlo, n)
                for h in range(HT):
                    xt_ready(("A1", 1) if b == 0 else ("M", 0), h)
                for h in range(HT):
                    xt_ready(("O1", b), h)
                for t in range(T):
                    for h in range(HT):
                        last = mm3(ps[:, t, :], OTh1[:, h, tok(t)], OTl1[:, h, tok(t)], wo1h[:, h, :], wo1l[:, h, :],
                                   h == 0, h == HT - 1)
                    last.then_inc(s_y, 1)
            for b in range(B):
                pe.wait_ge(s_gw, 2)
                def second(gi):
                    i = gi % (E * FE)
                    pe.wait_ge(s_el, gi + 1)
                    if gi == 0:
                        pe.wait_ge(s_yread, LN["M", 0])
                    if i % FE == 0 and gi >= FE:
                        pe.wait_ge(s_acc, gi // FE)
                    for t in range(T):
                        last = mm3(ps[:, t, :], eah[gi % 2][:, tok(t)], eal[gi % 2][:, tok(t)],
                                   mwh[gi % WSLOTS][:, H:], mwl[gi % WSLOTS][:, H:], i % FE == 0, i % FE == FE - 1)
                        if gi == B * E * FE - 1:
                            last.then_inc(s_last, 1)
                    if gi < B * E * FE - 1:
                        last.then_inc(s_e2, 1)

                for i in range(E * FE):
                    gi = b * E * FE + i
                    pe.wait_ge(s_wlo, n + 1)
                    n += 1
                    if gi >= 2:
                        pe.wait_ge(s_ea, gi - 1)
                    for h in range(HT):
                        if i == 0:
                            xt_ready(("M", b), h)
                        last = mm3(ps[:, 4 + gi % 2, :], mwh[gi % WSLOTS][:, tok(h)], mwl[gi % WSLOTS][:, tok(h)],
                                   XTh[:, h, :], XTl[:, h, :], h == 0, h == HT - 1)
                    last.then_inc(s_pre, 1)
                    if i == 0:
                        for h in range(HT):
                            last = mm3(ps[:, 6, :], gwh[:, h, :], gwl[:, h, :], XTh[:, h, :], XTl[:, h, :], h == 0,
                                       h == HT - 1)
                        last.then_inc(s_lgT, 1)
                    if i == 1:
                        pe.wait_ge(s_lgTe, b + 1)
                        for t in range(T):
                            last = nc.tensor.transpose(ps[:, 7, tok(t)], lgT[:, tok(t)], ident[:])
                        last.then_inc(s_lg, 1)
                    if i:
                        second(gi - 1)
                    if i == 1:
                        pe.wait_ge(s_as, b + 1)
                        mm(ps[:, 6, 0:2], onesf[:], asum2[:], start=True, stop=True).then_inc(s_rkb, 1)
                    if i == 3:
                        pe.wait_ge(s_rk, 2 * (b + 1))
                        mm(ps[:, 6, 8:8 + E], row0[:], g[9][:, 0, :], start=True, stop=True).then_inc(s_rkb, 2)
                if b == 0:
                    pe.wait_ge(s_ea, E * FE)
                    pe.wait_ge(s_rkb, 3)
                    pe.wait_ge(s_acc, 1)
                    pe.wait_ge(s_lnout, 4 * (LN["A1", 1] + 1))
                    transposes(("M", 1), xs[1])
                second(b * E * FE + E * FE - 1)


_IN = ("x", "xT", "smallc", "bo0", "w_qkv0", "w_o0", "w_ffn", "cosb", "sinb", "bq1", "bo1",
       "w_qkv1", "w_o1", "gwr", "awt", "b2", "gb", "w_moe")


def tiles(w):
    return np.ascontiguousarray(w.reshape(-1, P, w.shape[1]).transpose(1, 0, 2)).reshape(P, -1)


def lay_out(a):
    f = np.float32
    x = a["L0_attn_x"]
    heads = np.arange(NH * HD).reshape(NKV // 2, 2, GROUP, HD).transpose(0, 2, 1, 3).reshape(-1)
    cols = np.concatenate([heads, np.arange(NH * HD, QKV1)])
    inv = 1.0 / 10000.0 ** (np.arange(0, HD, 2, dtype=f) / HD)
    ang = np.arange(S, dtype=f)[:, None] * inv[None, :].astype(f)
    cos = np.repeat(np.cos(ang).astype(f), 2, axis=1)
    sin = np.stack([-np.sin(ang), np.sin(ang)], axis=-1).astype(f).reshape(S, HD)
    by_tile = lambda v: np.ascontiguousarray(v.reshape(T, P, -1).transpose(1, 0, 2))
    smallc = np.zeros((P, 64), f)
    smallc[:, 0:3] = a["L0_attn_bqkv"].reshape(3, P).T
    smallc[:, 3:7] = a["L0_ffn_ln_w"].reshape(HT, P).T
    smallc[:, 8:20] = a["L1_ffn_b1"].reshape(E * FE, P).T
    gate, up, down = (a["L0_ffn_" + k] for k in ("gate_w", "up_w", "down_w"))
    w_ffn = np.concatenate([
        gate.reshape(NI, P, HT, P).transpose(0, 3, 2, 1).reshape(NI, P, H),
        up.reshape(NI, P, HT, P).transpose(0, 3, 2, 1).reshape(NI, P, H),
        down.T.reshape(NI, P, H)], axis=2)
    w_qkv1 = tiles(a["L1_attn_w_qkv"][cols].T).reshape(P, 2, CHUNK).transpose(1, 0, 2)
    w_o1 = tiles(a["L1_attn_w_o"].T[heads]).reshape(P, 2, 2 * H).transpose(1, 0, 2)
    w1, w2 = a["L1_ffn_w1"], a["L1_ffn_w2"]
    w_moe = np.concatenate([
        w1.reshape(E, HT, P, FE, P).transpose(0, 3, 2, 1, 4).reshape(E * FE, P, H),
        w2.reshape(E * FE, P, H)], axis=2)
    gwr = np.zeros((P, HT, P), f)
    gwr[:, :, 0:E] = a["L1_ffn_gate_w"][0:H].reshape(HT, P, E).transpose(1, 0, 2)
    text = (np.arange(S) >= VISION).astype(f)
    awt = np.stack([text / ((S - VISION) * H), (1 - text) / (VISION * H)]).astype(f)
    return {
        "x": x.reshape(B, T, P, H).transpose(0, 2, 1, 3),
        "xT": x.transpose(0, 2, 1).reshape(B, HT, P, S).transpose(0, 2, 1, 3),
        "smallc": smallc,
        "bo0": a["L0_attn_bo"], "w_qkv0": tiles(a["L0_attn_Wqkv"]), "w_o0": a["L0_attn_Wo"], "w_ffn": w_ffn,
        "cosb": by_tile(cos), "sinb": by_tile(sin),
        "bq1": a["L1_attn_b_qkv"][cols], "bo1": a["L1_attn_b_o"], "w_qkv1": w_qkv1, "w_o1": w_o1,
        "gwr": gwr, "awt": awt.reshape(2, T, P).transpose(2, 0, 1), "b2": a["L1_ffn_b2"],
        "gb": np.stack([a["L1_ffn_gate_w"][H], a["L1_ffn_gate_b"]]), "w_moe": w_moe,
    }


def kernel(**inputs):
    import concourse.bacc as bacc
    from concourse.bass_utils import run_bass_kernel_spmd

    nc = bacc.Bacc("TRN2", target_bir_lowering=False, num_devices=1)
    arrays = {n: np.ascontiguousarray(v) for n, v in lay_out({k: np.asarray(v) for k, v in inputs.items()}).items()}
    dram = {n: nc.dram_tensor(f"in_{n}", arrays[n].shape, mybir.dt.from_np(arrays[n].dtype),
                              kind="ExternalInput").ap() for n in _IN}
    dram["out"] = nc.dram_tensor("out_0", (B, P, T, H), F32, kind="ExternalOutput").ap()
    post_ln_layers(nc, dram)
    r = run_bass_kernel_spmd(nc, [{f"in_{n}": arrays[n] for n in _IN}], core_ids=[0])
    return r.results[0]["out_0"].transpose(0, 2, 1, 3).reshape(B, S, H)
```
